# Optimizing a Trainium2 kernel written in Bass

```python
import numpy as np
import jax
import jax.numpy as jnp

def _softmax(x, axis=-1):
    return jax.nn.softmax(x, axis=axis)

def _gelu(x):
    return jax.nn.gelu(x, approximate=True)

def _silu(x):
    return jax.nn.silu(x)

def _sigmoid(x):
    return jax.nn.sigmoid(x)

def _layernorm(x, axis=-1, eps=1e-05):
    m = jnp.mean(x, axis=axis, keepdims=True)
    v = jnp.var(x, axis=axis, keepdims=True)
    return (x - m) / jnp.sqrt(v + eps)

def _scatter_add(tgt, idx, src, axis=0):
    return tgt.at[idx].add(src)

def _segment_sum(src, seg, n):
    return jax.ops.segment_sum(src, seg, n)
kernel_name = 'mk_sandwich_d2_jaxref_r8_cc8d99'

def setup_inputs(seed: int=0):
    np.random.seed(seed)
    _w = jnp.asarray

    def _L0_attn_setup():
        import jax, jax.numpy as jnp
        import numpy as np
        B, S, H = (1, 256, 512)
        NH, NKV, HD = (32, 8, 128)
        GROUPS = NH // NKV
        ROPE_THETA = 10000.0

        def _rope_cos_sin(seq_len, head_dim, dtype):
            inv_freq = 1.0 / ROPE_THETA ** (jnp.arange(0, head_dim, 2, dtype=jnp.float32) / head_dim)
            t = jnp.arange(seq_len, dtype=jnp.float32)
            freqs = jnp.einsum('i,j->ij', t, inv_freq)
            emb = jnp.concatenate([freqs, freqs], axis=-1)
            return (jnp.cos(emb).astype(dtype), jnp.sin(emb).astype(dtype))

        def _rotate_half(x):
            x1, x2 = (x[..., :x.shape[-1] // 2], x[..., x.shape[-1] // 2:])
            return jnp.concatenate([-x2, x1], axis=-1)
        key = jax.random.key(seed)
        ks = jax.random.split(key, 5)
        scale = 0.02
        return {'hidden_states': jax.random.normal(ks[0], (B, S, H), jnp.float32), 'Wq': jax.random.normal(ks[1], (NH * HD, H), jnp.float32) * scale, 'Wk': jax.random.normal(ks[2], (NKV * HD, H), jnp.float32) * scale, 'Wv': jax.random.normal(ks[3], (NKV * HD, H), jnp.float32) * scale, 'Wo': jax.random.normal(ks[4], (H, NH * HD), jnp.float32) * scale}
    _L0_attn_in = _L0_attn_setup()

    def _L0_ffn_setup():
        import jax, jax.numpy as jnp
        import numpy as np
        B_, S, D_IN, D_OUT = (4, 256, 512, 512)
        N, RANK, ALPHA = (8, 16, 32)
        SCALE = ALPHA / RANK
        key = jax.random.key(seed)
        kx, ka, kb, kw, kbias = jax.random.split(key, 5)
        x = jax.random.normal(kx, (B_, S, D_IN), dtype=jnp.float32)
        lora_A = jax.random.normal(ka, (N, RANK, D_IN), dtype=jnp.float32) * (1.0 / np.sqrt(D_IN))
        lora_B = jax.random.normal(kb, (N, D_OUT, RANK), dtype=jnp.float32) * (1.0 / np.sqrt(RANK))
        W = jax.random.normal(kw, (D_OUT, D_IN), dtype=jnp.float32) * (1.0 / np.sqrt(D_IN))
        bias = jax.random.normal(kbias, (D_OUT,), dtype=jnp.float32) * 0.01
        lora_weights = jnp.full((N,), 1.0 / N, dtype=jnp.float32)
        return {'x': x, 'lora_A': lora_A, 'lora_B': lora_B, 'W': W, 'bias': bias, 'lora_weights': lora_weights}
    _L0_ffn_in = _L0_ffn_setup()

    def _L1_attn_setup():
        import jax, jax.numpy as jnp
        import numpy as np
        B, N, D = (2, 256, 512)
        H, HD = (32, 128)
        EPS = 1e-06

        def rmsnorm(x, w):
            xf = x.astype(jnp.float32)
            var = jnp.mean(xf * xf, axis=-1, keepdims=True)
            return (w * (xf * jax.lax.rsqrt(var + EPS))).astype(x.dtype)
        key = jax.random.key(seed)
        ks = jax.random.split(key, 11)
        s = 1.0 / np.sqrt(D)
        return {'hidden_states': jax.random.normal(ks[0], (B, N, D), jnp.float32), 'Wq': jax.random.normal(ks[1], (D, H * HD), jnp.float32) * s, 'bq': jax.random.normal(ks[2], (H * HD,), jnp.float32) * 0.01, 'Wk': jax.random.normal(ks[3], (D, H * HD), jnp.float32) * s, 'bk': jax.random.normal(ks[4], (H * HD,), jnp.float32) * 0.01, 'Wv': jax.random.normal(ks[5], (D, H * HD), jnp.float32) * s, 'bv': jax.random.normal(ks[6], (H * HD,), jnp.float32) * 0.01, 'Wo': jax.random.normal(ks[7], (H * HD, D), jnp.float32) * s, 'bo': jax.random.normal(ks[8], (D,), jnp.float32) * 0.01, 'gq': jnp.ones((HD,), jnp.float32), 'gk': jnp.ones((HD,), jnp.float32)}
    _L1_attn_in = _L1_attn_setup()

    def _L1_ffn_setup():
        import jax, jax.numpy as jnp
        import numpy as np
        DIM = 512
        HID = 1376
        R = 16
        SCALING = 32.0 / 16.0

        def _lora_linear(x, w, a, b):
            base = jnp.einsum('bsd,od->bso', x, w)
            low = jnp.einsum('bsr,or->bso', jnp.einsum('bsd,rd->bsr', x, a), b)
            return base + low * SCALING
        key = jax.random.key(seed)
        ks = jax.random.split(key, 10)
        s_in = 1.0 / np.sqrt(DIM)
        s_hid = 1.0 / np.sqrt(HID)
        return {'x': jax.random.normal(ks[0], (4, 256, DIM), jnp.float32), 'w1': jax.random.normal(ks[1], (HID, DIM), jnp.float32) * s_in, 'w3': jax.random.normal(ks[2], (HID, DIM), jnp.float32) * s_in, 'w2': jax.random.normal(ks[3], (DIM, HID), jnp.float32) * s_hid, 'lora_A1': jax.random.normal(ks[4], (R, DIM), jnp.float32) * s_in, 'lora_B1': jax.random.normal(ks[5], (HID, R), jnp.float32) * 0.02, 'lora_A3': jax.random.normal(ks[6], (R, DIM), jnp.float32) * s_in, 'lora_B3': jax.random.normal(ks[7], (HID, R), jnp.float32) * 0.02, 'lora_A2': jax.random.normal(ks[8], (R, HID), jnp.float32) * s_hid, 'lora_B2': jax.random.normal(ks[9], (DIM, R), jnp.float32) * 0.02}
    _L1_ffn_in = _L1_ffn_setup()
    _d = {'L0_attn_hidden_states': _L0_attn_in['hidden_states'], 'L0_attn_Wq': _L0_attn_in['Wq'], 'L0_attn_Wk': _L0_attn_in['Wk'], 'L0_attn_Wv': _L0_attn_in['Wv'], 'L0_attn_Wo': _L0_attn_in['Wo'], 'L0_ffn_lora_A': _L0_ffn_in['lora_A'], 'L0_ffn_lora_B': _L0_ffn_in['lora_B'], 'L0_ffn_W': _L0_ffn_in['W'], 'L0_ffn_bias': _L0_ffn_in['bias'], 'L0_ffn_lora_weights': _L0_ffn_in['lora_weights'], 'L1_attn_Wq': _L1_attn_in['Wq'], 'L1_attn_bq': _L1_attn_in['bq'], 'L1_attn_Wk': _L1_attn_in['Wk'], 'L1_attn_bk': _L1_attn_in['bk'], 'L1_attn_Wv': _L1_attn_in['Wv'], 'L1_attn_bv': _L1_attn_in['bv'], 'L1_attn_Wo': _L1_attn_in['Wo'], 'L1_attn_bo': _L1_attn_in['bo'], 'L1_attn_gq': _L1_attn_in['gq'], 'L1_attn_gk': _L1_attn_in['gk'], 'L1_ffn_w1': _L1_ffn_in['w1'], 'L1_ffn_w3': _L1_ffn_in['w3'], 'L1_ffn_w2': _L1_ffn_in['w2'], 'L1_ffn_lora_A1': _L1_ffn_in['lora_A1'], 'L1_ffn_lora_B1': _L1_ffn_in['lora_B1'], 'L1_ffn_lora_A3': _L1_ffn_in['lora_A3'], 'L1_ffn_lora_B3': _L1_ffn_in['lora_B3'], 'L1_ffn_lora_A2': _L1_ffn_in['lora_A2'], 'L1_ffn_lora_B2': _L1_ffn_in['lora_B2']}
    _x0 = _d['L0_attn_hidden_states']
    _d['L0_attn_hidden_states'] = jax.random.normal(jax.random.fold_in(jax.random.key(seed), 1), (2, 512, 512), dtype=_x0.dtype)
    del _x0
    return _d

def reference(L0_attn_hidden_states, L0_attn_Wq, L0_attn_Wk, L0_attn_Wv, L0_attn_Wo, L0_ffn_lora_A, L0_ffn_lora_B, L0_ffn_W, L0_ffn_bias, L0_ffn_lora_weights, L1_attn_Wq, L1_attn_bq, L1_attn_Wk, L1_attn_bk, L1_attn_Wv, L1_attn_bv, L1_attn_Wo, L1_attn_bo, L1_attn_gq, L1_attn_gk, L1_ffn_w1, L1_ffn_w3, L1_ffn_w2, L1_ffn_lora_A1, L1_ffn_lora_B1, L1_ffn_lora_A3, L1_ffn_lora_B3, L1_ffn_lora_A2, L1_ffn_lora_B2):

    def _L0_attn_ref(hidden_states, Wq, Wk, Wv, Wo):
        import jax, jax.numpy as jnp
        import numpy as np
        B, S, H = (1, 256, 512)
        NH, NKV, HD = (32, 8, 128)
        GROUPS = NH // NKV
        ROPE_THETA = 10000.0

        def _rope_cos_sin(seq_len, head_dim, dtype):
            inv_freq = 1.0 / ROPE_THETA ** (jnp.arange(0, head_dim, 2, dtype=jnp.float32) / head_dim)
            t = jnp.arange(seq_len, dtype=jnp.float32)
            freqs = jnp.einsum('i,j->ij', t, inv_freq)
            emb = jnp.concatenate([freqs, freqs], axis=-1)
            return (jnp.cos(emb).astype(dtype), jnp.sin(emb).astype(dtype))

        def _rotate_half(x):
            x1, x2 = (x[..., :x.shape[-1] // 2], x[..., x.shape[-1] // 2:])
            return jnp.concatenate([-x2, x1], axis=-1)
        b, s, _ = hidden_states.shape
        dtype = hidden_states.dtype
        q = jnp.einsum('bsh,oh->bso', hidden_states, Wq).reshape(b, s, NH, HD).transpose(0, 2, 1, 3)
        k = jnp.einsum('bsh,oh->bso', hidden_states, Wk).reshape(b, s, NKV, HD).transpose(0, 2, 1, 3)
        v = jnp.einsum('bsh,oh->bso', hidden_states, Wv).reshape(b, s, NKV, HD).transpose(0, 2, 1, 3)
        cos, sin = _rope_cos_sin(s, HD, dtype)
        cos, sin = (cos[None, None], sin[None, None])
        q = q * cos + _rotate_half(q) * sin
        k = k * cos + _rotate_half(k) * sin
        qg = q.reshape(b, NKV, GROUPS, s, HD)
        scores = jnp.einsum('bkgqd,bksd->bkgqs', qg, k) / jnp.sqrt(jnp.asarray(HD, dtype))
        causal = jnp.tril(jnp.ones((s, s), dtype=bool))
        scores = jnp.where(causal[None, None, None], scores, jnp.asarray(-jnp.inf, scores.dtype))
        attn = jax.nn.softmax(scores.astype(jnp.float32), axis=-1).astype(dtype)
        out = jnp.einsum('bkgqs,bksd->bkgqd', attn, v)
        out = out.reshape(b, NH, s, HD).transpose(0, 2, 1, 3).reshape(b, s, NH * HD)
        return jnp.einsum('bso,ho->bsh', out, Wo)

    def _L0_ffn_ref(x, lora_A, lora_B, W, bias, lora_weights):
        import jax, jax.numpy as jnp
        import numpy as np
        B_, S, D_IN, D_OUT = (4, 256, 512, 512)
        N, RANK, ALPHA = (8, 16, 32)
        SCALE = ALPHA / RANK
        h = jnp.einsum('bsd,nrd->nbsr', x, lora_A)
        coef = (SCALE * lora_weights)[:, None, None]
        lora_out = jnp.einsum('nbsr,nor->bso', h, lora_B * coef)
        base = jnp.einsum('bsd,od->bso', x, W) + bias
        return base + lora_out

    def _L1_attn_ref(hidden_states, Wq, bq, Wk, bk, Wv, bv, Wo, bo, gq, gk):
        import jax, jax.numpy as jnp
        import numpy as np
        B, N, D = (2, 256, 512)
        H, HD = (32, 128)
        EPS = 1e-06

        def rmsnorm(x, w):
            xf = x.astype(jnp.float32)
            var = jnp.mean(xf * xf, axis=-1, keepdims=True)
            return (w * (xf * jax.lax.rsqrt(var + EPS))).astype(x.dtype)
        b, n, _ = hidden_states.shape
        q = (hidden_states @ Wq + bq).reshape(b, n, H, HD)
        k = (hidden_states @ Wk + bk).reshape(b, n, H, HD)
        v = (hidden_states @ Wv + bv).reshape(b, n, H, HD)
        q = rmsnorm(q, gq)
        k = rmsnorm(k, gk)
        scale = 1.0 / np.sqrt(HD)
        scores = jnp.einsum('bnhd,bmhd->bhnm', q, k) * scale
        attn = jax.nn.softmax(scores.astype(jnp.float32), axis=-1).astype(q.dtype)
        out = jnp.einsum('bhnm,bmhd->bnhd', attn, v).reshape(b, n, H * HD)
        return out @ Wo + bo

    def _L1_ffn_ref(x, w1, w3, w2, lora_A1, lora_B1, lora_A3, lora_B3, lora_A2, lora_B2):
        import jax, jax.numpy as jnp
        import numpy as np
        DIM = 512
        HID = 1376
        R = 16
        SCALING = 32.0 / 16.0

        def _lora_linear(x, w, a, b):
            base = jnp.einsum('bsd,od->bso', x, w)
            low = jnp.einsum('bsr,or->bso', jnp.einsum('bsd,rd->bsr', x, a), b)
            return base + low * SCALING
        h1 = _lora_linear(x, w1, lora_A1, lora_B1)
        h3 = _lora_linear(x, w3, lora_A3, lora_B3)
        g = jax.nn.silu(h1) * h3
        return _lora_linear(g, w2, lora_A2, lora_B2)
    x = L0_attn_hidden_states
    x = x + _layernorm(_L0_attn_ref(_layernorm(x, axis=-1), L0_attn_Wq, L0_attn_Wk, L0_attn_Wv, L0_attn_Wo), axis=-1)
    x = x + _layernorm(_L0_ffn_ref(_layernorm(x, axis=-1), L0_ffn_lora_A, L0_ffn_lora_B, L0_ffn_W, L0_ffn_bias, L0_ffn_lora_weights), axis=-1)
    x = x + _layernorm(_L1_attn_ref(_layernorm(x, axis=-1), L1_attn_Wq, L1_attn_bq, L1_attn_Wk, L1_attn_bk, L1_attn_Wv, L1_attn_bv, L1_attn_Wo, L1_attn_bo, L1_attn_gq, L1_attn_gk), axis=-1)
    x = x + _layernorm(_L1_ffn_ref(_layernorm(x, axis=-1), L1_ffn_w1, L1_ffn_w3, L1_ffn_w2, L1_ffn_lora_A1, L1_ffn_lora_B1, L1_ffn_lora_A3, L1_ffn_lora_B3, L1_ffn_lora_A2, L1_ffn_lora_B2), axis=-1)
    return x

_drawn_inputs = setup_inputs


def setup_inputs(seed=0):
    import zlib

    import numpy as np

    out = dict(_drawn_inputs(seed))
    spreads = {'L0_ffn_lora_weights': (0.125, 0.2), 'L1_attn_gq': (1.0, 0.6), 'L1_attn_gk': (1.0, 0.6)}
    factors = {'L0_ffn_bias': 8.0,
     'L1_attn_bq': 23.485,
     'L1_attn_bk': 64.0,
     'L1_attn_bv': 5.514,
     'L1_attn_bo': 8.0}
    for name, (base, spread) in spreads.items():
        noise = np.random.default_rng([zlib.crc32(name.encode()), seed]).standard_normal(out[name].shape)
        drawn = base * np.exp(spread * noise) if base else spread * noise
        out[name] = jnp.asarray(drawn.astype(out[name].dtype))
    for name, factor in factors.items():
        out[name] = (out[name] * factor).astype(out[name].dtype)
    return out
```

```python
from contextlib import ExitStack

import concourse.bass as bass
from concourse import mybir

ALU = mybir.AluOpType
ACT = mybir.ActivationFunctionType
AXX = mybir.AxisListType.X
F32 = mybir.dt.float32
F32R = mybir.dt.float32r

P = 128
B, S, D = 2, 512, 512
T = B * S
TT = T // P
TB = S // P
C = D // P
HD = 128
NH = 32
GH = 4
NG = NH // GH
SLOTS = GH * B
TILES = SLOTS * TB
HID = 1376
HT = -(-HID // P)
HP = HT * P
RK = 16
SCALE = float(HD) ** -0.5
LN_EPS = 1e-5
RMS_EPS = 1e-6
MASKED = -1e30

TURN, PV, OUT = 2, 6, 7
STEPS = OUT + TILES


def steps_of(*items):
    by = {}
    for step, item in sorted(items, key=lambda x: x[0]):
        by.setdefault(step, []).append(item)
    return by


def in_order(by):
    return [x for step in sorted(by) for x in by[step]]


BANK0 = [(4 * (s - 1) + 1, ("q", s)) for s in range(1, SLOTS)] + [(8, ("k", 1)), (10, ("v", 1)), (11, ("vt", 1))]
BANK0_NEXT = [(28, ("k", 0)), (30, ("v", 0)), (32, ("vt", 0)), (33, ("q", 0))]
WORK0 = [(4 * s + 3, ("wo", s)) for s in range(SLOTS)] + [(4 * (s - 2) + 2, ("wq", s)) for s in range(2, SLOTS)]
WORK0_NEXT = [(14, ("wk", 0)), (16, ("wv", 0)), (26, ("wq", 0)), (30, ("wq", 1))]

BANK1 = ([(-1, ("tq", 0)), (-1, ("tk", 0))]
         + [(t, ("v", 0, t)) for t in range(TB)]
         + [(4 * (s - 1) + 1, ("tq", s)) for s in range(1, SLOTS)]
         + [(4 * (s - 1) + 2, ("tk", s)) for s in range(1, SLOTS)]
         + [(3 + t, ("q", 1, t)) for t in range(TB)]
         + [(n, ("k", 1, t)) for t, n in enumerate((7, 8, 9, 9))]
         + [(18 + t, ("v", 1, t)) for t in range(TB)])
BANK1_NEXT = ([(n, ("q", 0, t)) for t, n in enumerate((22, 23, 24, 26))]
              + [(n, ("k", 0, t)) for t, n in enumerate((27, 28, 30, 32))])
WORK1 = [(4 * s + 3, ("wo", s)) for s in range(SLOTS)]
WORK1_NEXT = [(n, (kind, c)) for kind, at in (("wq", (9, 10, 12, 13)), ("wk", (14, 16, 17, 18)),
                                              ("wv", (22, 24, 25, 26))) for c, n in enumerate(at)]
TO_NORM, TO_SCALE = 1, (2, 2, 3, 3)


class Body:

    def __init__(self, i, last, bank, bank_next, work, work_next, first_bank, first_work):
        self.i, self.last = i, last
        self.bank_at = steps_of(*bank, *([] if last else bank_next))
        self.work_at = steps_of(*work, *([] if last else work_next))
        self.order = in_order(self.bank_at)
        self.work_order = in_order(self.work_at)
        self.whole = in_order(steps_of(*bank, *bank_next))
        self.n_work = len(work) + len(work_next)
        self.first_bank, self.first_work = first_bank, first_work
        self.next_work = {x for _, x in work_next}

    def start(self, kinds=None):
        n = lambda xs: sum(kinds is None or x[0] in kinds for x in xs)
        return self.i * n(self.whole) + n(self.first_bank)

    def done(self, x, kinds=None):
        upto = self.order[:self.order.index(x) + 1]
        return self.start(kinds) + sum(kinds is None or y[0] in kinds for y in upto)

    def parity(self, x, kinds=None):
        upto = [y for y in self.order[:self.order.index(x)] if kinds is None or y[0] in kinds]
        return len(upto) % 2

    def work_start(self):
        return self.i * self.n_work + len(self.first_work)

    def work_done(self, x):
        return self.work_start() + self.work_order.index(x) + 1


class Split:

    def __init__(self, hi, lo):
        self.hi, self.lo = hi, lo

    def __getitem__(self, at):
        return Split(self.hi[at], self.lo[at])

    @property
    def passes(self):
        return self.hi, self.lo


def product(nc, out, left, right, first=True, last=True):
    nc.tensor.matmul(out, left.hi, right.lo, start=first, stop=False, skip_group_check=True)
    nc.tensor.matmul(out, left.lo, right.hi, start=False, stop=False, skip_group_check=True)
    return nc.tensor.matmul(out, left.hi, right.hi, start=False, stop=last, skip_group_check=True)


def rest(engine, out, full, hi):
    return engine.tensor_tensor(out, full, hi.bitcast(F32), ALU.subtract)


class Program:
    def __init__(self, nc, a, out, upto):
        self.nc, self.a, self.out, self.upto = nc, a, out, upto

    def sb(self, ctx, name, shape, dt=F32):
        return ctx.enter_context(self.nc.sbuf_tensor(name, shape, dt))

    def split(self, ctx, name, shape):
        return Split(self.sb(ctx, name + "_hi", shape, F32R), self.sb(ctx, name + "_lo", shape, F32R))

    def banks(self, ctx, name, n):
        return [ctx.enter_context(self.nc.psum_tensor(f"{name}{i}", [P, 512], F32)) for i in range(n)]

    def sem(self, ctx, name):
        return ctx.enter_context(self.nc.semaphore(name))


def norm_phase(p, ctx0, name, x, xT, ident, half, update=None, load=None, store=None, bias=None):
    nc = p.nc
    with ExitStack() as ctx:
        sb = lambda n, s, dt=F32: p.sb(ctx, f"{name}_{n}", s, dt)
        sem = lambda n: p.sem(ctx0, f"{name}_{n}")
        rounds = ([0] if update is not None else []) + ([1] if xT is not None else [])
        stats = sb("stats", [P, 2, TT, 6])
        mv = sb("mv", [P, 2, TT, 2])
        var = sb("var", [P, 2, TT])
        rstd = sb("rstd", [P, 2, TT])
        z = sb("z", [P, 2, D])
        turned = p.banks(ctx, f"{name}_turned", 2)
        x_in, stat, aggr, vare, rs, zr, added = map(sem, "x_in stat aggr vare rs zr added".split())
        if xT is not None:
            tr, hi, lo = sem("tr"), sem("hi"), sem("lo")
        if store is not None:
            stored = sem("stored")
        if bias is not None:
            bias_in, biased = sem("bias_in"), sem("biased")
        if bias is not None:
            brow = sb("brow", [P, D])
        block = ctx.enter_context(nc.Block())
        nr = len(rounds)

        @block.sync
        def _(sp):
            if load is not None:
                sp.dma_start(x[:], load).then_inc(x_in, 16)
            if bias is not None:
                sp.dma_start(brow[:], bias.to_broadcast([P, D])).then_inc(bias_in, 16)
            if store is not None:
                sp.wait_ge(added, TT)
                sp.dma_start(store, x[:]).then_inc(stored, 16)
                sp.wait_ge(stored, 16)

        def turn_lo(dve, t):
            dve.wait_ge(hi, t + 1)
            rest(dve, xT.lo[:, :, t * P:(t + 1) * P], turned[t % 2][:].rearrange("p (c t) -> p c t", c=C),
                 xT.hi[:, :, t * P:(t + 1) * P]).then_inc(lo, 1)

        @block.vector
        def _(dve):
            if bias is not None:
                dve.wait_ge(bias_in, 16)
                for t in range(TT):
                    dve.tensor_tensor(update[:, t, :], update[:, t, :], brow[:], ALU.add).then_inc(biased, 1)
                dve.wait_ge(biased, TT)
            if load is not None:
                dve.wait_ge(x_in, 16)
            for r, which in enumerate(rounds):
                src = update if which == 0 else x
                for t in range(TT):
                    if which == 1 and update is not None:
                        dve.wait_ge(added, t + 1)
                    dve.bn_stats(stats[:, which, t, :], src[:, t, :]).then_inc(stat, 1)
                for t in range(TT):
                    dve.wait_ge(stat, r * TT + t + 1)
                    dve.bn_aggr(mv[:, which, t, :], stats[:, which, t, :]).then_inc(aggr, 1)
                dve.wait_ge(aggr, (r + 1) * TT)
                dve.tensor_scalar(var[:, which, :], mv[:, which, :, 1], LN_EPS, None, ALU.add).then_inc(vare, 1)
                dve.wait_ge(rs, r + 1)
                for t in range(TT):
                    if which == 0:
                        dve.tensor_scalar(update[:, t, :], update[:, t, :], mv[:, 0, t, 0:1], rstd[:, 0, t:t + 1],
                                          ALU.subtract, ALU.mult).then_inc(zr, 1)
                        dve.wait_ge(zr, t + 1)
                        dve.tensor_tensor(x[:, t, :], x[:, t, :], update[:, t, :], ALU.add).then_inc(added, 1)
                    else:
                        if t >= 2:
                            dve.wait_ge(tr, t - 1)
                        dve.tensor_scalar(z[:, t % 2, :], x[:, t, :], mv[:, 1, t, 0:1], rstd[:, 1, t:t + 1],
                                          ALU.subtract, ALU.mult).then_inc(zr, 1)
                        if t >= 1:
                            turn_lo(dve, t - 1)
                if which == 1:
                    turn_lo(dve, TT - 1)

        @block.gpsimd
        def _(pool):
            for r, which in enumerate(rounds):
                pool.wait_ge(vare, r + 1)
                pool.tensor_tensor(rstd[:, which, :], var[:, which, :], half[:, 0:TT], ALU.pow).then_inc(rs, 1)

        @block.tensor
        def _(pe):
            if xT is not None:
                for t in range(TT):
                    pe.wait_ge(zr, (nr - 1) * TT + t + 1)
                    if t >= 2:
                        pe.wait_ge(lo, t - 1)
                    for c in range(C):
                        last = pe.transpose(turned[t % 2][:, c * P:(c + 1) * P], z[:, t % 2, c * P:(c + 1) * P],
                                            ident[:])
                    last.then_inc(tr, 1)

        @block.scalar
        def _(act):
            if xT is not None:
                for t in range(TT):
                    act.wait_ge(tr, t + 1)
                    act.activation(xT.hi[:, :, t * P:(t + 1) * P],
                                   turned[t % 2][:].rearrange("p (c t) -> p c t", c=C), ACT.Copy).then_inc(hi, 1)


def attention_phase(p, ctx0, layer, xT, acc, ident, half):
    nc, a = p.nc, p.a
    causal = layer == 0
    L = f"l{layer}"
    if causal:
        first_bank = [("k", 0), ("v", 0), ("vt", 0), ("q", 0)]
        first_work = [("wk", 0), ("wv", 0), ("wq", 0), ("wq", 1)]
        tables = BANK0, BANK0_NEXT, WORK0, WORK0_NEXT, first_bank, first_work
    else:
        first_bank = [(m, 0, t) for m in "qk" for t in range(TB)]
        first_work = [(m, c) for m in ("wq", "wk", "wv") for c in range(C)]
        tables = BANK1, BANK1_NEXT, WORK1, WORK1_NEXT, first_bank, first_work
    HI = ("vt",) if causal else ("v", "tq", "tk")
    QK = ("q", "k")
    width = [(t + 1) * P if causal else S for t in range(TB)]
    with ExitStack() as ctx:
        sb = lambda n, s, dt=F32: p.sb(ctx, f"{L}_{n}", s, dt)
        split = lambda n, s: p.split(ctx, f"{L}_{n}", s)
        sem = lambda n: p.sem(ctx0, f"{L}_{n}")

        score = p.banks(ctx, f"{L}_score", 2)
        turned = p.banks(ctx, f"{L}_turned", 2)
        pv_bank, = p.banks(ctx, f"{L}_pv", 1)
        out_bank, = p.banks(ctx, f"{L}_out", 1)
        general = p.banks(ctx, f"{L}_general", 2)

        NPR = 3
        probs = sb("probs", [P, NPR, S])
        probsT = split("probsT", [P, TB, S])
        qT = split("qT", [P, 2, S])
        kT = split("kT", [P, 2, S])
        oT = split("oT", [P, S])
        w_out = split("w_out", [P, 2, D])
        stage = sb("stage", [P, 2, 512])
        negtop = sb("negtop", [P, TILES])
        total = sb("total", [P, TILES])
        inv = sb("inv", [P, TILES])

        s_score, s_negtop, s_exp, s_inv, s_norm, s_turn, s_turn_hi, s_turn_lo = map(
            sem, "score negtop exp inv norm turn turn_hi turn_lo".split())
        s_pv, s_o_hi, s_o_lo, s_out, s_added = map(sem, "pv o_hi o_lo out added".split())
        s_bank, s_bank_hi, s_free = map(sem, "bank bank_hi bank_free".split())
        s_stage = [sem("stage_even"), sem("stage_odd")]
        s_w_hi, s_w = sem("w_hi"), sem("w")
        s_const, s_zero = sem("const"), sem("zero")

        if causal:
            cos = sb("cos", [P, S])
            sin = sb("sin", [P, S])
            mask = sb("mask", [P, S])
            top = sb("top", [P, TILES])
            rope = sb("rope", [P, 2, 2, S])
            v_turn = sb("v_turn", [P, S])
            v = split("v", [P, B, TB * HD])
            w_q = split("w_q", [P, 2, C * HD])
            w_k = split("w_k", [P, C * HD])
            w_v = split("w_v", [P, C * HD])
            s_top, s_rope_mul, s_rope_add, s_rope_hi, s_rope_lo = map(
                sem, "top rope_mul rope_add rope_hi rope_lo".split())
        else:
            y = sb("y", [P, B, 2, TB, GH * HD])
            v = split("v", [P, TB, GH * HD])
            w_q = split("w_q", [P, C, GH * HD])
            w_k = split("w_k", [P, C, GH * HD])
            w_v = split("w_v", [P, C, GH * HD])
            b_qk = sb("b_qk", [P, 2, GH * HD])
            b_v = sb("b_v", [P, GH])
            gains = sb("gains", [P, 3])
            squares = sb("squares", [P, GH, HD])
            sumsq = sb("sumsq", [P, B, 2, TB * GH])
            meansq = sb("meansq", [P, B, 2, TB * GH])
            rrms = sb("rrms", [P, B, 2, TB * GH])
            s_sq, s_var, s_rrms, s_yn, s_gain = map(sem, "sq var rrms yn gain".split())
            s_bq, s_bk, s_bv = map(sem, "bq bk bv".split())

        def w_dest(x):
            kind, j = x
            if kind == "wo":
                return w_out[:, j % 2]
            w = {"wq": w_q, "wk": w_k, "wv": w_v}[kind]
            if causal:
                return w[:, j % 2] if kind == "wq" else w[:, :]
            return w[:, j]

        def w_source(i, x, group):
            kind, j = x
            if kind == "wo" or (causal and kind == "wq"):
                return a[f"{L}_{kind}"][group * GH + j % GH]
            return a[f"{L}_{kind}"][group] if causal else a[f"{L}_{kind}"][group * C + j]

        def loop(engine, body):
            with engine.Fori(0, NG - 1) as i:
                body(Body(i, False, *tables))
            body(Body(NG - 1, True, *tables))

        def parity(x, m, kinds=None):
            return m.parity(x, kinds) if m is not None else [
                y for y in first_bank if kinds is None or y[0] in kinds].index(x) % 2

        def done(x, m, kinds=None):
            return m.done(x, kinds) if m is not None else [
                y for y in first_bank if kinds is None or y[0] in kinds].index(x) + 1

        def work_done(x, m):
            return m.work_done(x) if m is not None else first_work.index(x) + 1

        block = ctx.enter_context(nc.Block())

        @block.sync
        def _(sp):
            def load(k, group, x, free):
                if free is not None:
                    sp.wait_ge(s_w, free)
                sp.dma_start(stage[:, k % 2], w_source(None, x, group)).then_inc(s_stage[k % 2], 16)

            for k, x in enumerate(first_work):
                load(k, 0, x, k - 1 if k >= 2 else None)
                if k == 1 and causal:
                    sp.dma_start(cos[:], a["cos"]).then_inc(s_const, 16)
                    sp.dma_start(sin[:], a["sin"]).then_inc(s_const, 16)
                    sp.dma_start(mask[:], a["mask"]).then_inc(s_const, 16)
                if k == 1 and not causal:
                    sp.dma_start(b_qk[:, 0], a["l1_bq"][0:1].to_broadcast([P, GH * HD])).then_inc(s_bq, 16)
                    sp.dma_start(b_qk[:, 1], a["l1_bk"][0:1].to_broadcast([P, GH * HD])).then_inc(s_bk, 16)
                    sp.dma_start(gains[:, 0:1], a["l1_gq"]).then_inc(s_const, 16)
                    sp.dma_start(gains[:, 1:2], a["l1_gk"]).then_inc(s_const, 16)
                    sp.dma_start(b_v[:], a["l1_bv"][0]).then_inc(s_bv, 16)

            def body(m):
                for step in range(-1, STEPS):
                    for x in m.work_at.get(step, []):
                        k = m.work_order.index(x)
                        load(k, m.i + 1 if x in m.next_work else m.i, x, m.work_start() + k - 1)
                    if not causal and not m.last and step in (13, 18):
                        r = (13, 18).index(step)
                        sp.wait_ge(s_free, m.done(("qk"[r], 1, TB - 1)))
                        sp.dma_start(b_qk[:, r], a[("l1_bq", "l1_bk")[r]][bass.ds(m.i + 1, 1)].to_broadcast(
                            [P, GH * HD])).then_inc((s_bq, s_bk)[r], 16)
                if not causal and not m.last:
                    sp.wait_ge(s_o_lo, (m.i + 1) * SLOTS)
                    sp.dma_start(b_v[:], a["l1_bv"][m.i + 1]).then_inc(s_bv, 16)

            loop(sp, body)

        @block.tensor
        def _(pe):
            def bank_use(x, m):
                kind = x[0]
                if m is not None or done(x, m) > 2:
                    pe.wait_ge(s_free, done(x, m) - 2)
                bank = general[parity(x, m)]
                if kind in ("tq", "tk"):
                    slot, r = x[1], kind == "tk"
                    par, h = slot // GH, slot % GH
                    if slot == GH:
                        pe.wait_ge(s_yn, m.i * 16 + 8 + 4 * (r + 1))
                    for t in range(TB):
                        last = pe.transpose(bank[:, t * P:(t + 1) * P], y[:, par, int(r), t, h * HD:(h + 1) * HD],
                                            ident[:])
                elif causal and kind == "vt":
                    pe.wait_ge(s_free, done(("v", x[1]), m))
                    for t in range(TB):
                        last = pe.transpose(bank[:, t * P:(t + 1) * P], v_turn[:, t * P:(t + 1) * P], ident[:])
                elif causal:
                    w = {"q": ("wq", x[1]), "k": ("wk", 0), "v": ("wv", 0)}[kind]
                    if m is None or (w in m.work_order and x not in (("k", 1), ("v", 1), ("q", 1))):
                        pe.wait_ge(s_w, work_done(w, m))
                    batch = x[1] // GH if kind == "q" else x[1]
                    left = w_dest(w)
                    for c in range(C):
                        last = product(nc, bank[:], left[:, c * HD:(c + 1) * HD],
                                       xT[:, c, batch * S:(batch + 1) * S], c == 0, c == C - 1)
                else:
                    batch, t = x[1], x[2]
                    w = {"q": w_q, "k": w_k, "v": w_v}[kind]
                    if kind != "v" and batch == 0 and t == 0:
                        pe.wait_ge(s_w, work_done((f"w{kind}", C - 1), m))
                    at = batch * S + t * P
                    for c in range(C):
                        last = product(nc, bank[:], xT[:, c, at:at + P], w[:, c], c == 0, c == C - 1)
                last.then_inc(s_bank, 1)

            for x in first_bank:
                bank_use(x, None)

            def body(m):
                n_tile, n_slot = m.i * TILES, m.i * SLOTS
                pe.wait_ge(s_w, m.work_start())
                pe.wait_ge(s_free, m.start())
                if causal:
                    pe.wait_ge(s_rope_lo, m.start(QK))
                else:
                    pe.wait_ge(s_yn, m.i * 16 + 8)
                for n in range(-1, STEPS):
                    if 0 <= n < TILES:
                        slot, t = divmod(n, TB)
                        if t == 0 and causal and slot > 0:
                            pe.wait_ge(s_rope_lo, m.done(("q", slot), QK))
                        if t == 0 and not causal:
                            pe.wait_ge(s_free, m.done(("tk", slot)))
                        if n >= 2:
                            pe.wait_ge(s_exp, n_tile + n - 1)
                        kp = slot // GH if causal else slot % 2
                        last = product(nc, score[n % 2][:, 0:width[t]], qT[:, slot % 2, t * P:(t + 1) * P],
                                       kT[:, kp, 0:width[t]])
                        last.then_inc(s_score, 1)
                    for x in m.bank_at.get(n, []):
                        bank_use(x, m)
                    if 0 <= n - OUT < TILES:
                        slot, t = divmod(n - OUT, TB)
                        if t == 0:
                            pe.wait_ge(s_o_lo, n_slot + slot + 1)
                            pe.wait_ge(s_w, m.work_done(("wo", slot)))
                        if n - OUT >= 1:
                            pe.wait_ge(s_added, n_tile + n - OUT)
                        last = product(nc, out_bank[:], oT[:, t * P:(t + 1) * P], w_out[:, slot % 2])
                        last.then_inc(s_out, 1)
                    if n >= PV and (n - PV) % TB == 0 and (n - PV) // TB < SLOTS:
                        slot = (n - PV) // TB
                        pe.wait_ge(s_turn_lo, n_tile + TB * (slot + 1))
                        if slot >= 1:
                            pe.wait_ge(s_o_lo, n_slot + slot)
                        h = slot % GH
                        if causal and slot == GH:
                            pe.wait_ge(s_free, m.done(("vt", 1)))
                        if not causal and h == 0:
                            pe.wait_ge(s_free, m.done(("v", slot // GH, TB - 1)))
                        for k in range(TB):
                            left = v[:, slot // GH, k * HD:(k + 1) * HD] if causal else v[:, k, h * HD:(h + 1) * HD]
                            q0 = k * P if causal else 0
                            last = product(nc, pv_bank[:, q0:S], left, probsT[:, k, q0:S], k == 0, k == TB - 1)
                        last.then_inc(s_pv, 1)
                    if 0 <= n - TURN < TILES:
                        j = n - TURN
                        pe.wait_ge(s_norm, n_tile + j + 1)
                        if j >= 2:
                            pe.wait_ge(s_turn_lo, n_tile + j - 1)
                        for k in range(width[j % TB] // P):
                            last = pe.transpose(turned[j % 2][:, k * P:(k + 1) * P],
                                                probs[:, j % NPR, k * P:(k + 1) * P], ident[:])
                        last.then_inc(s_turn, 1)

            loop(pe, body)

        @block.scalar
        def _(act):
            def work(x, m, k):
                free = {}
                if m is not None:
                    if x[0] == "wo" and x[1] >= 2:
                        act.wait_ge(s_out, m.i * TILES + TB * (x[1] - 1))
                    if causal:
                        user = {"wq": ("q", (x[1] - 2) % SLOTS), "wk": ("k", 1), "wv": ("v", 1)}.get(x[0])
                        if x == ("wq", 2):
                            act.wait_ge(s_bank, m.start())
                        elif user:
                            act.wait_ge(s_bank, m.done(user))
                    elif x[0] != "wo":
                        act.wait_ge(s_bank, m.done((x[0][1], 1, TB - 1)))
                w0 = m.work_start() if m is not None else 0
                act.wait_ge(s_stage[k % 2], 8 * (w0 + k - k % 2) + 16)
                act.activation(w_dest(x).hi, stage[:, k % 2], ACT.Copy).then_inc(s_w_hi, 1)

            def bank_hi(x, m):
                bank = general[parity(x, m)]
                if x[0] in HI:
                    act.wait_ge(s_bank, done(x, m))
                if x[0] == "vt":
                    act.activation(v.hi[:, x[1]], bank[:], ACT.Copy).then_inc(s_bank_hi, 1)
                elif x[0] == "v" and not causal:
                    act.wait_ge(s_pv, m.i * SLOTS + GH) if x[1] else None
                    act.activation(v.hi[:, x[2]], bank[:], ACT.Copy).then_inc(s_bank_hi, 1)
                elif x[0] == "tq":
                    act.activation(qT.hi[:, x[1] % 2], bank[:], ACT.Copy).then_inc(s_bank_hi, 1)
                elif x[0] == "tk":
                    act.activation(kT.hi[:, x[1] % 2], bank[:], ACT.Copy, scale=gains[:, 2:3]).then_inc(s_bank_hi, 1)

            def rope_hi(x, m):
                act.wait_ge(s_rope_add, done(x, m, QK))
                to = qT.hi[:, x[1] % 2] if x[0] == "q" else kT.hi[:, x[1]]
                act.activation(to, rope[:, parity(x, m, QK), 0], ACT.Copy).then_inc(s_rope_hi, 1)

            def square_count(x, m):
                if m is None:
                    return first_bank.index(x) + 1
                return m.i * 16 + 8 + (0 if x[1] else 8) + (4 if x[0] == "k" else 0) + x[2] + 1

            def square(x, m):
                act.wait_ge(s_free, done(x, m))
                r = int(x[0] == "k")
                n = square_count(x, m)
                if m is not None or n > 1:
                    act.wait_ge(s_sq, n - 1)
                for h in range(GH):
                    j = x[2] * GH + h
                    last = act.activation(squares[:, h], y[:, x[1], r, x[2], h * HD:(h + 1) * HD], ACT.Square,
                                          accum_out=sumsq[:, x[1], r, j:j + 1])
                last.then_inc(s_sq, 1)

            for k, x in enumerate(first_work):
                work(x, None, k)
            for x in first_bank:
                if x[0] in HI:
                    bank_hi(x, None)
                elif x[0] in QK:
                    rope_hi(x, None) if causal else square(x, None)
            if not causal:
                act.wait_ge(s_gain, 1)

            def body(m):
                n_tile, n_slot = m.i * TILES, m.i * SLOTS
                if not causal:
                    act.wait_ge(s_bv, (m.i + 1) * 16)
                for n in range(-1, STEPS):
                    if 0 <= n < TILES:
                        t = n % TB
                        act.wait_ge(s_negtop, n_tile + n + 1)
                        if n >= NPR:
                            act.wait_ge(s_turn, n_tile + n - NPR + 1)
                        act.activation(probs[:, n % NPR, 0:width[t]], score[n % 2][:, 0:width[t]], ACT.Exp,
                                       bias=negtop[:, n:n + 1], scale=SCALE if causal else 1.0,
                                       accum_out=total[:, n:n + 1]).then_inc(s_exp, 1)
                    for x in m.bank_at.get(n, []):
                        if x[0] in HI:
                            bank_hi(x, m)
                    if n >= PV and (n - PV) % TB == 0 and (n - PV) // TB < SLOTS:
                        slot = (n - PV) // TB
                        act.wait_ge(s_pv, n_slot + slot + 1)
                        if slot >= 1:
                            act.wait_ge(s_out, n_tile + TB * slot)
                        if causal:
                            act.activation(oT.hi[:], pv_bank[:], ACT.Copy).then_inc(s_o_hi, 1)
                        else:
                            h = slot % GH
                            act.activation(oT.hi[:], pv_bank[:], ACT.Identity, bias=b_v[:, h:h + 1]).then_inc(s_o_hi, 1)
                    if 0 <= n - TURN < TILES:
                        j = n - TURN
                        slot, t = divmod(j, TB)
                        kt = width[t] // P
                        act.wait_ge(s_turn, n_tile + j + 1)
                        if t == 0 and slot >= 1:
                            act.wait_ge(s_pv, n_slot + slot)
                        act.activation(probsT.hi[:, 0:kt, t * P:(t + 1) * P],
                                       turned[j % 2][:, 0:kt * P].rearrange("p (k q) -> p k q", k=kt),
                                       ACT.Copy).then_inc(s_turn_hi, 1)
                    for x in m.bank_at.get(n, []):
                        if x[0] in QK:
                            rope_hi(x, m) if causal else square(x, m)
                    for x in m.work_at.get(n, []):
                        work(x, m, m.work_order.index(x))

            loop(act, body)

        @block.vector
        def _(dve):
            def bank_use(x, m):
                bank, kind = general[parity(x, m)], x[0]
                if kind in HI:
                    dve.wait_ge(s_bank_hi, done(x, m, HI))
                else:
                    dve.wait_ge(s_bank, done(x, m))
                if causal and kind in QK:
                    r = parity(x, m, QK)
                    count = done(x, m, QK)
                    if m is not None:
                        dve.wait_ge(s_rope_lo, count - 2)
                    half_p = HD // 2
                    dve.tensor_tensor(rope[:, r, 0], bank[:], cos[:], ALU.mult)
                    dve.tensor_tensor(rope[0:half_p, r, 1], bank[half_p:HD, :], sin[half_p:HD, :], ALU.mult)
                    last = dve.tensor_tensor(rope[half_p:HD, r, 1], bank[0:half_p, :], sin[0:half_p, :], ALU.mult)
                elif causal and kind == "v":
                    last = dve.tensor_copy(v_turn[:], bank[:])
                elif kind == "vt":
                    last = rest(dve, v.lo[:, x[1]], bank[:], v.hi[:, x[1]])
                elif kind == "v":
                    last = rest(dve, v.lo[:, x[2]], bank[:], v.hi[:, x[2]])
                elif kind == "tq":
                    last = rest(dve, qT.lo[:, x[1] % 2], bank[:], qT.hi[:, x[1] % 2])
                elif kind == "tk":
                    last = dve.scalar_tensor_tensor(kT.lo[:, x[1] % 2], bank[:], gains[:, 2:3],
                                                    kT.hi[:, x[1] % 2].bitcast(F32), ALU.mult, ALU.subtract)
                else:
                    r = int(kind == "k")
                    if x[1:] == (0, 0):
                        dve.wait_ge((s_bq, s_bk)[r], 16 if m is None else (m.i + 2) * 16)
                    last = dve.tensor_tensor(y[:, x[1], r, x[2]], bank[:], b_qk[:, r], ALU.add)
                last.then_inc(s_free, 1)

            def norm(par, r, m):
                n = (r + 1) if m is None else m.i * 4 + 2 + (1 - par) * 2 + r + 1
                dve.wait_ge(s_sq, 4 * n)
                dve.tensor_scalar(meansq[:, par, r], sumsq[:, par, r], 1.0 / HD, RMS_EPS, ALU.mult, ALU.add)\
                    .then_inc(s_var, 1)

            for t in range(TT):
                last = dve.memset(acc[:, t], 0.0)
            last.then_inc(s_zero, 1)
            if causal:
                dve.wait_ge(s_const, 48)
            else:
                dve.wait_ge(s_const, 32)
                dve.scalar_tensor_tensor(gains[:, 2:3], gains[:, 0:1], SCALE, gains[:, 1:2], ALU.mult, ALU.mult)\
                    .then_inc(s_gain, 1)
            for x in first_bank:
                bank_use(x, None)
                if not causal and x[2] == TB - 1:
                    norm(0, int(x[0] == "k"), None)
            if not causal:
                dve.wait_ge(s_gain, 1)
            dve.wait_ge(s_zero, 1)

            def body(m):
                n_tile, n_slot = m.i * TILES, m.i * SLOTS
                for n in range(-1, STEPS):
                    if 0 <= n - 1 < TILES:
                        dve.wait_ge(s_exp, n_tile + n)
                        dve.reciprocal(inv[:, n - 1:n], total[:, n - 1:n]).then_inc(s_inv, 1)
                    if 0 <= n < TILES:
                        t = n % TB
                        dve.wait_ge(s_score, n_tile + n + 1)
                        if causal:
                            dve.nop(nofuse=True)
                            bank = score[n % 2][:, 0:width[t]]
                            dve.tensor_tensor_reduce(bank, bank, mask[:, S - width[t]:S], 1.0, MASKED, ALU.add, ALU.max,
                                                     top[:, n:n + 1]).then_inc(s_top, 1)
                            dve.wait_ge(s_top, n_tile + n + 1)
                            dve.tensor_scalar(negtop[:, n:n + 1], top[:, n:n + 1], -SCALE, None, ALU.mult)\
                                .then_inc(s_negtop, 1)
                        else:
                            dve.tensor_reduce(negtop[:, n:n + 1], score[n % 2][:], AXX, ALU.max, negate=True)\
                                .then_inc(s_negtop, 1)
                    for x in m.bank_at.get(n, []):
                        bank_use(x, m)
                    if 0 <= n - OUT < TILES:
                        slot, t = divmod(n - OUT, TB)
                        row = slot // GH * TB + t
                        dve.wait_ge(s_out, n_tile + n - OUT + 1)
                        dve.tensor_tensor(acc[:, row], out_bank[:], acc[:, row], ALU.add).then_inc(s_added, 1)
                    if n >= PV and (n - PV) % TB == 0 and (n - PV) // TB < SLOTS:
                        slot = (n - PV) // TB
                        dve.wait_ge(s_o_hi, n_slot + slot + 1)
                        if causal:
                            rest(dve, oT.lo[:], pv_bank[:], oT.hi[:]).then_inc(s_o_lo, 1)
                        else:
                            h = slot % GH
                            dve.scalar_tensor_tensor(oT.lo[:], pv_bank[:], b_v[:, h:h + 1], oT.hi[:].bitcast(F32),
                                                     ALU.add, ALU.subtract).then_inc(s_o_lo, 1)
                    if 0 <= n - TURN < TILES:
                        j = n - TURN
                        t = j % TB
                        kt = width[t] // P
                        dve.wait_ge(s_turn_hi, n_tile + j + 1)
                        rest(dve, probsT.lo[:, 0:kt, t * P:(t + 1) * P],
                             turned[j % 2][:, 0:kt * P].rearrange("p (k q) -> p k q", k=kt),
                             probsT.hi[:, 0:kt, t * P:(t + 1) * P]).then_inc(s_turn_lo, 1)
                    if not causal:
                        for x in m.bank_at.get(n - TO_NORM, []):
                            if x[0] in QK and x[2] == TB - 1:
                                norm(x[1], int(x[0] == "k"), m)

            loop(dve, body)

        @block.gpsimd
        def _(pool):
            def work(x, m, k):
                w0 = m.work_start() if m is not None else 0
                pool.wait_ge(s_w_hi, w0 + k + 1)
                rest(pool, w_dest(x).lo, stage[:, k % 2], w_dest(x).hi).then_inc(s_w, 1)

            def rope_add(x, m):
                r = parity(x, m, QK)
                pool.wait_ge(s_free, done(x, m))
                pool.tensor_tensor(rope[:, r, 0], rope[:, r, 0], rope[:, r, 1], ALU.add).then_inc(s_rope_add, 1)

            def rope_lo(x, m):
                r = parity(x, m, QK)
                pool.wait_ge(s_rope_hi, done(x, m, QK))
                hi, lo = (qT.hi[:, x[1] % 2], qT.lo[:, x[1] % 2]) if x[0] == "q" else (kT.hi[:, x[1]], kT.lo[:, x[1]])
                rest(pool, lo, rope[:, r, 0], hi).then_inc(s_rope_lo, 1)

            def norm(par, r, m):
                n = (r + 1) if m is None else m.i * 4 + 2 + (1 - par) * 2 + r + 1
                pool.wait_ge(s_var, n)
                pool.tensor_tensor(rrms[:, par, r], meansq[:, par, r], half[:], ALU.pow).then_inc(s_rrms, 1)
                pool.wait_ge(s_rrms, n)

            def scale(par, r, t):
                rows = y[:, par, r, t].rearrange("p (h d) -> p h d", h=GH)
                by = rrms[:, par, r, t * GH:(t + 1) * GH].unsqueeze(2).broadcast_to([P, GH, HD])
                pool.tensor_tensor(rows, rows, by, ALU.mult).then_inc(s_yn, 1)

            for k, x in enumerate(first_work):
                work(x, None, k)
            for x in first_bank:
                if causal and x[0] in QK:
                    rope_add(x, None)
                    rope_lo(x, None)
                if not causal and x[2] == TB - 1:
                    norm(0, int(x[0] == "k"), None)
                    for t in range(TB):
                        scale(0, int(x[0] == "k"), t)

            def body(m):
                n_tile = m.i * TILES
                for n in range(-1, STEPS):
                    if 0 <= n - 1 < TILES:
                        t = (n - 1) % TB
                        tile = probs[:, (n - 1) % NPR, 0:width[t]]
                        pool.wait_ge(s_inv, n_tile + n)
                        pool.nop(nofuse=True)
                        pool.tensor_scalar(tile, tile, inv[:, n - 1:n], 1.0, ALU.mult, ALU.mult).then_inc(s_norm, 1)
                    if causal:
                        for x in m.bank_at.get(n - 1, []):
                            if x[0] in QK:
                                rope_lo(x, m)
                        for x in m.bank_at.get(n, []):
                            if x[0] in QK:
                                rope_add(x, m)
                    else:
                        for x in m.bank_at.get(n - TO_NORM, []):
                            if x[0] in QK and x[2] == TB - 1:
                                norm(x[1], int(x[0] == "k"), m)
                        for t, d in enumerate(TO_SCALE):
                            for x in m.bank_at.get(n - d, []):
                                if x[0] in QK and x[2] == TB - 1:
                                    scale(x[1], int(x[0] == "k"), t)
                    for x in m.work_at.get(n, []):
                        work(x, m, m.work_order.index(x))

            loop(pool, body)


def linear_phase(p, ctx0, xT, acc):
    nc, a = p.nc, p.a
    NR = 8 * RK
    with ExitStack() as ctx:
        sb = lambda n, s, dt=F32: p.sb(ctx, f"lin_{n}", s, dt)
        split = lambda n, s: p.split(ctx, f"lin_{n}", s)
        sem = lambda n: p.sem(ctx0, f"lin_{n}")
        w_raw, a_raw, b_raw = sb("w_raw", [P, C, D]), sb("a_raw", [NR, D]), sb("b_raw", [NR, D])
        mix, bias, whole = sb("mix", [NR, 1]), sb("bias", [P, D]), sb("whole", [P, C, D])
        la, lb, w = split("la", [NR, D]), split("lb", [NR, D]), split("w", [P, C, D])
        merge, rows = p.banks(ctx, "lin_merge", 2), p.banks(ctx, "lin_rows", 2)
        s_a, s_b, s_w, s_bias = sem("a_in"), sem("b_in"), sem("w_in"), sem("bias_in")
        s_scaled, s_hi, s_lo, s_merged, s_whole, s_w_hi, s_w_lo, s_rows, s_taken = map(
            sem, "scaled hi lo merged whole w_hi w_lo rows taken".split())
        block = ctx.enter_context(nc.Block())

        @block.sync
        def _(sp):
            sp.dma_start(a_raw[:], a["l0_a"]).then_inc(s_a, 16)
            for n in range(8):
                sp.dma_start(mix[n * RK:(n + 1) * RK], a["l0_mix"][n:n + 1].to_broadcast([RK, 1])).then_inc(s_b, 16)
            sp.dma_start(b_raw[:], a["l0_b"]).then_inc(s_b, 16)
            sp.dma_start(w_raw[:], a["l0_w"].rearrange("(c p) o -> p c o", p=P)).then_inc(s_w, 16)
            sp.dma_start(bias[:], a["l0_bias"].to_broadcast([P, D])).then_inc(s_bias, 16)

        @block.scalar
        def _(act):
            act.wait_ge(s_a, 16)
            act.activation(la.hi[:], a_raw[:], ACT.Copy).then_inc(s_hi, 1)
            act.wait_ge(s_scaled, 1)
            act.activation(lb.hi[:], b_raw[:], ACT.Copy).then_inc(s_hi, 1)
            for c in range(C):
                act.wait_ge(s_whole, c + 1)
                act.activation(w.hi[:, c], whole[:, c], ACT.Copy).then_inc(s_w_hi, 1)

        @block.vector
        def _(dve):
            dve.wait_ge(s_b, 9 * 16)
            dve.tensor_scalar(b_raw[:], b_raw[:], mix[:], 2.0, ALU.mult, ALU.mult).then_inc(s_scaled, 1)
            dve.wait_ge(s_hi, 1)
            rest(dve, la.lo[:], a_raw[:], la.hi[:]).then_inc(s_lo, 1)
            dve.wait_ge(s_hi, 2)
            rest(dve, lb.lo[:], b_raw[:], lb.hi[:]).then_inc(s_lo, 1)
            dve.wait_ge(s_w, 16)
            for c in range(C):
                dve.wait_ge(s_merged, c + 1)
                dve.tensor_tensor(whole[:, c], merge[c % 2][:], w_raw[:, c], ALU.add).then_inc(s_whole, 1)
                dve.wait_ge(s_w_hi, c + 1)
                rest(dve, w.lo[:, c], whole[:, c], w.hi[:, c]).then_inc(s_w_lo, 1)
            dve.wait_ge(s_bias, 16)
            for t in range(TT):
                dve.wait_ge(s_rows, t + 1)
                dve.tensor_tensor(acc[:, t], rows[t % 2][:], bias[:], ALU.add).then_inc(s_taken, 1)

        @block.tensor
        def _(pe):
            pe.wait_ge(s_lo, 2)
            for c in range(C):
                if c >= 2:
                    pe.wait_ge(s_whole, c - 1)
                product(nc, merge[c % 2][:], la[:, c * P:(c + 1) * P], lb[:, :]).then_inc(s_merged, 1)
            pe.wait_ge(s_w_lo, C)
            for t in range(TT):
                if t >= 2:
                    pe.wait_ge(s_taken, t - 1)
                for c in range(C):
                    last = product(nc, rows[t % 2][:], xT[:, c, t * P:(t + 1) * P], w[:, c], c == 0, c == C - 1)
                last.then_inc(s_rows, 1)


def swiglu_phase(p, ctx0, xT, acc):
    nc, a = p.nc, p.a
    R3 = 96
    with ExitStack() as ctx:
        sb = lambda n, s, dt=F32: p.sb(ctx, f"ffn_{n}", s, dt)
        split = lambda n, s: p.split(ctx, f"ffn_{n}", s)
        sem = lambda n: p.sem(ctx0, f"ffn_{n}")
        w1, w3 = split("w1", [P, HT, C * P]), split("w3", [P, HT, C * P])
        w2 = split("w2", [P, HT, D])
        side_raw = acc[0:R3, 1:4]
        side = sb("side", [R3, 3, D], F32R)
        tile_raw = sb("tile_raw", [R3, 2, 3 * P])
        tile = sb("tile", [R3, 2, 3 * P], F32R)
        stage = sb("stage", [P, 3, 512])
        gate, gated = acc[:, TB], acc[:, TB + 1]
        gT = split("gT", [P, 2, S])
        merge, (h1, h3) = p.banks(ctx, "ffn_merge", 2), p.banks(ctx, "ffn_h", 2)
        rows = p.banks(ctx, "ffn_rows", TB)
        s_side, s_side_hi, s_side_lo = sem("side_in"), sem("side_hi"), sem("side_lo")
        s_tile = [sem("tile_even"), sem("tile_odd")]
        s_stage = [sem("w1_in"), sem("w3_in"), sem("w2_in")]
        s_tile_hi, s_tile_lo, s_merged, s_whole, s_w_hi, s_w_lo = map(
            sem, "tile_hi tile_lo merged whole w_hi w_lo".split())
        s_h1, s_h3, s_gate, s_gated, s_g_hi, s_g_lo, s_used, s_rows, s_taken = map(
            sem, "h1 h3 gate gated g_hi g_lo used rows taken".split())
        block = ctx.enter_context(nc.Block())
        weights = w1, w3, w2

        @block.sync
        def _(sp):
            for j, n in enumerate(("f_a1", "f_a3", "f_b2")):
                sp.dma_start(side_raw[:, j], a[n]).then_inc(s_side, 16)
            for o in range(HT):
                if o >= 2:
                    sp.wait_ge(s_tile_lo, o - 1)
                sp.dma_start(tile_raw[:, o % 2], a["f_tile"][o]).then_inc(s_tile[o % 2], 16)
                for j in range(3):
                    if o >= 1:
                        sp.wait_ge(s_w_lo, 3 * (o - 1) + j + 1)
                    sp.dma_start(stage[:, j], a[("f_w1", "f_w3", "f_w2")[j]][o]).then_inc(s_stage[j], 16)

        @block.tensor
        def _(pe):
            def prepare(o):
                pe.wait_ge(s_tile_lo, o + 1)
                for j in range(3):
                    k = 3 * o + j
                    if k >= 2:
                        pe.wait_ge(s_whole, k - 1)
                    low = tile[:, o % 2, j * P:(j + 1) * P]
                    if j < 2:
                        for c in range(C):
                            last = pe.matmul(merge[k % 2][:, c * P:(c + 1) * P], side[:, j, c * P:(c + 1) * P], low,
                                             start=True, stop=True, skip_group_check=True)
                    else:
                        last = pe.matmul(merge[k % 2][:], low, side[:, j], start=True, stop=True)
                    last.then_inc(s_merged, 1)

            def down(b, o):
                n = b * HT + o
                pe.wait_ge(s_g_lo, n + 1)
                if b == 0:
                    pe.wait_ge(s_w_lo, 3 * o + 3)
                if b == 1 and o == 0:
                    pe.wait_ge(s_taken, TB)
                for t in range(TB):
                    last = product(nc, rows[t][:], gT[:, n % 2, t * P:(t + 1) * P], w2[:, o], o == 0, o == HT - 1)
                last.then_inc(s_rows if o == HT - 1 else s_used, 1)

            pe.wait_ge(s_side_lo, 1)
            prepare(0)
            prepare(1)
            for b in range(B):
                for o in range(HT):
                    n = b * HT + o
                    for j, (h, s_h, out_of) in enumerate(((h1, s_h1, s_gate), (h3, s_h3, s_gated))):
                        if b == 0:
                            pe.wait_ge(s_w_lo, 3 * o + j + 1)
                        if n >= 1:
                            pe.wait_ge(out_of, n)
                        for c in range(C):
                            last = product(nc, h[:], weights[j][:, o, c * P:(c + 1) * P],
                                           xT[:, c, b * S:(b + 1) * S], c == 0, c == C - 1)
                        last.then_inc(s_h, 1)
                    if b == 0 and o + 2 < HT:
                        prepare(o + 2)
                    if n >= 1:
                        down(*divmod(n - 1, HT))
            down(B - 1, HT - 1)

        @block.scalar
        def _(act):
            def tile_hi(o):
                act.wait_ge(s_tile[o % 2], 16 * (o // 2 + 1))
                if o >= 2:
                    act.wait_ge(s_merged, 3 * (o - 1))
                act.activation(tile[:, o % 2], tile_raw[:, o % 2], ACT.Copy).then_inc(s_tile_hi, 1)

            def whole_hi(o):
                for j in range(3):
                    act.wait_ge(s_whole, 3 * o + j + 1)
                    act.activation(weights[j].hi[:, o], stage[:, j], ACT.Copy).then_inc(s_w_hi, 1)

            act.wait_ge(s_side, 48)
            act.activation(side[:], side_raw, ACT.Copy, scale=2.0).then_inc(s_side_hi, 1)
            tile_hi(0)
            tile_hi(1)
            whole_hi(0)
            for b in range(B):
                for o in range(HT):
                    n = b * HT + o
                    if b == 0:
                        if o + 2 < HT:
                            tile_hi(o + 2)
                        if o + 1 < HT:
                            whole_hi(o + 1)
                    act.wait_ge(s_h1, n + 1)
                    if n >= 1:
                        act.wait_ge(s_gated, n)
                    act.activation(gate, h1[:], ACT.Silu).then_inc(s_gate, 1)
                    act.wait_ge(s_gated, n + 1)
                    if n >= 2:
                        done_b, done_o = divmod(n - 2, HT)
                        if done_o == HT - 1:
                            act.wait_ge(s_rows, done_b + 1)
                        else:
                            act.wait_ge(s_used, n - 1 - done_b)
                    act.activation(gT.hi[:, n % 2], gated, ACT.Copy).then_inc(s_g_hi, 1)
                    if n == HT:
                        act.wait_ge(s_rows, 1)
                        for t in range(TB):
                            last = act.activation(acc[:, t], rows[t][:], ACT.Copy).then_inc(s_taken, 1)
            act.wait_ge(s_rows, B)
            for t in range(TB):
                act.activation(acc[:, TB + t], rows[t][:], ACT.Copy).then_inc(s_taken, 1)

        @block.vector
        def _(dve):
            def tile_lo(o):
                dve.wait_ge(s_tile_hi, o + 1)
                dve.tensor_tensor(tile[64:96, o % 2], tile_raw[64:96, o % 2], tile[64:96, o % 2].bitcast(F32),
                                  ALU.subtract).then_inc(s_tile_lo, 1)

            def whole(o):
                for j in range(3):
                    k = 3 * o + j
                    dve.wait_ge(s_stage[j], 16 * (o + 1))
                    dve.wait_ge(s_merged, k + 1)
                    dve.tensor_tensor(stage[:, j], merge[k % 2][:], stage[:, j], ALU.add).then_inc(s_whole, 1)

            dve.wait_ge(s_side_hi, 1)
            dve.scalar_tensor_tensor(side[32:64], side_raw[32:64], 2.0, side[32:64].bitcast(F32), ALU.mult,
                                     ALU.subtract).then_inc(s_side_lo, 1)
            tile_lo(0)
            tile_lo(1)
            whole(0)
            for b in range(B):
                for o in range(HT):
                    n = b * HT + o
                    if b == 0:
                        if o + 2 < HT:
                            tile_lo(o + 2)
                        if o + 1 < HT:
                            whole(o + 1)
                    dve.wait_ge(s_gate, n + 1)
                    dve.wait_ge(s_h3, n + 1)
                    if n >= 1:
                        dve.wait_ge(s_g_lo, n)
                    dve.tensor_tensor(gated, h3[:], gate, ALU.mult).then_inc(s_gated, 1)
                    dve.wait_ge(s_g_hi, n + 1)
                    rest(dve, gT.lo[:, n % 2], gated, gT.hi[:, n % 2]).then_inc(s_g_lo, 1)

        @block.gpsimd
        def _(pool):
            for o in range(HT):
                for j in range(3):
                    pool.wait_ge(s_w_hi, 3 * o + j + 1)
                    rest(pool, weights[j].lo[:, o], stage[:, j], weights[j].hi[:, o]).then_inc(s_w_lo, 1)


def build(nc, a, out, upto=99):
    p = Program(nc, a, out, upto)
    with ExitStack() as ctx:
        ident = p.sb(ctx, "ident", [P, P])
        half = p.sb(ctx, "half", [P, TB * GH])
        acc = p.sb(ctx, "acc", [P, TT, D])
        xT = p.split(ctx, "xT", [P, C, T])
        made = p.sem(ctx, "made")
        x_rows = a["x"].rearrange("(t p) d -> p t d", p=P)
        out_rows = out.rearrange("(t p) d -> p t d", p=P)
        kept = nc.dram_tensor("x_kept", [T, D], F32, kind="Internal").ap().rearrange("(t p) d -> p t d", p=P)

        with nc.Block() as block:
            @block.gpsimd
            def _(pool):
                pool.memset(ident[:], 0.0).then_inc(made, 1)
                pool.wait_ge(made, 1)
                pool.affine_select(out=ident[:], in_=ident[:], compare_op=ALU.not_equal, fill=1.0, base=0,
                                   pattern=[[-1, P]], channel_multiplier=1).then_inc(made, 1)
                pool.memset(half[:], -0.5).then_inc(made, 1)
                pool.wait_ge(made, 3)

        def normed(name, **how):
            with ExitStack() as inner:
                x = p.sb(inner, f"{name}_x", [P, TT, D])
                norm_phase(p, ctx, name, x, ident=ident, half=half, **how)

        normed("norm0", xT=xT, load=x_rows)
        if upto == 0: return dump(p, ctx, xT.hi[:, 0:4, :].rearrange("p c t -> p (c t)").bitcast(F32), xT)
        attention_phase(p, ctx, 0, xT, acc, ident, half)
        if upto == 1: return dump(p, ctx, acc[:].rearrange("p t d -> p (t d)"), acc)
        normed("norm1", xT=xT, update=acc, load=x_rows, store=kept)
        linear_phase(p, ctx, xT, acc)
        if upto == 2: return dump(p, ctx, acc[:].rearrange("p t d -> p (t d)"), acc)
        normed("norm2", xT=xT, update=acc, load=kept, store=kept)
        attention_phase(p, ctx, 1, xT, acc, ident, half)
        if upto == 3: return dump(p, ctx, acc[:].rearrange("p t d -> p (t d)"), acc)
        normed("norm3", xT=xT, update=acc, load=kept, store=kept, bias=a["l1_bo"])
        swiglu_phase(p, ctx, xT, acc)
        if upto == 4: return dump(p, ctx, acc[:].rearrange("p t d -> p (t d)"), acc)
        normed("norm4", xT=None, update=acc, load=kept, store=out_rows)


def dump(p, ctx, src, t):
    s = p.sem(ctx, "dump")
    with p.nc.Block() as block:
        @block.sync
        def _(sp):
            sp.dma_start(p.out.rearrange("(p t) d -> p (t d)", p=P), src).then_inc(s, 16)
            sp.wait_ge(s, 16)


def layout(v):
    import numpy as np

    f = {k: np.asarray(x) for k, x in v.items()}
    tall = lambda w, n: w.T.reshape(C, P, n, HD).transpose(2, 1, 0, 3).reshape(n, P, C * HD)
    wide = lambda w: w.reshape(C, P, NG, GH * HD).transpose(2, 0, 1, 3).reshape(NG * C, P, GH * HD)
    inv_freq = (1.0 / np.float32(10000.0) ** (np.arange(0, HD, 2, dtype=np.float32) / np.float32(HD)))
    angle = np.arange(S, dtype=np.float32)[None, :] * inv_freq.astype(np.float32)[:, None]
    c, s = np.cos(angle), np.sin(angle)
    ahead = np.arange(P)[None, :] > np.arange(P)[:, None]
    out = {
        "x": f["L0_attn_hidden_states"].reshape(T, D),
        "l0_wq": tall(f["L0_attn_Wq"], NH), "l0_wk": tall(f["L0_attn_Wk"], NG), "l0_wv": tall(f["L0_attn_Wv"], NG),
        "l0_wo": f["L0_attn_Wo"].T.reshape(NH, HD, D),
        "cos": np.concatenate([c, c]), "sin": np.concatenate([s, -s]),
        "mask": np.concatenate([np.zeros((P, S - P)), np.where(ahead, MASKED, 0.0)], axis=1),
        "l0_w": f["L0_ffn_W"].T, "l0_a": f["L0_ffn_lora_A"].reshape(8 * RK, D),
        "l0_b": f["L0_ffn_lora_B"].transpose(0, 2, 1).reshape(8 * RK, D), "l0_bias": f["L0_ffn_bias"].reshape(1, D),
        "l0_mix": f["L0_ffn_lora_weights"].reshape(8, 1),
        "l1_wq": wide(f["L1_attn_Wq"]), "l1_wk": wide(f["L1_attn_Wk"]), "l1_wv": wide(f["L1_attn_Wv"]),
        "l1_wo": f["L1_attn_Wo"].reshape(NH, HD, D),
        "l1_bq": f["L1_attn_bq"].reshape(NG, GH * HD), "l1_bk": f["L1_attn_bk"].reshape(NG, GH * HD),
        "l1_bv": f["L1_attn_bv"].reshape(NG, GH, HD).transpose(0, 2, 1), "l1_bo": f["L1_attn_bo"].reshape(1, D),
        "l1_gq": f["L1_attn_gq"].reshape(HD, 1), "l1_gk": f["L1_attn_gk"].reshape(HD, 1),
    }

    def padded(w):
        return np.concatenate([w, np.zeros((w.shape[0], HP - HID), w.dtype)], axis=1)

    def thrice(w):
        three = np.zeros((3, 32, w.shape[1]), w.dtype)
        three[:, :RK] = w
        return three.reshape(96, w.shape[1])

    for n in "13":
        out[f"f_w{n}"] = padded(f[f"L1_ffn_w{n}"].T).reshape(C, P, HT, P).transpose(2, 1, 0, 3).reshape(HT, P, C * P)
        out[f"f_a{n}"] = thrice(f[f"L1_ffn_lora_A{n}"])
    out["f_w2"] = padded(f["L1_ffn_w2"]).T.reshape(HT, P, D)
    out["f_b2"] = thrice(f["L1_ffn_lora_B2"].T)
    ranks = f["L1_ffn_lora_B1"].T, f["L1_ffn_lora_B3"].T, f["L1_ffn_lora_A2"]
    out["f_tile"] = np.stack([thrice(padded(w)).reshape(96, HT, P) for w in ranks]).transpose(2, 1, 0, 3).reshape(
        HT, 96, 3 * P)
    return {k: np.ascontiguousarray(x, dtype=np.float32) for k, x in out.items()}


def kernel(**inputs):
    import concourse.bacc as bacc
    from concourse.bass_utils import run_bass_kernel_spmd

    nc = bacc.Bacc("TRN2", target_bir_lowering=False, num_devices=1)
    arrays = layout(inputs)
    a = {k: nc.dram_tensor(k, x.shape, F32, kind="ExternalInput").ap() for k, x in arrays.items()}
    out = nc.dram_tensor("out", (T, D), F32, kind="ExternalOutput").ap()
    build(nc, a, out)
    r = run_bass_kernel_spmd(nc, [arrays], core_ids=[0])
    return r.results[0]["out"].reshape(B, S, D)
```

```python
from contextlib import ExitStack

import concourse.bass as bass
from concourse import mybir

ALU = mybir.AluOpType
ACT = mybir.ActivationFunctionType
AXX = mybir.AxisListType.X
F32 = mybir.dt.float32
F32R = mybir.dt.float32r

P = 128
B, S, D = 2, 512, 512
T = B * S
TT = T // P
TB = S // P
C = D // P
HD = 128
NH = 32
GH = 4
NG = NH // GH
SLOTS = GH * B
TILES = SLOTS * TB
HID = 1376
HT = -(-HID // P)
HP = HT * P
RK = 16
SCALE = float(HD) ** -0.5
LN_EPS = 1e-5
RMS_EPS = 1e-6
MASKED = -2.0 ** 100

TURN, EVAC, PV, OUT = 2, 3, 7, 8
TAIL = OUT + TILES


def steps_of(*items):
    by = {}
    for step, item in sorted(items, key=lambda x: x[0]):
        by.setdefault(step, []).append(item)
    return by


def in_order(by):
    return [x for step in sorted(by) for x in by[step]]


FIRST_BANK0 = [("k", 0), ("v", 0), ("vt", 0), ("q", 0)]
BANK0 = [(4 * s - 3, ("q", s)) for s in range(1, SLOTS)] + [(7, ("k", 1)), (11, ("v", 1)), (15, ("vt", 1))]
BANK0_NEXT = [(19, ("k", 0)), (23, ("v", 0)), (27, ("vt", 0)), (29, ("q", 0))]
FIRST_WORK0 = [("wk", 0), ("wv", 0), ("wq", 0), ("wq", 1)]
WORK0 = [(4 * s + 3, ("wo", s)) for s in range(SLOTS)] + [(4 * s - 6, ("wq", s)) for s in range(2, SLOTS)]
WORK0_NEXT = [(12, ("wk", 0)), (16, ("wv", 0)), (24, ("wq", 0)), (28, ("wq", 1))]

FIRST_BANK1 = ([(m, 0, t) for m in "qk" for t in range(TB)] + [("q", 1, t) for t in range(TB)]
               + [("tq", 0), ("tk", 0)])
BANK1 = ([(4 * s - 3, ("tq", s)) for s in range(1, SLOTS)]
         + [(4 * s - 2, ("tk", s)) for s in range(1, SLOTS)]
         + [(n, ("k", 1, t)) for t, n in enumerate((0, 1, 2, 8))]
         + [(TB * GH * b + PV - TB + t, ("v", b, t)) for b in range(B) for t in range(TB)])
BANK1_NEXT = ([(n, ("q", 0, t)) for t, n in enumerate((10, 12, 13, 14))]
              + [(n, ("k", 0, t)) for t, n in enumerate((16, 17, 18, 24))]
              + [(n, ("q", 1, t)) for t, n in enumerate((26, 28, 29, 30))]
              + [(29, ("tq", 0)), (30, ("tk", 0))])
FIRST_WORK1 = [(m, c) for m in ("wq", "wk", "wv") for c in range(C)]
WORK1 = [(4 * s + 3, ("wo", s)) for s in range(SLOTS)]
WORK1_NEXT = [(n, (kind, c)) for kind, at in (("wq", (1, 2, 4, 6)), ("wk", (9, 10, 12, 13)),
                                              ("wv", (24, 26, 28, 30))) for c, n in enumerate(at)]
TO_NORM, TO_SCALE = 1, (1, 2, 2, 3)
QK = ("q", "k")


def any_use(x):
    return True


def of_qk(x):
    return x[0] in QK


def last_of_qk(x):
    return x[0] in QK and x[2] == TB - 1


class Before:

    def __init__(self, first_bank, first_work):
        self.order, self.work_order = first_bank, first_work

    def done(self, x, kind=any_use):
        return sum(map(kind, self.order[:self.order.index(x) + 1]))

    def parity(self, x, kind=any_use):
        return (self.done(x, kind) - kind(x)) % 2

    def work_done(self, x):
        return self.work_order.index(x) + 1


class Body:

    def __init__(self, i, first, last, bank, bank_next, work, work_next, before):
        self.i, self.first, self.last = i, first, last
        self.bank_at = steps_of(*bank, *([] if last else bank_next))
        self.work_at = steps_of(*work, *([] if last else work_next))
        self.order = in_order(self.bank_at)
        self.work_order = in_order(self.work_at)
        self.whole = in_order(steps_of(*bank, *bank_next))
        self.n_work = len(work) + len(work_next)
        self.before = before
        self.next_work = {x for _, x in work_next}
        self.prev = before if first else Body(i - 1, True, False, bank, bank_next, work, work_next, before)

    def start(self, kind=any_use):
        return self.i * sum(map(kind, self.whole)) + sum(map(kind, self.before.order))

    def done(self, x, kind=any_use):
        return self.start(kind) + sum(map(kind, self.order[:self.order.index(x) + 1]))

    def parity(self, x, kind=any_use):
        return sum(map(kind, self.order[:self.order.index(x)])) % 2

    def work_start(self):
        return self.i * self.n_work + len(self.before.work_order)

    def work_done(self, x):
        return self.work_start() + self.work_order.index(x) + 1

    def uses(self, n):
        if n >= 0 or self.first:
            return [(x, self) for x in self.bank_at.get(n, [])]
        return [(x, self.prev) for x in self.prev.bank_at.get(n + TILES, [])]

    def lagged(self, n, of=TILES):
        return n < of and (n >= 0 or not self.first)

    def steps(self):
        return range(TAIL if self.last else TILES)

    def slot_at(self, n, lag):
        slot, t = divmod(n - lag, TB)
        return slot if t == 0 and self.lagged(slot, SLOTS) else None


def wait_past(engine, sem, m, per, count):
    if m.first and not (isinstance(count, int) and count > 0):
        return
    engine.wait_ge(sem, m.i * per + count)


class Split:

    def __init__(self, hi, lo):
        self.hi, self.lo = hi, lo

    def __getitem__(self, at):
        return Split(self.hi[at], self.lo[at])

    @property
    def passes(self):
        return self.hi, self.lo


def product(nc, out, left, right, first=True, last=True):
    nc.tensor.matmul(out, left.hi, right.lo, start=first, stop=False, skip_group_check=True)
    nc.tensor.matmul(out, left.lo, right.hi, start=False, stop=False, skip_group_check=True)
    return nc.tensor.matmul(out, left.hi, right.hi, start=False, stop=last, skip_group_check=True)


def rest(engine, out, full, hi):
    return engine.tensor_tensor(out, full, hi.bitcast(F32), ALU.subtract)


class Program:

    def __init__(self, nc, a):
        self.nc, self.a = nc, a

    def sb(self, ctx, name, shape, dt=F32):
        return ctx.enter_context(self.nc.sbuf_tensor(name, shape, dt))

    def split(self, ctx, name, shape):
        return Split(self.sb(ctx, name + "_hi", shape, F32R), self.sb(ctx, name + "_lo", shape, F32R))

    def banks(self, ctx, name, n):
        return [ctx.enter_context(self.nc.psum_tensor(f"{name}{i}", [P, 512], F32)) for i in range(n)]

    def sem(self, ctx, name):
        return ctx.enter_context(self.nc.semaphore(name))


def norm_phase(p, ctx0, name, x, xT, ident, half, update=None, load=None, store=None, bias=None):
    nc = p.nc
    with ExitStack() as ctx:
        sb = lambda n, s, dt=F32: p.sb(ctx, f"{name}_{n}", s, dt)
        sem = lambda n: p.sem(ctx0, f"{name}_{n}")
        rounds = ([0] if update is not None else []) + ([1] if xT is not None else [])
        stats = sb("stats", [P, 2, TT, 6])
        mv = sb("mv", [P, 2, TT, 2])
        var = sb("var", [P, 2, TT])
        rstd = sb("rstd", [P, 2, TT])
        z = sb("z", [P, 2, D])
        turned = p.banks(ctx, f"{name}_turned", 2)
        x_in, stat, aggr, vare, rs, zr, added = map(sem, "x_in stat aggr vare rs zr added".split())
        if xT is not None:
            tr, hi, lo = sem("tr"), sem("hi"), sem("lo")
        if store is not None:
            stored = sem("stored")
        if bias is not None:
            bias_in, biased = sem("bias_in"), sem("biased")
        if bias is not None:
            brow = sb("brow", [P, D])
        block = ctx.enter_context(nc.Block())
        nr = len(rounds)

        @block.sync
        def _(sp):
            if load is not None:
                sp.dma_start(x[:], load).then_inc(x_in, 16)
            if bias is not None:
                sp.dma_start(brow[:], bias.to_broadcast([P, D])).then_inc(bias_in, 16)
            if store is not None:
                sp.wait_ge(added, TT)
                sp.dma_start(store, x[:]).then_inc(stored, 16)
                sp.wait_ge(stored, 16)

        def turn_lo(dve, t):
            dve.wait_ge(hi, t + 1)
            rest(dve, xT.lo[:, :, t * P:(t + 1) * P], turned[t % 2][:].rearrange("p (c t) -> p c t", c=C),
                 xT.hi[:, :, t * P:(t + 1) * P]).then_inc(lo, 1)

        @block.vector
        def _(dve):
            if bias is not None:
                dve.wait_ge(bias_in, 16)
                for t in range(TT):
                    dve.tensor_tensor(update[:, t, :], update[:, t, :], brow[:], ALU.add).then_inc(biased, 1)
                dve.wait_ge(biased, TT)
            if load is not None:
                dve.wait_ge(x_in, 16)
            for r, which in enumerate(rounds):
                src = update if which == 0 else x
                for t in range(TT):
                    if which == 1 and update is not None:
                        dve.wait_ge(added, t + 1)
                    dve.bn_stats(stats[:, which, t, :], src[:, t, :]).then_inc(stat, 1)
                for t in range(TT):
                    dve.wait_ge(stat, r * TT + t + 1)
                    dve.bn_aggr(mv[:, which, t, :], stats[:, which, t, :]).then_inc(aggr, 1)
                dve.wait_ge(aggr, (r + 1) * TT)
                dve.tensor_scalar(var[:, which, :], mv[:, which, :, 1], LN_EPS, None, ALU.add).then_inc(vare, 1)
                dve.wait_ge(rs, r + 1)
                for t in range(TT):
                    if which == 0:
                        dve.tensor_scalar(update[:, t, :], update[:, t, :], mv[:, 0, t, 0:1], rstd[:, 0, t:t + 1],
                                          ALU.subtract, ALU.mult).then_inc(zr, 1)
                        dve.wait_ge(zr, t + 1)
                        dve.tensor_tensor(x[:, t, :], x[:, t, :], update[:, t, :], ALU.add).then_inc(added, 1)
                    else:
                        if t >= 2:
                            dve.wait_ge(tr, t - 1)
                        dve.tensor_scalar(z[:, t % 2, :], x[:, t, :], mv[:, 1, t, 0:1], rstd[:, 1, t:t + 1],
                                          ALU.subtract, ALU.mult).then_inc(zr, 1)
                        if t >= 1:
                            turn_lo(dve, t - 1)
                if which == 1:
                    turn_lo(dve, TT - 1)

        @block.gpsimd
        def _(pool):
            for r, which in enumerate(rounds):
                pool.wait_ge(vare, r + 1)
                pool.tensor_tensor(rstd[:, which, :], var[:, which, :], half[:, 0:TT], ALU.pow).then_inc(rs, 1)

        @block.tensor
        def _(pe):
            if xT is not None:
                for t in range(TT):
                    pe.wait_ge(zr, (nr - 1) * TT + t + 1)
                    if t >= 2:
                        pe.wait_ge(lo, t - 1)
                    for c in range(C):
                        last = pe.transpose(turned[t % 2][:, c * P:(c + 1) * P], z[:, t % 2, c * P:(c + 1) * P],
                                            ident[:])
                    last.then_inc(tr, 1)

        @block.scalar
        def _(act):
            if xT is not None:
                for t in range(TT):
                    act.wait_ge(tr, t + 1)
                    act.activation(xT.hi[:, :, t * P:(t + 1) * P],
                                   turned[t % 2][:].rearrange("p (c t) -> p c t", c=C), ACT.Copy).then_inc(hi, 1)


def attention_phase(p, ctx0, layer, xT, acc, ident, half):
    nc, a = p.nc, p.a
    causal = layer == 0
    L = f"l{layer}"
    tables = ((BANK0, BANK0_NEXT, WORK0, WORK0_NEXT, Before(FIRST_BANK0, FIRST_WORK0)) if causal
              else (BANK1, BANK1_NEXT, WORK1, WORK1_NEXT, Before(FIRST_BANK1, FIRST_WORK1)))
    before = tables[-1]
    HI = ("vt",) if causal else ("v", "tq", "tk")

    def of_hi(x):
        return x[0] in HI

    width = [(t + 1) * P if causal else S for t in range(TB)]
    with ExitStack() as ctx:
        sb = lambda n, s, dt=F32: p.sb(ctx, f"{L}_{n}", s, dt)
        split = lambda n, s: p.split(ctx, f"{L}_{n}", s)
        sem = lambda n: p.sem(ctx0, f"{L}_{n}")

        score = p.banks(ctx, f"{L}_score", 2)
        turned = p.banks(ctx, f"{L}_turned", 2)
        pv_bank, = p.banks(ctx, f"{L}_pv", 1)
        out_bank, = p.banks(ctx, f"{L}_out", 1)
        general = p.banks(ctx, f"{L}_general", 2)

        NPR = 4
        probs = sb("probs", [P, NPR, S])
        probsT = split("probsT", [P, TB, S])
        qT = split("qT", [P, 2, S])
        kT = split("kT", [P, 2, S])
        oT = split("oT", [P, S])
        w_out = split("w_out", [P, 2, D])
        stage = sb("stage", [P, 2, 512])
        negtop = sb("negtop", [P, TILES])
        total = sb("total", [P, TILES])
        inv = sb("inv", [P, TILES])

        s_score, s_negtop, s_exp, s_inv, s_norm, s_turn, s_turn_hi, s_turn_lo = map(
            sem, "score negtop exp inv norm turn turn_hi turn_lo".split())
        s_pv, s_o_hi, s_o_lo, s_out, s_added = map(sem, "pv o_hi o_lo out added".split())
        s_bank, s_bank_hi, s_free = map(sem, "bank bank_hi bank_free".split())
        s_stage = [sem("stage_even"), sem("stage_odd")]
        s_w_hi, s_w = sem("w_hi"), sem("w")
        s_const, s_zero = sem("const"), sem("zero")

        if causal:
            trig = sb("trig", [P, 4, S])
            mask_raw = sb("mask_raw", [P, P])
            mask = sb("mask", [P, P], F32R)
            ident_r = sb("ident_r", [P, P], F32R)
            s_mask = sem("mask")
            rope = sb("rope", [P, 2, 2, S])
            v_turn = sb("v_turn", [P, S])
            v = split("v", [P, B, TB * HD])
            w_q = split("w_q", [P, 2, C * HD])
            w_k = split("w_k", [P, C * HD])
            w_v = split("w_v", [P, C * HD])
            s_rope_swap, s_rope_sin, s_rope_add, s_rope_hi, s_rope_lo = map(
                sem, "rope_swap rope_sin rope_add rope_hi rope_lo".split())
        else:
            y = sb("y", [P, B, 2, TB, GH * HD])
            v = split("v", [P, TB, GH * HD])
            w_q = split("w_q", [P, C, GH * HD])
            w_k = split("w_k", [P, C, GH * HD])
            w_v = split("w_v", [P, C, GH * HD])
            b_qk = sb("b_qk", [P, 2, GH * HD])
            b_v = sb("b_v", [P, GH])
            b_v_all = sb("b_v_all", [P, NH])
            gains = sb("gains", [P, 3])
            squares = sb("squares", [P, GH, HD])
            sumsq = sb("sumsq", [P, B, 2, TB * GH])
            meansq = sb("meansq", [P, B, 2, TB * GH])
            s_sq, s_var, s_rrms, s_yn, s_gain = map(sem, "sq var rrms yn gain".split())
            s_bq, s_bk, s_bv = map(sem, "bq bk bv".split())

        def w_dest(x):
            kind, j = x
            if kind == "wo":
                return w_out[:, j % 2]
            w = {"wq": w_q, "wk": w_k, "wv": w_v}[kind]
            if causal:
                return w[:, j % 2] if kind == "wq" else w[:, :]
            return w[:, j]

        def w_source(x, group):
            kind, j = x
            if kind == "wo" or (causal and kind == "wq"):
                return a[f"{L}_{kind}"][group * GH + j % GH]
            return a[f"{L}_{kind}"][group] if causal else a[f"{L}_{kind}"][group * C + j]

        def loop(engine, body):
            body(Body(0, True, False, *tables))
            with engine.Fori(1, NG - 1) as i:
                body(Body(i, False, False, *tables))
            body(Body(NG - 1, False, True, *tables))

        block = ctx.enter_context(nc.Block())

        @block.sync
        def _(sp):
            def load(k, group, x, free):
                if free is not None:
                    sp.wait_ge(s_w, free)
                sp.dma_start(stage[:, k % 2], w_source(x, group)).then_inc(s_stage[k % 2], 16)

            for k, x in enumerate(before.work_order):
                load(k, 0, x, k - 1 if k >= 2 else None)
                if k == 1 and causal:
                    sp.dma_start(trig[:], a["trig"]).then_inc(s_const, 16)
                    sp.dma_start(mask_raw[:], a["mask"]).then_inc(s_const, 16)
                if k == 1 and not causal:
                    sp.dma_start(b_qk[:, 0], a["l1_bq"][0:1].to_broadcast([P, GH * HD])).then_inc(s_bq, 16)
                    sp.dma_start(b_qk[:, 1], a["l1_bk"][0:1].to_broadcast([P, GH * HD])).then_inc(s_bk, 16)
                    sp.dma_start(gains[:, 0:1], a["l1_gq"]).then_inc(s_const, 16)
                    sp.dma_start(gains[:, 1:2], a["l1_gk"]).then_inc(s_const, 16)
                    sp.dma_start(b_v_all[:], a["l1_bv"]).then_inc(s_const, 16)

            def body(m):
                for n in range(TILES):
                    for x in m.work_at.get(n, []):
                        k = m.work_order.index(x)
                        load(k, m.i + 1 if x in m.next_work else m.i, x, m.work_start() + k - 1)
                    if not causal and not m.last and n in (1, 9):
                        if n == 1:
                            sp.wait_ge(s_free, m.start())
                        else:
                            sp.wait_ge(s_free, m.done(("k", 1, TB - 1)))
                        r = int(n == 9)
                        sp.dma_start(b_qk[:, r], a[("l1_bq", "l1_bk")[r]][bass.ds(m.i + 1, 1)].to_broadcast(
                            [P, GH * HD])).then_inc((s_bq, s_bk)[r], 16)

            loop(sp, body)

        @block.tensor
        def _(pe):
            def bank_use(x, m, part=range(C)):
                kind = x[0]
                if 0 in part and (m is not before or m.done(x) > 2):
                    pe.wait_ge(s_free, m.done(x) - 2)
                bank = general[m.parity(x)]
                if kind in ("tq", "tk"):
                    slot, r = x[1], int(kind == "tk")
                    par, h = slot // GH, slot % GH
                    if h == 0:
                        pe.wait_ge(s_yn, (m.prev if (kind, slot) == ("tq", GH) else m).done(
                            ("qk"[r], par, TB - 1), of_qk))
                    for t in range(TB):
                        last = pe.transpose(bank[:, t * P:(t + 1) * P], y[:, par, r, t, h * HD:(h + 1) * HD],
                                            ident[:])
                elif causal and kind == "vt":
                    pe.wait_ge(s_free, m.done(("v", x[1])))
                    for t in range(TB):
                        last = pe.transpose(bank[:, t * P:(t + 1) * P], v_turn[:, t * P:(t + 1) * P], ident[:])
                elif causal:
                    w = {"q": ("wq", x[1]), "k": ("wk", 0), "v": ("wv", 0)}[kind]
                    if 0 in part:
                        own = m is before or x not in (("q", 1), ("k", 1), ("v", 1))
                        pe.wait_ge(s_w, (m if own else m.prev).work_done(w))
                    batch = x[1] // GH if kind == "q" else x[1]
                    left = w_dest(w)
                    for c in part:
                        last = product(nc, bank[:], left[:, c * HD:(c + 1) * HD],
                                       xT[:, c, batch * S:(batch + 1) * S], c == 0, c == C - 1)
                else:
                    batch, t = x[1], x[2]
                    w = {"q": w_q, "k": w_k, "v": w_v}[kind]
                    if batch == 0 and t == 0:
                        pe.wait_ge(s_w, (m.prev if kind == "v" else m).work_done((f"w{kind}", C - 1)))
                    at = batch * S + t * P
                    for c in range(C):
                        last = product(nc, bank[:], xT[:, c, at:at + P], w[:, c], c == 0, c == C - 1)
                if C - 1 in part:
                    last.then_inc(s_bank, 1)

            def halves(x):
                return causal and x[0] != "vt"

            for x in before.order:
                bank_use(x, before)
            if causal:
                pe.wait_ge(s_mask, 2)

            def body(m):
                for n in m.steps():
                    if n < TILES:
                        slot, t = divmod(n, TB)
                        if t == 0:
                            own = m.prev if slot == 0 else m
                            if causal:
                                pe.wait_ge(s_rope_lo, own.done(("q", slot), of_qk))
                            else:
                                pe.wait_ge(s_free, own.done(("tk", slot)))
                        wait_past(pe, s_exp, m, TILES, n - 1)
                        kp = slot // GH if causal else slot % 2
                        last = product(nc, score[n % 2][:, 0:width[t]], qT[:, slot % 2, t * P:(t + 1) * P],
                                       kT[:, kp, 0:width[t]])
                        if causal:
                            last = pe.matmul(score[n % 2][:, t * P:(t + 1) * P], ident_r[:], mask[:], start=False,
                                             stop=True, skip_group_check=True)
                        last.then_inc(s_score, 1)
                    if m.lagged(n - OUT):
                        slot, t = divmod(n - OUT, TB)
                        if t == 0:
                            own = m if slot >= 0 else m.prev
                            pe.wait_ge(s_w, own.work_done(("wo", slot % SLOTS)))
                            wait_past(pe, s_o_lo, m, SLOTS, slot + 1)
                        wait_past(pe, s_added, m, TILES, n - OUT)
                        last = product(nc, out_bank[:], oT[:, t * P:(t + 1) * P], w_out[:, slot % 2])
                        last.then_inc(s_out, 1)
                    slot = m.slot_at(n, PV)
                    if slot is not None:
                        wait_past(pe, s_turn_lo, m, TILES, TB * (slot + 1))
                        wait_past(pe, s_o_lo, m, SLOTS, slot)
                        b, h = divmod(slot % SLOTS, GH)
                        own = m if slot >= 0 else m.prev
                        if causal and h == 0:
                            pe.wait_ge(s_free, (m if b else m.prev).done(("vt", b)))
                        if not causal and h == 0:
                            pe.wait_ge(s_free, own.done(("v", b, TB - 1)))
                        for k in range(TB):
                            left = v[:, b, k * HD:(k + 1) * HD] if causal else v[:, k, h * HD:(h + 1) * HD]
                            q0 = k * P if causal else 0
                            last = product(nc, pv_bank[:, q0:S], left, probsT[:, k, q0:S], k == 0, k == TB - 1)
                        last.then_inc(s_pv, 1)
                    for x, _ in m.uses(n) if n < TILES else []:
                        bank_use(x, m, range(C // 2, C) if halves(x) else range(C))
                    if m.lagged(n - TURN):
                        j = n - TURN
                        wait_past(pe, s_norm, m, TILES, j + 1)
                        wait_past(pe, s_turn_lo, m, TILES, j - 1)
                        for k in range(width[j % TB] // P):
                            last = pe.transpose(turned[j % 2][:, k * P:(k + 1) * P],
                                                probs[:, j % NPR, k * P:(k + 1) * P], ident[:])
                        last.then_inc(s_turn, 1)
                    for x in m.bank_at.get(n + 1, []):
                        if halves(x):
                            bank_use(x, m, range(C // 2))

            loop(pe, body)

        @block.scalar
        def _(act):
            def work(x, m, k):
                if m is before:
                    start = 0
                else:
                    start = m.work_start()
                    if x[0] == "wo":
                        wait_past(act, s_out, m, TILES, TB * (x[1] - 1))
                    elif causal:
                        user = {"wq": ("q", (x[1] - 2) % SLOTS), "wk": ("k", 1), "wv": ("v", 1)}[x[0]]
                        act.wait_ge(s_bank, (m.prev if x == ("wq", 2) else m).done(user))
                    elif x[0] == "wq":
                        act.wait_ge(s_bank, m.start())
                    else:
                        act.wait_ge(s_bank, m.done((x[0][1], 1, TB - 1)))
                act.wait_ge(s_stage[k % 2], 8 * (start + k - k % 2) + 16)
                act.activation(w_dest(x).hi, stage[:, k % 2], ACT.Copy).then_inc(s_w_hi, 1)

            def bank_hi(x, m):
                bank = general[m.parity(x)]
                if x[0] in HI:
                    act.wait_ge(s_bank, m.done(x))
                if x[0] == "vt":
                    act.activation(v.hi[:, x[1]], bank[:], ACT.Copy).then_inc(s_bank_hi, 1)
                elif x[0] == "v" and not causal:
                    wait_past(act, s_pv, m, SLOTS, x[1] * GH)
                    act.activation(v.hi[:, x[2]], bank[:], ACT.Copy).then_inc(s_bank_hi, 1)
                elif x[0] == "tq":
                    act.activation(qT.hi[:, x[1] % 2], bank[:], ACT.Copy).then_inc(s_bank_hi, 1)
                elif x[0] == "tk":
                    act.activation(kT.hi[:, x[1] % 2], bank[:], ACT.Copy, scale=gains[:, 2:3]).then_inc(s_bank_hi, 1)

            def rope_swap(x, m):
                r, count = m.parity(x, of_qk), m.done(x, of_qk)
                act.wait_ge(s_bank, m.done(x))
                if m is not before:
                    act.wait_ge(s_rope_add, count - 2)
                bank, h = general[m.parity(x)], HD // 2
                act.activation(rope[0:h, r, 1], bank[h:HD, :], ACT.Copy)
                act.activation(rope[h:HD, r, 1], bank[0:h, :], ACT.Copy).then_inc(s_rope_swap, 1)

            def rope_hi(x, m):
                act.wait_ge(s_rope_add, m.done(x, of_qk))
                to = qT.hi[:, x[1] % 2] if x[0] == "q" else kT.hi[:, x[1]]
                act.activation(to, rope[:, m.parity(x, of_qk), 0], ACT.Copy).then_inc(s_rope_hi, 1)

            def square(x, m):
                act.wait_ge(s_free, m.done(x))
                r = int(x[0] == "k")
                n = m.done(x, of_qk)
                if m is not before or n > 1:
                    act.wait_ge(s_sq, n - 1)
                for h in range(GH):
                    j = x[2] * GH + h
                    last = act.activation(squares[:, h], y[:, x[1], r, x[2], h * HD:(h + 1) * HD], ACT.Square,
                                          accum_out=sumsq[:, x[1], r, j:j + 1])
                last.then_inc(s_sq, 1)

            if not causal:
                act.wait_ge(s_gain, 1)
            for k, x in enumerate(before.work_order):
                work(x, before, k)
            for x in before.order:
                if x[0] in HI:
                    bank_hi(x, before)
                elif x[0] in QK and causal:
                    rope_swap(x, before)
                    rope_hi(x, before)
                elif x[0] in QK:
                    square(x, before)

            def exponentials(m, n):
                t = n % TB
                act.wait_ge(s_negtop, m.i * TILES + n + 1)
                wait_past(act, s_turn, m, TILES, n - NPR + 1)
                act.activation(probs[:, n % NPR, 0:width[t]], score[n % 2][:, 0:width[t]], ACT.Exp,
                               bias=negtop[:, n:n + 1], accum_out=total[:, n:n + 1]).then_inc(s_exp, 1)

            def turned_hi(m, j):
                slot, t = divmod(j, TB)
                kt = width[t] // P
                wait_past(act, s_turn, m, TILES, j + 1)
                if t == 0:
                    wait_past(act, s_pv, m, SLOTS, slot)
                act.activation(probsT.hi[:, 0:kt, t * P:(t + 1) * P],
                               turned[j % 2][:, 0:kt * P].rearrange("p (k q) -> p k q", k=kt),
                               ACT.Copy).then_inc(s_turn_hi, 1)

            def output_hi(m, slot):
                wait_past(act, s_pv, m, SLOTS, slot + 1)
                wait_past(act, s_out, m, TILES, TB * slot)
                if causal:
                    act.activation(oT.hi[:], pv_bank[:], ACT.Copy).then_inc(s_o_hi, 1)
                else:
                    h = slot % GH
                    if 0 <= slot < GH:
                        act.wait_ge(s_bv, m.i * GH + h + 1)
                    act.activation(oT.hi[:], pv_bank[:], ACT.Identity, bias=b_v[:, h:h + 1]).then_inc(s_o_hi, 1)

            def body(m):
                for n in m.steps():
                    slot = m.slot_at(n, PV)
                    if slot is None and m.lagged(n - EVAC):
                        turned_hi(m, n - EVAC)
                    if n < TILES:
                        exponentials(m, n)
                    if slot is not None:
                        output_hi(m, slot)
                        if m.lagged(n - EVAC):
                            turned_hi(m, n - EVAC)
                    for x, own in m.uses(n - 1):
                        if x[0] in QK:
                            rope_hi(x, own) if causal else square(x, own)
                    for x in m.work_at.get(n, []):
                        work(x, m, m.work_order.index(x))
                    for x, own in m.uses(n):
                        if x[0] in HI:
                            bank_hi(x, own)
                        elif causal and x[0] in QK:
                            rope_swap(x, own)

            loop(act, body)

        @block.vector
        def _(dve):
            def bank_use(x, m):
                bank, kind = general[m.parity(x)], x[0]
                if kind in HI:
                    dve.wait_ge(s_bank_hi, m.done(x, of_hi))
                else:
                    dve.wait_ge(s_bank, m.done(x))
                if causal and kind in QK:
                    r = m.parity(x, of_qk)
                    count = m.done(x, of_qk)
                    if m is not before:
                        dve.wait_ge(s_rope_lo, count - 2)
                    dve.wait_ge(s_rope_swap, count)
                    last = dve.tensor_tensor(rope[:, r, 0], bank[:], trig[:, 2 * (kind == "q")], ALU.mult)
                elif causal and kind == "v":
                    last = dve.tensor_copy(v_turn[:], bank[:])
                elif kind == "vt":
                    last = rest(dve, v.lo[:, x[1]], bank[:], v.hi[:, x[1]])
                elif kind == "v":
                    last = rest(dve, v.lo[:, x[2]], bank[:], v.hi[:, x[2]])
                elif kind == "tq":
                    last = rest(dve, qT.lo[:, x[1] % 2], bank[:], qT.hi[:, x[1] % 2])
                elif kind == "tk":
                    last = dve.scalar_tensor_tensor(kT.lo[:, x[1] % 2], bank[:], gains[:, 2:3],
                                                    kT.hi[:, x[1] % 2].bitcast(F32), ALU.mult, ALU.subtract)
                else:
                    r = int(kind == "k")
                    if x[1:] == (0, 0):
                        dve.wait_ge((s_bq, s_bk)[r], 16 if m is before else (m.i + 2) * 16)
                    last = dve.tensor_tensor(y[:, x[1], r, x[2]], bank[:], b_qk[:, r], ALU.add)
                last.then_inc(s_free, 1)

            def norm(x, m):
                at = slice(None), x[1], int(x[0] == "k")
                dve.wait_ge(s_sq, m.done(x, of_qk))
                dve.tensor_scalar(meansq[at], sumsq[at], 1.0 / HD, RMS_EPS, ALU.mult, ALU.add).then_inc(s_var, 1)

            for t in range(TT):
                last = dve.memset(acc[:, t], 0.0)
            last.then_inc(s_zero, 1)
            if causal:
                dve.wait_ge(s_const, 32)
                dve.tensor_copy(mask[:], mask_raw[:]).then_inc(s_mask, 1)
                dve.tensor_copy(ident_r[:], ident[:]).then_inc(s_mask, 1)
            else:
                dve.wait_ge(s_const, 48)
                dve.scalar_tensor_tensor(gains[:, 2:3], gains[:, 0:1], SCALE, gains[:, 1:2], ALU.mult, ALU.mult)\
                    .then_inc(s_gain, 1)
                dve.wait_ge(s_gain, 1)
            for x in before.order:
                bank_use(x, before)
                if not causal and last_of_qk(x):
                    norm(x, before)
            dve.wait_ge(s_zero, 1)

            def turned_lo(m, j):
                t = j % TB
                kt = width[t] // P
                wait_past(dve, s_turn_hi, m, TILES, j + 1)
                rest(dve, probsT.lo[:, 0:kt, t * P:(t + 1) * P],
                     turned[j % 2][:, 0:kt * P].rearrange("p (k q) -> p k q", k=kt),
                     probsT.hi[:, 0:kt, t * P:(t + 1) * P]).then_inc(s_turn_lo, 1)

            def add_rows(m, j):
                slot, t = divmod(j % TILES, TB)
                row = slot // GH * TB + t
                wait_past(dve, s_out, m, TILES, j + 1)
                dve.tensor_tensor(acc[:, row], out_bank[:], acc[:, row], ALU.add).then_inc(s_added, 1)

            def output_lo(m, slot):
                wait_past(dve, s_o_hi, m, SLOTS, slot + 1)
                if causal:
                    rest(dve, oT.lo[:], pv_bank[:], oT.hi[:]).then_inc(s_o_lo, 1)
                else:
                    h = slot % GH
                    dve.scalar_tensor_tensor(oT.lo[:], pv_bank[:], b_v[:, h:h + 1], oT.hi[:].bitcast(F32),
                                             ALU.add, ALU.subtract).then_inc(s_o_lo, 1)

            def body(m):
                for n in m.steps():
                    if m.lagged(n - 1):
                        j = (n - 1) % TILES
                        wait_past(dve, s_exp, m, TILES, n)
                        dve.reciprocal(inv[:, j:j + 1], total[:, j:j + 1]).then_inc(s_inv, 1)
                    if n < TILES:
                        dve.wait_ge(s_score, m.i * TILES + n + 1)
                        dve.tensor_reduce(negtop[:, n:n + 1], score[n % 2][:, 0:width[n % TB]], AXX, ALU.max,
                                          negate=True).then_inc(s_negtop, 1)
                    slot = m.slot_at(n, PV)
                    if slot is None and m.lagged(n - EVAC):
                        turned_lo(m, n - EVAC)
                    if m.lagged(n - OUT):
                        add_rows(m, n - OUT)
                    if slot is not None:
                        output_lo(m, slot)
                        if m.lagged(n - EVAC):
                            turned_lo(m, n - EVAC)
                    for x, own in m.uses(n):
                        bank_use(x, own)
                    if not causal:
                        for x, own in m.uses(n - TO_NORM):
                            if last_of_qk(x):
                                norm(x, own)
                        h, t = divmod(n, TB)
                        if t == 1 and h < GH:
                            dve.tensor_copy(b_v[:, h:h + 1], b_v_all[:, bass.ds(m.i * GH + h, 1)]).then_inc(s_bv, 1)

            loop(dve, body)

        @block.gpsimd
        def _(pool):
            def work(x, m, k):
                w0 = m.work_start() if m is not before else 0
                pool.wait_ge(s_w_hi, w0 + k + 1)
                rest(pool, w_dest(x).lo, stage[:, k % 2], w_dest(x).hi).then_inc(s_w, 1)

            def rope_add(x, m):
                r, count = m.parity(x, of_qk), m.done(x, of_qk)
                pool.wait_ge(s_rope_swap, count)
                pool.tensor_tensor(rope[:, r, 1], rope[:, r, 1], trig[:, 2 * (x[0] == "q") + 1], ALU.mult)\
                    .then_inc(s_rope_sin, 1)
                pool.wait_ge(s_rope_sin, count)
                pool.wait_ge(s_free, m.done(x))
                pool.tensor_tensor(rope[:, r, 0], rope[:, r, 0], rope[:, r, 1], ALU.add).then_inc(s_rope_add, 1)

            def rope_lo(x, m):
                r = m.parity(x, of_qk)
                pool.wait_ge(s_rope_hi, m.done(x, of_qk))
                hi, lo = (qT.hi[:, x[1] % 2], qT.lo[:, x[1] % 2]) if x[0] == "q" else (kT.hi[:, x[1]], kT.lo[:, x[1]])
                rest(pool, lo, rope[:, r, 0], hi).then_inc(s_rope_lo, 1)

            def norm(x, m):
                at = slice(None), x[1], int(x[0] == "k")
                n = m.done(x, last_of_qk)
                pool.wait_ge(s_var, n)
                pool.tensor_tensor(meansq[at], meansq[at], half[:], ALU.pow).then_inc(s_rrms, 1)
                pool.wait_ge(s_rrms, n)

            def scale(x, t):
                par, r = x[1], int(x[0] == "k")
                rows = y[:, par, r, t].rearrange("p (h d) -> p h d", h=GH)
                by = meansq[:, par, r, t * GH:(t + 1) * GH].unsqueeze(2).broadcast_to([P, GH, HD])
                pool.tensor_tensor(rows, rows, by, ALU.mult).then_inc(s_yn, 1)

            for k, x in enumerate(before.work_order):
                work(x, before, k)
            for x in before.order:
                if causal and x[0] in QK:
                    rope_add(x, before)
                    rope_lo(x, before)
                if not causal and last_of_qk(x):
                    norm(x, before)
                    for t in range(TB):
                        scale(x, t)

            def body(m):
                for n in m.steps():
                    if m.lagged(n - 1):
                        j = (n - 1) % TILES
                        tile = probs[:, j % NPR, 0:width[j % TB]]
                        wait_past(pool, s_inv, m, TILES, n)
                        pool.nop(nofuse=True)
                        pool.tensor_scalar(tile, tile, inv[:, j:j + 1], 1.0, ALU.mult, ALU.mult).then_inc(s_norm, 1)
                    if causal:
                        for x, own in m.uses(n - 2):
                            if x[0] in QK:
                                rope_lo(x, own)
                    else:
                        for x, own in m.uses(n - TO_NORM):
                            if last_of_qk(x):
                                norm(x, own)
                        for t, d in enumerate(TO_SCALE):
                            for x, own in m.uses(n - d):
                                if last_of_qk(x):
                                    scale(x, t)
                    for x in m.work_at.get(n, []):
                        work(x, m, m.work_order.index(x))
                    for x, own in m.uses(n) if causal else []:
                        if x[0] in QK:
                            rope_add(x, own)

            loop(pool, body)


def linear_phase(p, ctx0, xT, acc):
    nc, a = p.nc, p.a
    NR = 8 * RK
    with ExitStack() as ctx:
        sb = lambda n, s, dt=F32: p.sb(ctx, f"lin_{n}", s, dt)
        split = lambda n, s: p.split(ctx, f"lin_{n}", s)
        sem = lambda n: p.sem(ctx0, f"lin_{n}")
        w_raw, a_raw, b_raw = sb("w_raw", [P, C, D]), sb("a_raw", [NR, D]), sb("b_raw", [NR, D])
        mix, bias, whole = sb("mix", [NR, 1]), sb("bias", [P, D]), sb("whole", [P, C, D])
        la, lb, w = split("la", [NR, D]), split("lb", [NR, D]), split("w", [P, C, D])
        merge, rows = p.banks(ctx, "lin_merge", 2), p.banks(ctx, "lin_rows", 2)
        s_a, s_b, s_w, s_bias = sem("a_in"), sem("b_in"), sem("w_in"), sem("bias_in")
        s_scaled, s_hi, s_lo, s_merged, s_whole, s_w_hi, s_w_lo, s_rows, s_taken = map(
            sem, "scaled hi lo merged whole w_hi w_lo rows taken".split())
        block = ctx.enter_context(nc.Block())

        @block.sync
        def _(sp):
            sp.dma_start(a_raw[:], a["l0_a"]).then_inc(s_a, 16)
            for n in range(8):
                sp.dma_start(mix[n * RK:(n + 1) * RK], a["l0_mix"][n:n + 1].to_broadcast([RK, 1])).then_inc(s_b, 16)
            sp.dma_start(b_raw[:], a["l0_b"]).then_inc(s_b, 16)
            sp.dma_start(w_raw[:], a["l0_w"].rearrange("(c p) o -> p c o", p=P)).then_inc(s_w, 16)
            sp.dma_start(bias[:], a["l0_bias"].to_broadcast([P, D])).then_inc(s_bias, 16)

        @block.scalar
        def _(act):
            act.wait_ge(s_a, 16)
            act.activation(la.hi[:], a_raw[:], ACT.Copy).then_inc(s_hi, 1)
            act.wait_ge(s_scaled, 1)
            act.activation(lb.hi[:], b_raw[:], ACT.Copy).then_inc(s_hi, 1)
            for c in range(C):
                act.wait_ge(s_whole, c + 1)
                act.activation(w.hi[:, c], whole[:, c], ACT.Copy).then_inc(s_w_hi, 1)

        @block.vector
        def _(dve):
            dve.wait_ge(s_b, 9 * 16)
            dve.tensor_scalar(b_raw[:], b_raw[:], mix[:], 2.0, ALU.mult, ALU.mult).then_inc(s_scaled, 1)
            dve.wait_ge(s_hi, 1)
            rest(dve, la.lo[:], a_raw[:], la.hi[:]).then_inc(s_lo, 1)
            dve.wait_ge(s_hi, 2)
            rest(dve, lb.lo[:], b_raw[:], lb.hi[:]).then_inc(s_lo, 1)
            dve.wait_ge(s_w, 16)
            for c in range(C):
                dve.wait_ge(s_merged, c + 1)
                dve.tensor_tensor(whole[:, c], merge[c % 2][:], w_raw[:, c], ALU.add).then_inc(s_whole, 1)
                dve.wait_ge(s_w_hi, c + 1)
                rest(dve, w.lo[:, c], whole[:, c], w.hi[:, c]).then_inc(s_w_lo, 1)
            dve.wait_ge(s_bias, 16)
            for t in range(TT):
                dve.wait_ge(s_rows, t + 1)
                dve.tensor_tensor(acc[:, t], rows[t % 2][:], bias[:], ALU.add).then_inc(s_taken, 1)

        @block.tensor
        def _(pe):
            pe.wait_ge(s_lo, 2)
            for c in range(C):
                if c >= 2:
                    pe.wait_ge(s_whole, c - 1)
                product(nc, merge[c % 2][:], la[:, c * P:(c + 1) * P], lb[:, :]).then_inc(s_merged, 1)
            pe.wait_ge(s_w_lo, C)
            for t in range(TT):
                if t >= 2:
                    pe.wait_ge(s_taken, t - 1)
                for c in range(C):
                    last = product(nc, rows[t % 2][:], xT[:, c, t * P:(t + 1) * P], w[:, c], c == 0, c == C - 1)
                last.then_inc(s_rows, 1)


def swiglu_phase(p, ctx0, xT, acc):
    nc, a = p.nc, p.a
    R3 = 96
    with ExitStack() as ctx:
        sb = lambda n, s, dt=F32: p.sb(ctx, f"ffn_{n}", s, dt)
        split = lambda n, s: p.split(ctx, f"ffn_{n}", s)
        sem = lambda n: p.sem(ctx0, f"ffn_{n}")
        w1, w3 = split("w1", [P, HT, C * P]), split("w3", [P, HT, C * P])
        w2 = split("w2", [P, HT, D])
        side_raw = acc[0:R3, 1:4]
        side = sb("side", [R3, 3, D], F32R)
        tile_raw = sb("tile_raw", [R3, 2, 3 * P])
        tile = sb("tile", [R3, 2, 3 * P], F32R)
        stage = sb("stage", [P, 3, 512])
        gate, gated = acc[:, TB], acc[:, TB + 1]
        gT = split("gT", [P, 2, S])
        merge, (h1, h3) = p.banks(ctx, "ffn_merge", 2), p.banks(ctx, "ffn_h", 2)
        rows = p.banks(ctx, "ffn_rows", TB)
        s_side, s_side_hi, s_side_lo = sem("side_in"), sem("side_hi"), sem("side_lo")
        s_tile = [sem("tile_even"), sem("tile_odd")]
        s_stage = [sem("w1_in"), sem("w3_in"), sem("w2_in")]
        s_tile_hi, s_tile_lo, s_merged, s_whole, s_w_hi, s_w_lo = map(
            sem, "tile_hi tile_lo merged whole w_hi w_lo".split())
        s_h1, s_h3, s_gate, s_gated, s_g_hi, s_g_lo, s_used, s_rows, s_taken = map(
            sem, "h1 h3 gate gated g_hi g_lo used rows taken".split())
        block = ctx.enter_context(nc.Block())
        weights = w1, w3, w2

        @block.sync
        def _(sp):
            for j, n in enumerate(("f_a1", "f_a3", "f_b2")):
                sp.dma_start(side_raw[:, j], a[n]).then_inc(s_side, 16)
            for o in range(HT):
                if o >= 2:
                    sp.wait_ge(s_tile_lo, o - 1)
                sp.dma_start(tile_raw[:, o % 2], a["f_tile"][o]).then_inc(s_tile[o % 2], 16)
                for j in range(3):
                    if o >= 1:
                        sp.wait_ge(s_w_lo, 3 * (o - 1) + j + 1)
                    sp.dma_start(stage[:, j], a[("f_w1", "f_w3", "f_w2")[j]][o]).then_inc(s_stage[j], 16)

        @block.tensor
        def _(pe):
            def prepare(o):
                pe.wait_ge(s_tile_lo, o + 1)
                for j in range(3):
                    k = 3 * o + j
                    if k >= 2:
                        pe.wait_ge(s_whole, k - 1)
                    low = tile[:, o % 2, j * P:(j + 1) * P]
                    if j < 2:
                        for c in range(C):
                            last = pe.matmul(merge[k % 2][:, c * P:(c + 1) * P], side[:, j, c * P:(c + 1) * P], low,
                                             start=True, stop=True, skip_group_check=True)
                    else:
                        last = pe.matmul(merge[k % 2][:], low, side[:, j], start=True, stop=True)
                    last.then_inc(s_merged, 1)

            def down(b, o):
                n = b * HT + o
                pe.wait_ge(s_g_lo, n + 1)
                if b == 0:
                    pe.wait_ge(s_w_lo, 3 * o + 3)
                if b == 1 and o == 0:
                    pe.wait_ge(s_taken, TB)
                for t in range(TB):
                    last = product(nc, rows[t][:], gT[:, n % 2, t * P:(t + 1) * P], w2[:, o], o == 0, o == HT - 1)
                last.then_inc(s_rows if o == HT - 1 else s_used, 1)

            pe.wait_ge(s_side_lo, 1)
            prepare(0)
            prepare(1)
            for b in range(B):
                for o in range(HT):
                    n = b * HT + o
                    for j, (h, s_h, out_of) in enumerate(((h1, s_h1, s_gate), (h3, s_h3, s_gated))):
                        if b == 0:
                            pe.wait_ge(s_w_lo, 3 * o + j + 1)
                        if n >= 1:
                            pe.wait_ge(out_of, n)
                        for c in range(C):
                            last = product(nc, h[:], weights[j][:, o, c * P:(c + 1) * P],
                                           xT[:, c, b * S:(b + 1) * S], c == 0, c == C - 1)
                        last.then_inc(s_h, 1)
                    if b == 0 and o + 2 < HT:
                        prepare(o + 2)
                    if n >= 1:
                        down(*divmod(n - 1, HT))
            down(B - 1, HT - 1)

        @block.scalar
        def _(act):
            def tile_hi(o):
                act.wait_ge(s_tile[o % 2], 16 * (o // 2 + 1))
                if o >= 2:
                    act.wait_ge(s_merged, 3 * (o - 1))
                act.activation(tile[:, o % 2], tile_raw[:, o % 2], ACT.Copy).then_inc(s_tile_hi, 1)

            def whole_hi(o):
                for j in range(3):
                    act.wait_ge(s_whole, 3 * o + j + 1)
                    act.activation(weights[j].hi[:, o], stage[:, j], ACT.Copy).then_inc(s_w_hi, 1)

            act.wait_ge(s_side, 48)
            act.activation(side[:], side_raw, ACT.Copy, scale=2.0).then_inc(s_side_hi, 1)
            tile_hi(0)
            tile_hi(1)
            whole_hi(0)
            for b in range(B):
                for o in range(HT):
                    n = b * HT + o
                    if b == 0:
                        if o + 2 < HT:
                            tile_hi(o + 2)
                        if o + 1 < HT:
                            whole_hi(o + 1)
                    act.wait_ge(s_h1, n + 1)
                    if n >= 1:
                        act.wait_ge(s_gated, n)
                    act.activation(gate, h1[:], ACT.Silu).then_inc(s_gate, 1)
                    act.wait_ge(s_gated, n + 1)
                    if n >= 2:
                        done_b, done_o = divmod(n - 2, HT)
                        if done_o == HT - 1:
                            act.wait_ge(s_rows, done_b + 1)
                        else:
                            act.wait_ge(s_used, n - 1 - done_b)
                    act.activation(gT.hi[:, n % 2], gated, ACT.Copy).then_inc(s_g_hi, 1)
                    if n == HT:
                        act.wait_ge(s_rows, 1)
                        for t in range(TB):
                            last = act.activation(acc[:, t], rows[t][:], ACT.Copy).then_inc(s_taken, 1)
            act.wait_ge(s_rows, B)
            for t in range(TB):
                act.activation(acc[:, TB + t], rows[t][:], ACT.Copy).then_inc(s_taken, 1)

        @block.vector
        def _(dve):
            def tile_lo(o):
                dve.wait_ge(s_tile_hi, o + 1)
                dve.tensor_tensor(tile[64:96, o % 2], tile_raw[64:96, o % 2], tile[64:96, o % 2].bitcast(F32),
                                  ALU.subtract).then_inc(s_tile_lo, 1)

            def whole(o):
                for j in range(3):
                    k = 3 * o + j
                    dve.wait_ge(s_stage[j], 16 * (o + 1))
                    dve.wait_ge(s_merged, k + 1)
                    dve.tensor_tensor(stage[:, j], merge[k % 2][:], stage[:, j], ALU.add).then_inc(s_whole, 1)

            dve.wait_ge(s_side_hi, 1)
            dve.scalar_tensor_tensor(side[32:64], side_raw[32:64], 2.0, side[32:64].bitcast(F32), ALU.mult,
                                     ALU.subtract).then_inc(s_side_lo, 1)
            tile_lo(0)
            tile_lo(1)
            whole(0)
            for b in range(B):
                for o in range(HT):
                    n = b * HT + o
                    if b == 0:
                        if o + 2 < HT:
                            tile_lo(o + 2)
                        if o + 1 < HT:
                            whole(o + 1)
                    dve.wait_ge(s_gate, n + 1)
                    dve.wait_ge(s_h3, n + 1)
                    if n >= 1:
                        dve.wait_ge(s_g_lo, n)
                    dve.tensor_tensor(gated, h3[:], gate, ALU.mult).then_inc(s_gated, 1)
                    dve.wait_ge(s_g_hi, n + 1)
                    rest(dve, gT.lo[:, n % 2], gated, gT.hi[:, n % 2]).then_inc(s_g_lo, 1)

        @block.gpsimd
        def _(pool):
            for o in range(HT):
                for j in range(3):
                    pool.wait_ge(s_w_hi, 3 * o + j + 1)
                    rest(pool, weights[j].lo[:, o], stage[:, j], weights[j].hi[:, o]).then_inc(s_w_lo, 1)


def build(nc, a, out):
    p = Program(nc, a)
    with ExitStack() as ctx:
        ident = p.sb(ctx, "ident", [P, P])
        half = p.sb(ctx, "half", [P, TB * GH])
        acc = p.sb(ctx, "acc", [P, TT, D])
        xT = p.split(ctx, "xT", [P, C, T])
        made = p.sem(ctx, "made")
        x_rows = a["x"].rearrange("(t p) d -> p t d", p=P)
        out_rows = out.rearrange("(t p) d -> p t d", p=P)
        kept = nc.dram_tensor("x_kept", [T, D], F32, kind="Internal").ap().rearrange("(t p) d -> p t d", p=P)

        with nc.Block() as block:
            @block.gpsimd
            def _(pool):
                pool.memset(ident[:], 0.0).then_inc(made, 1)
                pool.wait_ge(made, 1)
                pool.affine_select(out=ident[:], in_=ident[:], compare_op=ALU.not_equal, fill=1.0, base=0,
                                   pattern=[[-1, P]], channel_multiplier=1).then_inc(made, 1)
                pool.memset(half[:], -0.5).then_inc(made, 1)
                pool.wait_ge(made, 3)

        def normed(name, **how):
            with ExitStack() as inner:
                x = p.sb(inner, f"{name}_x", [P, TT, D])
                norm_phase(p, ctx, name, x, ident=ident, half=half, **how)

        normed("norm0", xT=xT, load=x_rows)
        attention_phase(p, ctx, 0, xT, acc, ident, half)
        normed("norm1", xT=xT, update=acc, load=x_rows, store=kept)
        linear_phase(p, ctx, xT, acc)
        normed("norm2", xT=xT, update=acc, load=kept, store=kept)
        attention_phase(p, ctx, 1, xT, acc, ident, half)
        normed("norm3", xT=xT, update=acc, load=kept, store=kept, bias=a["l1_bo"])
        swiglu_phase(p, ctx, xT, acc)
        normed("norm4", xT=None, update=acc, load=kept, store=out_rows)


def layout(v):
    import numpy as np

    f = {k: np.asarray(x) for k, x in v.items()}
    tall = lambda w, n: w.T.reshape(C, P, n, HD).transpose(2, 1, 0, 3).reshape(n, P, C * HD)
    wide = lambda w: w.reshape(C, P, NG, GH * HD).transpose(2, 0, 1, 3).reshape(NG * C, P, GH * HD)
    inv_freq = (1.0 / np.float32(10000.0) ** (np.arange(0, HD, 2, dtype=np.float32) / np.float32(HD)))
    angle = np.arange(S, dtype=np.float32)[None, :] * inv_freq.astype(np.float32)[:, None]
    c, s = np.cos(angle), np.sin(angle)
    ahead = np.arange(P)[None, :] > np.arange(P)[:, None]
    out = {
        "x": f["L0_attn_hidden_states"].reshape(T, D),
        "l0_wq": tall(f["L0_attn_Wq"], NH), "l0_wk": tall(f["L0_attn_Wk"], NG), "l0_wv": tall(f["L0_attn_Wv"], NG),
        "l0_wo": f["L0_attn_Wo"].T.reshape(NH, HD, D),
        "trig": np.stack([x * k for k in (1.0, SCALE) for x in (np.concatenate([c, c]), np.concatenate([-s, s]))], 1),
        "mask": np.where(ahead, MASKED, 0.0),
        "l0_w": f["L0_ffn_W"].T, "l0_a": f["L0_ffn_lora_A"].reshape(8 * RK, D),
        "l0_b": f["L0_ffn_lora_B"].transpose(0, 2, 1).reshape(8 * RK, D), "l0_bias": f["L0_ffn_bias"].reshape(1, D),
        "l0_mix": f["L0_ffn_lora_weights"].reshape(8, 1),
        "l1_wq": wide(f["L1_attn_Wq"]), "l1_wk": wide(f["L1_attn_Wk"]), "l1_wv": wide(f["L1_attn_Wv"]),
        "l1_wo": f["L1_attn_Wo"].reshape(NH, HD, D),
        "l1_bq": f["L1_attn_bq"].reshape(NG, GH * HD), "l1_bk": f["L1_attn_bk"].reshape(NG, GH * HD),
        "l1_bv": f["L1_attn_bv"].reshape(NH, HD).T, "l1_bo": f["L1_attn_bo"].reshape(1, D),
        "l1_gq": f["L1_attn_gq"].reshape(HD, 1), "l1_gk": f["L1_attn_gk"].reshape(HD, 1),
    }

    def padded(w):
        return np.concatenate([w, np.zeros((w.shape[0], HP - HID), w.dtype)], axis=1)

    def thrice(w):
        three = np.zeros((3, 32, w.shape[1]), w.dtype)
        three[:, :RK] = w
        return three.reshape(96, w.shape[1])

    for n in "13":
        out[f"f_w{n}"] = padded(f[f"L1_ffn_w{n}"].T).reshape(C, P, HT, P).transpose(2, 1, 0, 3).reshape(HT, P, C * P)
        out[f"f_a{n}"] = thrice(f[f"L1_ffn_lora_A{n}"])
    out["f_w2"] = padded(f["L1_ffn_w2"]).T.reshape(HT, P, D)
    out["f_b2"] = thrice(f["L1_ffn_lora_B2"].T)
    ranks = f["L1_ffn_lora_B1"].T, f["L1_ffn_lora_B3"].T, f["L1_ffn_lora_A2"]
    out["f_tile"] = np.stack([thrice(padded(w)).reshape(96, HT, P) for w in ranks]).transpose(2, 1, 0, 3).reshape(
        HT, 96, 3 * P)
    return {k: np.ascontiguousarray(x, dtype=np.float32) for k, x in out.items()}


def kernel(**inputs):
    import concourse.bacc as bacc
    from concourse.bass_utils import run_bass_kernel_spmd

    nc = bacc.Bacc("TRN2", target_bir_lowering=False, num_devices=1)
    arrays = layout(inputs)
    a = {k: nc.dram_tensor(k, x.shape, F32, kind="ExternalInput").ap() for k, x in arrays.items()}
    out = nc.dram_tensor("out", (T, D), F32, kind="ExternalOutput").ap()
    build(nc, a, out)
    r = run_bass_kernel_spmd(nc, [arrays], core_ids=[0])
    return r.results[0]["out"].reshape(B, S, D)
```

```python
from contextlib import ExitStack

import concourse.bass as bass
from concourse import mybir

ALU = mybir.AluOpType
ACT = mybir.ActivationFunctionType
AXX = mybir.AxisListType.X
F32 = mybir.dt.float32
F32R = mybir.dt.float32r

P = 128
B, S, D = 2, 512, 512
T = B * S
TT = T // P
TB = S // P
C = D // P
HD = 128
NH = 32
GH = 4
NG = NH // GH
SLOTS = GH * B
TILES = SLOTS * TB
HID = 1376
HT = -(-HID // P)
HP = HT * P
RK = 16
SCALE = float(HD) ** -0.5
LN_EPS = 1e-5
RMS_EPS = 1e-6
MASKED = -2.0 ** 100

TURN, EVAC, PV, OUT = 2, 3, 7, 8
TAIL = OUT + TILES


def steps_of(*items):
    by = {}
    for step, item in sorted(items, key=lambda x: x[0]):
        by.setdefault(step, []).append(item)
    return by


def in_order(by):
    return [x for step in sorted(by) for x in by[step]]


FIRST_BANK0 = [("k", 0), ("v", 0), ("vt", 0), ("q", 0)]
BANK0 = [(4 * s - 4, ("q", s)) for s in range(1, SLOTS)] + [(6, ("k", 1)), (9, ("v", 1)), (14, ("vt", 1))]
BANK0_NEXT = [(18, ("k", 0)), (21, ("v", 0)), (26, ("vt", 0)), (28, ("q", 0))]
FIRST_WORK0 = [("wk", 0), ("wv", 0), ("wq", 0), ("wq", 1)]
WORK0 = [(4 * s + 3, ("wo", s)) for s in range(SLOTS)] + [(4 * s - 6, ("wq", s)) for s in range(2, SLOTS)]
WORK0_NEXT = [(12, ("wk", 0)), (16, ("wv", 0)), (24, ("wq", 0)), (28, ("wq", 1))]

FIRST_BANK1 = ([(m, 0, t) for m in "qk" for t in range(TB)] + [("q", 1, t) for t in range(TB)]
               + [("tq", 0), ("tk", 0)])
BANK1 = ([(4 * s - 3, ("tq", s)) for s in range(1, SLOTS)]
         + [(4 * s - 2, ("tk", s)) for s in range(1, SLOTS)]
         + [(n, ("k", 1, t)) for t, n in enumerate((0, 1, 2, 9))]
         + [(TB * GH * b + PV - TB + t, ("v", b, t)) for b in range(B) for t in range(TB)])
BANK1_NEXT = ([(n, ("q", 0, t)) for t, n in enumerate((10, 12, 13, 14))]
              + [(n, ("k", 0, t)) for t, n in enumerate((16, 17, 18, 25))]
              + [(n, ("q", 1, t)) for t, n in enumerate((26, 28, 29, 30))]
              + [(29, ("tq", 0)), (30, ("tk", 0))])
FIRST_WORK1 = [(m, c) for m in ("wq", "wk", "wv") for c in range(C)]
WORK1 = [(4 * s + 3, ("wo", s)) for s in range(SLOTS)]
WORK1_NEXT = [(n, (kind, c)) for kind, at in (("wq", (1, 2, 4, 6)), ("wk", (10, 12, 13, 14)),
                                              ("wv", (24, 26, 28, 30))) for c, n in enumerate(at)]
TO_NORM, TO_SCALE = 1, (1, 2, 2, 3)
QK = ("q", "k")


def any_use(x):
    return True


def of_qk(x):
    return x[0] in QK


def last_of_qk(x):
    return x[0] in QK and x[2] == TB - 1


class Before:

    def __init__(self, first_bank, first_work):
        self.order, self.work_order = first_bank, first_work

    def done(self, x, kind=any_use):
        return sum(map(kind, self.order[:self.order.index(x) + 1]))

    def parity(self, x, kind=any_use):
        return (self.done(x, kind) - kind(x)) % 2

    def work_done(self, x):
        return self.work_order.index(x) + 1


class Body:

    def __init__(self, i, first, last, bank, bank_next, work, work_next, before):
        self.i, self.first, self.last = i, first, last
        self.bank_at = steps_of(*bank, *([] if last else bank_next))
        self.work_at = steps_of(*work, *([] if last else work_next))
        self.order = in_order(self.bank_at)
        self.work_order = in_order(self.work_at)
        self.whole = in_order(steps_of(*bank, *bank_next))
        self.n_work = len(work) + len(work_next)
        self.before = before
        self.next_work = {x for _, x in work_next}
        self.prev = before if first else Body(i - 1, True, False, bank, bank_next, work, work_next, before)

    def start(self, kind=any_use):
        return self.i * sum(map(kind, self.whole)) + sum(map(kind, self.before.order))

    def done(self, x, kind=any_use):
        return self.start(kind) + sum(map(kind, self.order[:self.order.index(x) + 1]))

    def parity(self, x, kind=any_use):
        return sum(map(kind, self.order[:self.order.index(x)])) % 2

    def work_start(self):
        return self.i * self.n_work + len(self.before.work_order)

    def work_done(self, x):
        return self.work_start() + self.work_order.index(x) + 1

    def uses(self, n):
        if n >= 0 or self.first:
            return [(x, self) for x in self.bank_at.get(n, [])]
        return [(x, self.prev) for x in self.prev.bank_at.get(n + TILES, [])]

    def lagged(self, n, of=TILES):
        return n < of and (n >= 0 or not self.first)

    def steps(self):
        return range(TAIL if self.last else TILES)

    def slot_at(self, n, lag):
        slot, t = divmod(n - lag, TB)
        return slot if t == 0 and self.lagged(slot, SLOTS) else None


def wait_past(engine, sem, m, per, count):
    if m.first and not (isinstance(count, int) and count > 0):
        return
    engine.wait_ge(sem, m.i * per + count)


class Split:

    def __init__(self, hi, lo):
        self.hi, self.lo = hi, lo

    def __getitem__(self, at):
        return Split(self.hi[at], self.lo[at])

    @property
    def passes(self):
        return self.hi, self.lo


def product(nc, out, left, right, first=True, last=True):
    nc.tensor.matmul(out, left.hi, right.lo, start=first, stop=False, skip_group_check=True)
    nc.tensor.matmul(out, left.lo, right.hi, start=False, stop=False, skip_group_check=True)
    return nc.tensor.matmul(out, left.hi, right.hi, start=False, stop=last, skip_group_check=True)


def rest(engine, out, full, hi):
    return engine.tensor_tensor(out, full, hi.bitcast(F32), ALU.subtract)


class Program:

    def __init__(self, nc, a):
        self.nc, self.a = nc, a

    def sb(self, ctx, name, shape, dt=F32):
        return ctx.enter_context(self.nc.sbuf_tensor(name, shape, dt))

    def split(self, ctx, name, shape):
        return Split(self.sb(ctx, name + "_hi", shape, F32R), self.sb(ctx, name + "_lo", shape, F32R))

    def split_and_words(self, ctx, name, shape):
        with ExitStack() as early:
            words = Split(self.sb(early, name + "_hi_words", shape), self.sb(early, name + "_lo_words", shape))
        return self.split(ctx, name, shape), words

    def banks(self, ctx, name, n):
        return [ctx.enter_context(self.nc.psum_tensor(f"{name}{i}", [P, 512], F32)) for i in range(n)]

    def sem(self, ctx, name):
        return ctx.enter_context(self.nc.semaphore(name))


class RowNorms:

    def __init__(self, p, ctx, ctx0, name, rounds, half):
        self.half = half
        self.stats = p.sb(ctx, f"{name}_stats", [P, rounds, TT, 6])
        self.mean_var = p.sb(ctx, f"{name}_mean_var", [P, rounds, TT, 2])
        self.var = p.sb(ctx, f"{name}_var", [P, rounds, TT])
        self.rstd = p.sb(ctx, f"{name}_rstd", [P, rounds, TT])
        self.bias = p.sb(ctx, f"{name}_bias", [P, rounds, TT])
        sems = lambda what: [p.sem(ctx0, f"{name}_{what}{r}") for r in range(rounds)]
        self.measured, self.rooted, self.biased, self.normed = map(sems, "measured rooted biased normed".split())

    def sums(self, dve, r, t, rows):
        dve.bn_stats(self.stats[:, r, t], rows).then_inc(self.measured[r], 1)

    def spread(self, dve, *tiles):
        for r, t in tiles:
            dve.wait_ge(self.measured[r], 3 * t + 1)
            dve.bn_aggr(self.mean_var[:, r, t], self.stats[:, r, t]).then_inc(self.measured[r], 1)
        for r, t in tiles:
            dve.wait_ge(self.measured[r], 3 * t + 2)
            dve.tensor_scalar(self.var[:, r, t:t + 1], self.mean_var[:, r, t, 1:2], LN_EPS, None, ALU.add)\
                .then_inc(self.measured[r], 1)

    def root(self, pool, r, t):
        pool.wait_ge(self.measured[r], 3 * t + 3)
        pool.tensor_tensor(self.rstd[:, r, t:t + 1], self.var[:, r, t:t + 1], self.half[:, 0:1], ALU.pow)\
            .then_inc(self.rooted[r], 1)

    def center(self, dve, r, t):
        dve.wait_ge(self.rooted[r], t + 1)
        dve.scalar_tensor_tensor(self.bias[:, r, t:t + 1], self.mean_var[:, r, t, 0:1], -1.0,
                                 self.rstd[:, r, t:t + 1], ALU.mult, ALU.mult).then_inc(self.biased[r], 1)

    def scaled(self, act, r, t, out, rows):
        act.wait_ge(self.biased[r], t + 1)
        act.activation(out, rows, ACT.Identity, bias=self.bias[:, r, t:t + 1], scale=self.rstd[:, r, t:t + 1])\
            .then_inc(self.normed[r], 1)


def attention_phase(p, ctx0, layer, xT, acc, ident, half, x_rows=None):
    nc, a = p.nc, p.a
    causal = layer == 0
    L = f"l{layer}"
    tables = ((BANK0, BANK0_NEXT, WORK0, WORK0_NEXT, Before(FIRST_BANK0, FIRST_WORK0)) if causal
              else (BANK1, BANK1_NEXT, WORK1, WORK1_NEXT, Before(FIRST_BANK1, FIRST_WORK1)))
    before = tables[-1]
    HI = ("vt",) if causal else ("v", "tq", "tk")

    def of_hi(x):
        return x[0] in HI

    width = [(t + 1) * P if causal else S for t in range(TB)]
    with ExitStack() as ctx:
        sb = lambda n, s, dt=F32: p.sb(ctx, f"{L}_{n}", s, dt)
        split = lambda n, s: p.split(ctx, f"{L}_{n}", s)
        sem = lambda n: p.sem(ctx0, f"{L}_{n}")

        score = p.banks(ctx, f"{L}_score", 2)
        turned = p.banks(ctx, f"{L}_turned", 2)
        pv_bank, = p.banks(ctx, f"{L}_pv", 1)
        out_bank, = p.banks(ctx, f"{L}_out", 1)
        general = p.banks(ctx, f"{L}_general", 2)

        NPR = 4
        probs = sb("probs", [P, NPR, S])
        probsT = split("probsT", [P, TB, S])
        qT = split("qT", [P, 2, S])
        kT = split("kT", [P, 2, S])
        oT = split("oT", [P, S])
        w_out = split("w_out", [P, 2, D])
        stage = sb("stage", [P, 2, 512])
        negtop = sb("negtop", [P, TILES])
        total = sb("total", [P, TILES])
        inv = sb("inv", [P, TILES])

        s_score, s_negtop, s_exp, s_inv, s_norm, s_turn, s_turn_hi, s_turn_lo = map(
            sem, "score negtop exp inv norm turn turn_hi turn_lo".split())
        s_pv, s_o_hi, s_o_lo, s_out, s_added = map(sem, "pv o_hi o_lo out added".split())
        s_bank, s_bank_hi, s_free = map(sem, "bank bank_hi bank_free".split())
        s_stage = [sem("stage_even"), sem("stage_odd")]
        s_w_hi, s_w = sem("w_hi"), sem("w")
        s_const, s_zero = sem("const"), sem("zero")

        if causal:
            trig = sb("trig", [P, 4, S])
            mask_raw = sb("mask_raw", [P, P])
            mask = sb("mask", [P, P], F32R)
            ident_r = sb("ident_r", [P, P], F32R)
            s_mask = sem("mask")
            rope = sb("rope", [P, 2, 2, S])
            v_turn = sb("v_turn", [P, S])
            v = split("v", [P, B, TB * HD])
            w_q = split("w_q", [P, 2, C * HD])
            w_k = split("w_k", [P, C * HD])
            w_v = split("w_v", [P, C * HD])
            z = rope[:, 1]
            norms = RowNorms(p, ctx, ctx0, "first_norm", 1, half)
            s_x, s_x_turn, s_x_hi, s_x_lo = [sem("x_in0"), sem("x_in1")], sem("x_turn"), sem("x_hi"), sem("x_lo")
            s_rope_swap, s_rope_sin, s_rope_add, s_rope_hi, s_rope_lo = map(
                sem, "rope_swap rope_sin rope_add rope_hi rope_lo".split())
        else:
            y = sb("y", [P, B, 2, TB, GH * HD])
            v = split("v", [P, TB, GH * HD])
            w_q = split("w_q", [P, C, GH * HD])
            w_k = split("w_k", [P, C, GH * HD])
            w_v = split("w_v", [P, C, GH * HD])
            b_qk = sb("b_qk", [P, 2, GH * HD])
            b_v = sb("b_v", [P, GH])
            b_v_all = sb("b_v_all", [P, NH])
            gains = sb("gains", [P, 3])
            squares = sb("squares", [P, GH, HD])
            sumsq = sb("sumsq", [P, B, 2, TB * GH])
            meansq = sb("meansq", [P, B, 2, TB * GH])
            s_sq, s_var, s_rrms, s_yn, s_gain = map(sem, "sq var rrms yn gain".split())
            s_bq, s_bk, s_bv, s_bo = map(sem, "bq bk bv bo".split())

        def w_dest(x):
            kind, j = x
            if kind == "wo":
                return w_out[:, j % 2]
            w = {"wq": w_q, "wk": w_k, "wv": w_v}[kind]
            if causal:
                return w[:, j % 2] if kind == "wq" else w[:, :]
            return w[:, j]

        def w_source(x, group):
            kind, j = x
            if kind == "wo" or (causal and kind == "wq"):
                return a[f"{L}_{kind}"][group * GH + j % GH]
            return a[f"{L}_{kind}"][group] if causal else a[f"{L}_{kind}"][group * C + j]

        ALTERNATE = TILES - OUT

        def out_of(m, j):
            return general[0] if m.last and j > ALTERNATE and j % 2 else out_bank

        def loop(engine, body):
            body(Body(0, True, False, *tables))
            with engine.Fori(1, NG - 1) as i:
                body(Body(i, False, False, *tables))
            body(Body(NG - 1, False, True, *tables))

        block = ctx.enter_context(nc.Block())

        AHEAD, WEIGHTS_AT = 2, 6

        def columns(t):
            return slice(t * P, (t + 1) * P)

        def x_turned(t):
            return turned[t % 2][:].rearrange("p (c t) -> p c t", c=C)

        @block.sync
        def _(sp):
            if causal:
                for b in range(B):
                    rows = slice(b * TB, (b + 1) * TB)
                    sp.dma_start(acc[:, rows], x_rows[:, rows]).then_inc(s_x[b], 16)
            def load(k, group, x, free):
                if free is not None:
                    sp.wait_ge(s_w, free)
                sp.dma_start(stage[:, k % 2], w_source(x, group)).then_inc(s_stage[k % 2], 16)

            for k, x in enumerate(before.work_order):
                load(k, 0, x, k - 1 if k >= 2 else None)
                if k == 1 and causal:
                    sp.dma_start(trig[:], a["trig"]).then_inc(s_const, 16)
                    sp.dma_start(mask_raw[:], a["mask"]).then_inc(s_const, 16)
                if k == 1 and not causal:
                    sp.dma_start(b_qk[:, 0], a["l1_bq"][0:1].to_broadcast([P, GH * HD])).then_inc(s_bq, 16)
                    sp.dma_start(b_qk[:, 1], a["l1_bk"][0:1].to_broadcast([P, GH * HD])).then_inc(s_bk, 16)
                    sp.dma_start(gains[:, 0:1], a["l1_gq"]).then_inc(s_const, 16)
                    sp.dma_start(gains[:, 1:2], a["l1_gk"]).then_inc(s_const, 16)
                    sp.dma_start(b_v_all[:], a["l1_bv"]).then_inc(s_const, 16)
                    sp.dma_start(acc[:, 0], a["l1_bo"].to_broadcast([P, D])).then_inc(s_bo, 16)

            def body(m):
                for n in range(TILES):
                    for x in m.work_at.get(n, []):
                        k = m.work_order.index(x)
                        load(k, m.i + 1 if x in m.next_work else m.i, x, m.work_start() + k - 1)
                    if not causal and not m.last and n in (1, 10):
                        if n == 1:
                            sp.wait_ge(s_free, m.start())
                        else:
                            sp.wait_ge(s_free, m.done(("k", 1, TB - 1)))
                        r = int(n == 10)
                        sp.dma_start(b_qk[:, r], a[("l1_bq", "l1_bk")[r]][bass.ds(m.i + 1, 1)].to_broadcast(
                            [P, GH * HD])).then_inc((s_bq, s_bk)[r], 16)

            loop(sp, body)

        @block.tensor
        def _(pe):
            def bank_use(x, m, part=range(C)):
                kind = x[0]
                if 0 in part and (m is not before or m.done(x) > 2):
                    pe.wait_ge(s_free, m.done(x) - 2)
                bank = general[m.parity(x)]
                if kind in ("tq", "tk"):
                    slot, r = x[1], int(kind == "tk")
                    par, h = slot // GH, slot % GH
                    if h == 0:
                        pe.wait_ge(s_yn, (m.prev if (kind, slot) == ("tq", GH) else m).done(
                            ("qk"[r], par, TB - 1), of_qk))
                    for t in range(TB):
                        last = pe.transpose(bank[:, t * P:(t + 1) * P], y[:, par, r, t, h * HD:(h + 1) * HD],
                                            ident[:])
                elif causal and kind == "vt":
                    pe.wait_ge(s_free, m.done(("v", x[1])))
                    for t in range(TB):
                        last = pe.transpose(bank[:, t * P:(t + 1) * P], v_turn[:, t * P:(t + 1) * P], ident[:])
                elif causal:
                    w = {"q": ("wq", x[1]), "k": ("wk", 0), "v": ("wv", 0)}[kind]
                    if 0 in part:
                        own = m is before or x not in (("q", 1), ("k", 1), ("v", 1))
                        pe.wait_ge(s_w, (m if own else m.prev).work_done(w))
                    batch = x[1] // GH if kind == "q" else x[1]
                    left = w_dest(w)
                    for c in part:
                        last = product(nc, bank[:], left[:, c * HD:(c + 1) * HD],
                                       xT[:, c, batch * S:(batch + 1) * S], c == 0, c == C - 1)
                else:
                    batch, t = x[1], x[2]
                    w = {"q": w_q, "k": w_k, "v": w_v}[kind]
                    if batch == 0 and t == 0:
                        pe.wait_ge(s_w, (m.prev if kind == "v" else m).work_done((f"w{kind}", C - 1)))
                    at = batch * S + t * P
                    for c in range(C):
                        last = product(nc, bank[:], xT[:, c, at:at + P], w[:, c], c == 0, c == C - 1)
                if C - 1 in part:
                    last.then_inc(s_bank, 1)

            def halves(x, n):
                return causal and x[0] != "vt" and n > 0

            def turn_rows(tiles):
                for t in tiles:
                    pe.wait_ge(norms.normed[0], t + 1)
                    if t >= 2:
                        pe.wait_ge(s_x_lo, t - 1)
                    for c in range(C):
                        last = pe.transpose(turned[t % 2][:, c * P:(c + 1) * P], z[:, t % 2, c * P:(c + 1) * P],
                                            ident[:])
                    last.then_inc(s_x_turn, 1)

            if causal:
                turn_rows(range(TT))
                pe.wait_ge(s_x_lo, TT)
            for x in before.order:
                bank_use(x, before)
            if causal:
                pe.wait_ge(s_mask, 2)

            def project(m, j):
                slot, t = divmod(j, TB)
                if t == 0:
                    own = m if slot >= 0 else m.prev
                    pe.wait_ge(s_w, own.work_done(("wo", slot % SLOTS)))
                    wait_past(pe, s_o_lo, m, SLOTS, slot + 1)
                if m.last and j == ALTERNATE + 1:
                    pe.wait_ge(s_free, m.done(m.order[-1]))
                else:
                    wait_past(pe, s_added, m, TILES, j - (m.last and j > ALTERNATE + 1))
                last = product(nc, out_of(m, j)[:], oT[:, t * P:(t + 1) * P], w_out[:, slot % 2])
                last.then_inc(s_out, 1)

            def body(m):
                for n in m.steps():
                    if n < TILES:
                        slot, t = divmod(n, TB)
                        if t == 0:
                            own = m.prev if slot == 0 else m
                            if causal:
                                pe.wait_ge(s_rope_lo, own.done(("q", slot), of_qk))
                            else:
                                pe.wait_ge(s_free, own.done(("tk", slot)))
                        wait_past(pe, s_exp, m, TILES, n - 1)
                        kp = slot // GH if causal else slot % 2
                        last = product(nc, score[n % 2][:, 0:width[t]], qT[:, slot % 2, t * P:(t + 1) * P],
                                       kT[:, kp, 0:width[t]])
                        if causal:
                            last = pe.matmul(score[n % 2][:, t * P:(t + 1) * P], ident_r[:], mask[:], start=False,
                                             stop=True, skip_group_check=True)
                        last.then_inc(s_score, 1)
                    late = (n - OUT) % TB == 0
                    if m.lagged(n - OUT) and not late:
                        project(m, n - OUT)
                    slot = m.slot_at(n, PV)
                    if slot is not None:
                        wait_past(pe, s_turn_lo, m, TILES, TB * (slot + 1))
                        wait_past(pe, s_o_lo, m, SLOTS, slot)
                        b, h = divmod(slot % SLOTS, GH)
                        own = m if slot >= 0 else m.prev
                        if causal and h == 0:
                            pe.wait_ge(s_free, (m if b else m.prev).done(("vt", b)))
                        if not causal and h == 0:
                            pe.wait_ge(s_free, own.done(("v", b, TB - 1)))
                        for k in range(TB):
                            left = v[:, b, k * HD:(k + 1) * HD] if causal else v[:, k, h * HD:(h + 1) * HD]
                            q0 = k * P if causal else 0
                            last = product(nc, pv_bank[:, q0:S], left, probsT[:, k, q0:S], k == 0, k == TB - 1)
                        last.then_inc(s_pv, 1)
                    for x, _ in m.uses(n) if n < TILES else []:
                        bank_use(x, m, range(C // 2, C) if halves(x, n) else range(C))
                    if m.lagged(n - OUT) and late:
                        project(m, n - OUT)
                    if m.lagged(n - TURN):
                        j = n - TURN
                        wait_past(pe, s_norm, m, TILES, j + 1)
                        wait_past(pe, s_turn_lo, m, TILES, j - 1)
                        for k in range(width[j % TB] // P):
                            last = pe.transpose(turned[j % 2][:, k * P:(k + 1) * P],
                                                probs[:, j % NPR, k * P:(k + 1) * P], ident[:])
                        last.then_inc(s_turn, 1)
                    for x in m.bank_at.get(n + 1, []):
                        if halves(x, n + 1):
                            bank_use(x, m, range(C // 2))

            loop(pe, body)

        @block.scalar
        def _(act):
            def work(x, m, k):
                if m is before:
                    start = 0
                else:
                    start = m.work_start()
                    if x[0] == "wo":
                        wait_past(act, s_out, m, TILES, TB * (x[1] - 1))
                    elif causal:
                        user = {"wq": ("q", (x[1] - 2) % SLOTS), "wk": ("k", 1), "wv": ("v", 1)}[x[0]]
                        act.wait_ge(s_bank, (m.prev if x == ("wq", 2) else m).done(user))
                    elif x[0] == "wq":
                        act.wait_ge(s_bank, m.start())
                    else:
                        act.wait_ge(s_bank, m.done((x[0][1], 1, TB - 1)))
                act.wait_ge(s_stage[k % 2], 8 * (start + k - k % 2) + 16)
                act.activation(w_dest(x).hi, stage[:, k % 2], ACT.Copy).then_inc(s_w_hi, 1)

            def bank_hi(x, m):
                bank = general[m.parity(x)]
                if x[0] in HI:
                    act.wait_ge(s_bank, m.done(x))
                if x[0] == "vt":
                    act.activation(v.hi[:, x[1]], bank[:], ACT.Copy).then_inc(s_bank_hi, 1)
                elif x[0] == "v" and not causal:
                    wait_past(act, s_pv, m, SLOTS, x[1] * GH)
                    act.activation(v.hi[:, x[2]], bank[:], ACT.Copy).then_inc(s_bank_hi, 1)
                elif x[0] == "tq":
                    act.activation(qT.hi[:, x[1] % 2], bank[:], ACT.Copy).then_inc(s_bank_hi, 1)
                elif x[0] == "tk":
                    act.activation(kT.hi[:, x[1] % 2], bank[:], ACT.Copy, scale=gains[:, 2:3]).then_inc(s_bank_hi, 1)

            def rope_swap(x, m):
                r, count = m.parity(x, of_qk), m.done(x, of_qk)
                act.wait_ge(s_bank, m.done(x))
                if m is not before:
                    act.wait_ge(s_rope_add, count - 2)
                bank, h = general[m.parity(x)], HD // 2
                act.activation(rope[0:h, r, 1], bank[h:HD, :], ACT.Copy)
                act.activation(rope[h:HD, r, 1], bank[0:h, :], ACT.Copy).then_inc(s_rope_swap, 1)

            def rope_hi(x, m):
                act.wait_ge(s_rope_add, m.done(x, of_qk))
                to = qT.hi[:, x[1] % 2] if x[0] == "q" else kT.hi[:, x[1]]
                act.activation(to, rope[:, m.parity(x, of_qk), 0], ACT.Copy).then_inc(s_rope_hi, 1)

            def square(x, m):
                act.wait_ge(s_free, m.done(x))
                r = int(x[0] == "k")
                n = m.done(x, of_qk)
                if m is not before or n > 1:
                    act.wait_ge(s_sq, n - 1)
                for h in range(GH):
                    j = x[2] * GH + h
                    last = act.activation(squares[:, h], y[:, x[1], r, x[2], h * HD:(h + 1) * HD], ACT.Square,
                                          accum_out=sumsq[:, x[1], r, j:j + 1])
                last.then_inc(s_sq, 1)

            if not causal:
                act.wait_ge(s_gain, 1)
            def norm_rows():
                for t in range(TT + 1):
                    if t == WEIGHTS_AT:
                        for k in range(AHEAD):
                            work(before.work_order[k], before, k)
                    if t < TT:
                        if t >= 2:
                            act.wait_ge(s_x_turn, t - 1)
                        norms.scaled(act, 0, t, z[:, t % 2], acc[:, t])
                    if t >= 1:
                        act.wait_ge(s_x_turn, t)
                        act.activation(xT.hi[:, :, columns(t - 1)], x_turned(t - 1), ACT.Copy).then_inc(s_x_hi, 1)

            if causal:
                norm_rows()
            for k in range(AHEAD if causal else 0, len(before.work_order)):
                work(before.work_order[k], before, k)
            for x in before.order:
                if x[0] in HI:
                    bank_hi(x, before)
                elif x[0] in QK and causal:
                    rope_swap(x, before)
                    rope_hi(x, before)
                elif x[0] in QK:
                    square(x, before)

            def exponentials(m, n):
                t = n % TB
                act.wait_ge(s_negtop, m.i * TILES + n + 1)
                wait_past(act, s_turn, m, TILES, n - NPR + 1)
                act.activation(probs[:, n % NPR, 0:width[t]], score[n % 2][:, 0:width[t]], ACT.Exp,
                               bias=negtop[:, n:n + 1], accum_out=total[:, n:n + 1]).then_inc(s_exp, 1)

            def turned_hi(m, j):
                slot, t = divmod(j, TB)
                kt = width[t] // P
                wait_past(act, s_turn, m, TILES, j + 1)
                if t == 0:
                    wait_past(act, s_pv, m, SLOTS, slot)
                act.activation(probsT.hi[:, 0:kt, t * P:(t + 1) * P],
                               turned[j % 2][:, 0:kt * P].rearrange("p (k q) -> p k q", k=kt),
                               ACT.Copy).then_inc(s_turn_hi, 1)

            def output_hi(m, slot):
                wait_past(act, s_pv, m, SLOTS, slot + 1)
                wait_past(act, s_out, m, TILES, TB * slot)
                if causal:
                    act.activation(oT.hi[:], pv_bank[:], ACT.Copy).then_inc(s_o_hi, 1)
                else:
                    h = slot % GH
                    if 0 <= slot < GH:
                        act.wait_ge(s_bv, m.i * GH + h + 1)
                    act.activation(oT.hi[:], pv_bank[:], ACT.Identity, bias=b_v[:, h:h + 1]).then_inc(s_o_hi, 1)

            def body(m):
                for n in m.steps():
                    slot = m.slot_at(n, PV)
                    if slot is None and m.lagged(n - EVAC):
                        turned_hi(m, n - EVAC)
                    if n < TILES:
                        exponentials(m, n)
                    if slot is not None:
                        output_hi(m, slot)
                        if m.lagged(n - EVAC):
                            turned_hi(m, n - EVAC)
                    for x, own in m.uses(n - 1):
                        if x[0] in QK:
                            rope_hi(x, own) if causal else square(x, own)
                    for x in m.work_at.get(n, []):
                        work(x, m, m.work_order.index(x))
                    for x, own in m.uses(n):
                        if x[0] in HI:
                            bank_hi(x, own)
                        elif causal and x[0] in QK:
                            rope_swap(x, own)

            loop(act, body)

        @block.vector
        def _(dve):
            def bank_use(x, m):
                bank, kind = general[m.parity(x)], x[0]
                if kind in HI:
                    dve.wait_ge(s_bank_hi, m.done(x, of_hi))
                else:
                    dve.wait_ge(s_bank, m.done(x))
                if causal and kind in QK:
                    r = m.parity(x, of_qk)
                    count = m.done(x, of_qk)
                    if m is not before:
                        dve.wait_ge(s_rope_lo, count - 2)
                    dve.wait_ge(s_rope_swap, count)
                    last = dve.tensor_tensor(rope[:, r, 0], bank[:], trig[:, 2 * (kind == "q")], ALU.mult)
                elif causal and kind == "v":
                    last = dve.tensor_copy(v_turn[:], bank[:])
                elif kind == "vt":
                    last = rest(dve, v.lo[:, x[1]], bank[:], v.hi[:, x[1]])
                elif kind == "v":
                    last = rest(dve, v.lo[:, x[2]], bank[:], v.hi[:, x[2]])
                elif kind == "tq":
                    last = rest(dve, qT.lo[:, x[1] % 2], bank[:], qT.hi[:, x[1] % 2])
                elif kind == "tk":
                    last = dve.scalar_tensor_tensor(kT.lo[:, x[1] % 2], bank[:], gains[:, 2:3],
                                                    kT.hi[:, x[1] % 2].bitcast(F32), ALU.mult, ALU.subtract)
                else:
                    r = int(kind == "k")
                    if x[1:] == (0, 0):
                        dve.wait_ge((s_bq, s_bk)[r], 16 if m is before else (m.i + 2) * 16)
                    last = dve.tensor_tensor(y[:, x[1], r, x[2]], bank[:], b_qk[:, r], ALU.add)
                last.then_inc(s_free, 1)

            def norm(x, m):
                at = slice(None), x[1], int(x[0] == "k")
                dve.wait_ge(s_sq, m.done(x, of_qk))
                dve.tensor_scalar(meansq[at], sumsq[at], 1.0 / HD, RMS_EPS, ALU.mult, ALU.add).then_inc(s_var, 1)

            def norm_rows():
                for t in range(TT + 2):
                    if t < TT:
                        dve.wait_ge(s_x[t // TB], 16)
                        norms.sums(dve, 0, t, acc[:, t])
                        norms.spread(dve, (0, t))
                        norms.center(dve, 0, t)
                    if t >= 2:
                        dve.wait_ge(s_x_hi, t - 1)
                        rest(dve, xT.lo[:, :, columns(t - 2)], x_turned(t - 2), xT.hi[:, :, columns(t - 2)])\
                            .then_inc(s_x_lo, 1)

            if causal:
                norm_rows()
                dve.wait_ge(s_const, 32)
                dve.tensor_copy(mask[:], mask_raw[:]).then_inc(s_mask, 1)
                dve.tensor_copy(ident_r[:], ident[:]).then_inc(s_mask, 1)
            else:
                dve.wait_ge(s_const, 48)
                dve.scalar_tensor_tensor(gains[:, 2:3], gains[:, 0:1], SCALE, gains[:, 1:2], ALU.mult, ALU.mult)\
                    .then_inc(s_gain, 1)
                dve.wait_ge(s_gain, 1)
            for x in before.order:
                bank_use(x, before)
                if not causal and last_of_qk(x):
                    norm(x, before)
            if causal:
                for t in range(TT):
                    last = dve.memset(acc[:, t], 0.0)
                last.then_inc(s_zero, 1)
            else:
                dve.wait_ge(s_bo, 16)
                for t in range(1, TT):
                    last = dve.tensor_copy(acc[:, t], acc[:, 0])
                last.then_inc(s_zero, 1)
            dve.wait_ge(s_zero, 1)

            def turned_lo(m, j):
                t = j % TB
                kt = width[t] // P
                wait_past(dve, s_turn_hi, m, TILES, j + 1)
                rest(dve, probsT.lo[:, 0:kt, t * P:(t + 1) * P],
                     turned[j % 2][:, 0:kt * P].rearrange("p (k q) -> p k q", k=kt),
                     probsT.hi[:, 0:kt, t * P:(t + 1) * P]).then_inc(s_turn_lo, 1)

            def add_rows(m, j):
                slot, t = divmod(j % TILES, TB)
                row = slot // GH * TB + t
                wait_past(dve, s_out, m, TILES, j + 1)
                dve.tensor_tensor(acc[:, row], out_of(m, j)[:], acc[:, row], ALU.add).then_inc(s_added, 1)

            def output_lo(m, slot):
                wait_past(dve, s_o_hi, m, SLOTS, slot + 1)
                if causal:
                    rest(dve, oT.lo[:], pv_bank[:], oT.hi[:]).then_inc(s_o_lo, 1)
                else:
                    h = slot % GH
                    dve.scalar_tensor_tensor(oT.lo[:], pv_bank[:], b_v[:, h:h + 1], oT.hi[:].bitcast(F32),
                                             ALU.add, ALU.subtract).then_inc(s_o_lo, 1)

            def body(m):
                for n in m.steps():
                    if m.lagged(n - 1):
                        j = (n - 1) % TILES
                        wait_past(dve, s_exp, m, TILES, n)
                        dve.reciprocal(inv[:, j:j + 1], total[:, j:j + 1]).then_inc(s_inv, 1)
                    if n < TILES:
                        dve.wait_ge(s_score, m.i * TILES + n + 1)
                        dve.tensor_reduce(negtop[:, n:n + 1], score[n % 2][:, 0:width[n % TB]], AXX, ALU.max,
                                          negate=True).then_inc(s_negtop, 1)
                    if m.lagged(n - OUT):
                        add_rows(m, n - OUT)
                    slot = m.slot_at(n, PV)
                    if slot is not None:
                        output_lo(m, slot)
                    if m.lagged(n - EVAC):
                        turned_lo(m, n - EVAC)
                    for x, own in m.uses(n):
                        bank_use(x, own)
                    if not causal:
                        for x, own in m.uses(n - TO_NORM):
                            if last_of_qk(x):
                                norm(x, own)
                        h, t = divmod(n, TB)
                        if t == 1 and h < GH:
                            dve.tensor_copy(b_v[:, h:h + 1], b_v_all[:, bass.ds(m.i * GH + h, 1)]).then_inc(s_bv, 1)

            loop(dve, body)

        @block.gpsimd
        def _(pool):
            def work(x, m, k):
                w0 = m.work_start() if m is not before else 0
                pool.wait_ge(s_w_hi, w0 + k + 1)
                rest(pool, w_dest(x).lo, stage[:, k % 2], w_dest(x).hi).then_inc(s_w, 1)

            def rope_add(x, m):
                r, count = m.parity(x, of_qk), m.done(x, of_qk)
                pool.wait_ge(s_rope_swap, count)
                pool.tensor_tensor(rope[:, r, 1], rope[:, r, 1], trig[:, 2 * (x[0] == "q") + 1], ALU.mult)\
                    .then_inc(s_rope_sin, 1)
                pool.wait_ge(s_rope_sin, count)
                pool.wait_ge(s_free, m.done(x))
                pool.tensor_tensor(rope[:, r, 0], rope[:, r, 0], rope[:, r, 1], ALU.add).then_inc(s_rope_add, 1)

            def rope_lo(x, m):
                r = m.parity(x, of_qk)
                pool.wait_ge(s_rope_hi, m.done(x, of_qk))
                hi, lo = (qT.hi[:, x[1] % 2], qT.lo[:, x[1] % 2]) if x[0] == "q" else (kT.hi[:, x[1]], kT.lo[:, x[1]])
                rest(pool, lo, rope[:, r, 0], hi).then_inc(s_rope_lo, 1)

            def norm(x, m):
                at = slice(None), x[1], int(x[0] == "k")
                n = m.done(x, last_of_qk)
                pool.wait_ge(s_var, n)
                pool.tensor_tensor(meansq[at], meansq[at], half[:], ALU.pow).then_inc(s_rrms, 1)
                pool.wait_ge(s_rrms, n)

            def scale(x, t):
                par, r = x[1], int(x[0] == "k")
                rows = y[:, par, r, t].rearrange("p (h d) -> p h d", h=GH)
                by = meansq[:, par, r, t * GH:(t + 1) * GH].unsqueeze(2).broadcast_to([P, GH, HD])
                pool.tensor_tensor(rows, rows, by, ALU.mult).then_inc(s_yn, 1)

            if causal:
                for t in range(TT):
                    if t == WEIGHTS_AT:
                        for k in range(AHEAD):
                            work(before.work_order[k], before, k)
                    norms.root(pool, 0, t)
            for k in range(AHEAD if causal else 0, len(before.work_order)):
                work(before.work_order[k], before, k)
            for x in before.order:
                if causal and x[0] in QK:
                    rope_add(x, before)
                    rope_lo(x, before)
                if not causal and last_of_qk(x):
                    norm(x, before)
                    for t in range(TB):
                        scale(x, t)

            def body(m):
                for n in m.steps():
                    if m.lagged(n - 1):
                        j = (n - 1) % TILES
                        tile = probs[:, j % NPR, 0:width[j % TB]]
                        wait_past(pool, s_inv, m, TILES, n)
                        pool.nop(nofuse=True)
                        pool.tensor_scalar(tile, tile, inv[:, j:j + 1], 1.0, ALU.mult, ALU.mult).then_inc(s_norm, 1)
                    if causal:
                        for x, own in m.uses(n - 2):
                            if x[0] in QK:
                                rope_lo(x, own)
                    else:
                        for x, own in m.uses(n - TO_NORM):
                            if last_of_qk(x):
                                norm(x, own)
                        for t, d in enumerate(TO_SCALE):
                            for x, own in m.uses(n - d):
                                if last_of_qk(x):
                                    scale(x, t)
                    for x in m.work_at.get(n, []):
                        work(x, m, m.work_order.index(x))
                    for x, own in m.uses(n) if causal else []:
                        if x[0] in QK:
                            rope_add(x, own)

            loop(pool, body)


def linear_phase(p, ctx0, xT, acc, ident, half, x_rows, kept):
    nc, a = p.nc, p.a
    NR = 8 * RK
    ATTN, LIN_IN, LIN_OUT, NEXT_IN = range(4)
    AT = {"attn": 0, "add": 1, "lin_in": 2, "turn": 3, "rows": 4, "take": 5, "lin_out": 6, "add_out": 7,
          "next_in": 8, "turn_next": 9}
    WEIGHTS_AT = 2
    with ExitStack() as ctx:
        sb = lambda n, s, dt=F32: p.sb(ctx, f"lin_{n}", s, dt)
        split = lambda n, s: p.split(ctx, f"lin_{n}", s)
        sem = lambda n: p.sem(ctx0, f"lin_{n}")
        x = sb("x", [P, TT, D])
        z, z_next = sb("z", [P, 2, D]), sb("z_next", [P, 2, D])
        w_raw, a_raw, b_raw = sb("w_raw", [P, C, D]), sb("a_raw", [NR, D]), sb("b_raw", [NR, D])
        mix, bias, whole = sb("mix", [NR, 1]), sb("bias", [P, D]), sb("whole", [P, C, D])
        la, lb, w = split("la", [NR, D]), split("lb", [NR, D]), split("w", [P, C, D])
        merge, rows = p.banks(ctx, "lin_merge", 2), p.banks(ctx, "lin_rows", 2)
        turned, turned_next = p.banks(ctx, "lin_turned", 2), p.banks(ctx, "lin_turned_next", 2)
        norms = RowNorms(p, ctx, ctx0, "lin_norm", 4, half)
        s_x = [sem("x_in0"), sem("x_in1")]
        s_a, s_b, s_w, s_bias = sem("a_in"), sem("b_in"), sem("w_in"), sem("bias_in")
        s_scaled, s_hi, s_lo, s_merged, s_whole, s_w_hi, s_w_lo, s_rows, s_taken = map(
            sem, "scaled hi lo merged whole w_hi w_lo rows taken".split())
        s_add, s_add_out, s_turn, s_x_hi, s_x_lo, s_turn_next, s_next_hi, s_next_lo, s_kept = map(
            sem, "add add_out turn x_hi x_lo turn_next next_hi next_lo kept".split())
        block = ctx.enter_context(nc.Block())

        def tiles_at(step, stage):
            if stage == "attn" and step < TB:
                return range(TB) if step == 0 else []
            t = step - AT[stage]
            return [t] if 0 <= t < TT else []

        steps = range(TT + AT["turn_next"])

        def cols(t):
            return slice(t * P, (t + 1) * P)

        def by_chunk(bank):
            return bank[:].rearrange("p (c t) -> p c t", c=C)

        @block.sync
        def _(sp):
            half_rows = lambda dram, b: dram[:, b * TB:(b + 1) * TB]
            sp.dma_start(a_raw[:], a["l0_a"]).then_inc(s_a, 16)
            sp.dma_start(half_rows(x[:], 0), half_rows(x_rows, 0)).then_inc(s_x[0], 16)
            sp.dma_start(b_raw[:], a["l0_b"]).then_inc(s_b, 16)
            for n in range(8):
                sp.dma_start(mix[n * RK:(n + 1) * RK], a["l0_mix"][n:n + 1].to_broadcast([RK, 1])).then_inc(s_b, 16)
            sp.dma_start(w_raw[:], a["l0_w"].rearrange("(c p) o -> p c o", p=P)).then_inc(s_w, 16)
            sp.dma_start(half_rows(x[:], 1), half_rows(x_rows, 1)).then_inc(s_x[1], 16)
            sp.dma_start(bias[:], a["l0_bias"].to_broadcast([P, D])).then_inc(s_bias, 16)
            for b in range(B):
                sp.wait_ge(s_add_out, (b + 1) * TB)
                sp.dma_start(half_rows(kept, b), half_rows(x[:], b)).then_inc(s_kept, 16)
            sp.wait_ge(s_kept, B * 16)

        @block.vector
        def _(dve):
            for step in steps:
                if step == WEIGHTS_AT:
                    dve.wait_ge(s_b, 9 * 16)
                    dve.tensor_scalar(b_raw[:], b_raw[:], mix[:], 2.0, ALU.mult, ALU.mult).then_inc(s_scaled, 1)
                    dve.wait_ge(s_hi, 1)
                    rest(dve, la.lo[:], a_raw[:], la.hi[:]).then_inc(s_lo, 1)
                    dve.wait_ge(s_hi, 2)
                    rest(dve, lb.lo[:], b_raw[:], lb.hi[:]).then_inc(s_lo, 1)
                    dve.wait_ge(s_w, 16)
                    for c in range(C + 1):
                        if c < C:
                            dve.wait_ge(s_merged, c + 1)
                            dve.tensor_tensor(whole[:, c], merge[c % 2][:], w_raw[:, c], ALU.add).then_inc(s_whole, 1)
                        if c >= 1:
                            dve.wait_ge(s_w_hi, c)
                            rest(dve, w.lo[:, c - 1], whole[:, c - 1], w.hi[:, c - 1]).then_inc(s_w_lo, 1)
                for t in tiles_at(step, "attn"):
                    norms.sums(dve, ATTN, t, acc[:, t])
                    if step == 0:
                        norms.spread(dve, (ATTN, t))
                for t in tiles_at(step, "lin_in"):
                    dve.wait_ge(s_add, t + 1)
                    norms.sums(dve, LIN_IN, t, x[:, t])
                norms.spread(dve, *[(ATTN, t) for t in tiles_at(step, "attn") if step],
                              *[(LIN_IN, t) for t in tiles_at(step, "lin_in")])
                for t in tiles_at(step, "turn"):
                    dve.wait_ge(s_x_hi, t + 1)
                    rest(dve, xT.lo[:, :, cols(t)], by_chunk(turned[t % 2]), xT.hi[:, :, cols(t)]).then_inc(s_x_lo, 1)
                for t in tiles_at(step, "lin_out"):
                    dve.wait_ge(s_taken, t + 1)
                    norms.sums(dve, LIN_OUT, t, acc[:, t])
                for t in tiles_at(step, "next_in"):
                    dve.wait_ge(s_add_out, t + 1)
                    norms.sums(dve, NEXT_IN, t, x[:, t])
                for t in tiles_at(step, "attn"):
                    norms.center(dve, ATTN, t)
                for t in tiles_at(step, "lin_in"):
                    norms.center(dve, LIN_IN, t)
                norms.spread(dve, *[(LIN_OUT, t) for t in tiles_at(step, "lin_out")],
                              *[(NEXT_IN, t) for t in tiles_at(step, "next_in")])
                for t in tiles_at(step, "turn_next"):
                    dve.wait_ge(s_next_hi, t + 1)
                    rest(dve, xT.lo[:, :, cols(t)], by_chunk(turned_next[t % 2]), xT.hi[:, :, cols(t)])\
                        .then_inc(s_next_lo, 1)
                for t in tiles_at(step, "take"):
                    if t == 0:
                        dve.wait_ge(s_bias, 16)
                    dve.wait_ge(s_rows, t + 1)
                    dve.tensor_tensor(acc[:, t], rows[t % 2][:], bias[:], ALU.add).then_inc(s_taken, 1)
                for t in tiles_at(step, "lin_out"):
                    norms.center(dve, LIN_OUT, t)
                for t in tiles_at(step, "next_in"):
                    norms.center(dve, NEXT_IN, t)

        @block.gpsimd
        def _(pool):
            for step in steps:
                for t in tiles_at(step, "add"):
                    pool.wait_ge(s_x[t // TB], 16)
                    pool.wait_ge(norms.normed[ATTN], t + 1)
                    pool.tensor_tensor(x[:, t], x[:, t], acc[:, t], ALU.add).then_inc(s_add, 1)
                for t in tiles_at(step, "add_out"):
                    pool.wait_ge(norms.normed[LIN_OUT], t + 1)
                    pool.tensor_tensor(x[:, t], x[:, t], acc[:, t], ALU.add).then_inc(s_add_out, 1)
                for t in tiles_at(step, "attn"):
                    norms.root(pool, ATTN, t)
                for t in tiles_at(step, "lin_in"):
                    norms.root(pool, LIN_IN, t)
                for t in tiles_at(step, "lin_out"):
                    norms.root(pool, LIN_OUT, t)
                for t in tiles_at(step, "next_in"):
                    norms.root(pool, NEXT_IN, t)

        @block.tensor
        def _(pe):
            for step in steps:
                if step == WEIGHTS_AT:
                    pe.wait_ge(s_lo, 2)
                    for c in range(C):
                        if c >= 2:
                            pe.wait_ge(s_whole, c - 1)
                        product(nc, merge[c % 2][:], la[:, c * P:(c + 1) * P], lb[:, :]).then_inc(s_merged, 1)
                for t in tiles_at(step, "turn"):
                    pe.wait_ge(norms.normed[LIN_IN], t + 1)
                    if t >= 2:
                        pe.wait_ge(s_x_lo, t - 1)
                    for c in range(C):
                        last = pe.transpose(turned[t % 2][:, c * P:(c + 1) * P], z[:, t % 2, c * P:(c + 1) * P],
                                            ident[:])
                    last.then_inc(s_turn, 1)
                for t in tiles_at(step, "turn_next"):
                    pe.wait_ge(norms.normed[NEXT_IN], t + 1)
                    if t >= 2:
                        pe.wait_ge(s_next_lo, t - 1)
                    for c in range(C):
                        last = pe.transpose(turned_next[t % 2][:, c * P:(c + 1) * P],
                                            z_next[:, t % 2, c * P:(c + 1) * P], ident[:])
                    last.then_inc(s_turn_next, 1)
                for t in tiles_at(step, "rows"):
                    if t == 0:
                        pe.wait_ge(s_w_lo, C)
                    pe.wait_ge(s_x_lo, t + 1)
                    if t >= 2:
                        pe.wait_ge(s_taken, t - 1)
                    for c in range(C):
                        last = product(nc, rows[t % 2][:], xT[:, c, cols(t)], w[:, c], c == 0, c == C - 1)
                    last.then_inc(s_rows, 1)

        @block.scalar
        def _(act):
            for step in steps:
                if step == WEIGHTS_AT:
                    act.wait_ge(s_a, 16)
                    act.activation(la.hi[:], a_raw[:], ACT.Copy).then_inc(s_hi, 1)
                    act.wait_ge(s_scaled, 1)
                    act.activation(lb.hi[:], b_raw[:], ACT.Copy).then_inc(s_hi, 1)
                    for c in range(C):
                        act.wait_ge(s_whole, c + 1)
                        act.activation(w.hi[:, c], whole[:, c], ACT.Copy).then_inc(s_w_hi, 1)
                for t in tiles_at(step, "turn"):
                    act.wait_ge(s_turn, t + 1)
                    act.activation(xT.hi[:, :, cols(t)], by_chunk(turned[t % 2]), ACT.Copy).then_inc(s_x_hi, 1)
                for t in tiles_at(step, "turn_next"):
                    act.wait_ge(s_rows, t + 1)
                    act.wait_ge(s_turn_next, t + 1)
                    act.activation(xT.hi[:, :, cols(t)], by_chunk(turned_next[t % 2]), ACT.Copy)\
                        .then_inc(s_next_hi, 1)
                for t in tiles_at(step, "attn"):
                    norms.scaled(act, ATTN, t, acc[:, t], acc[:, t])
                for t in tiles_at(step, "lin_in"):
                    if t >= 2:
                        act.wait_ge(s_turn, t - 1)
                    norms.scaled(act, LIN_IN, t, z[:, t % 2], x[:, t])
                for t in tiles_at(step, "lin_out"):
                    norms.scaled(act, LIN_OUT, t, acc[:, t], acc[:, t])
                for t in tiles_at(step, "next_in"):
                    if t >= 2:
                        act.wait_ge(s_turn_next, t - 1)
                    norms.scaled(act, NEXT_IN, t, z_next[:, t % 2], x[:, t])


def swiglu_phase(p, ctx0, xT, xT_words, acc, ident, half, kept, out_rows):
    nc, a = p.nc, p.a
    R3 = 96
    ATTN, FFN_IN, FFN_OUT = range(3)
    AT = {"attn": 0, "add": 1, "ffn_in": 2, "turn": 3}
    FIRST = range(TB + AT["turn"])
    LATER = {0: range(TB + AT["turn"], TB + AT["turn"] + 2), 1: range(TB + AT["turn"] + 2, TT + AT["turn"])}
    SIDE_AT, WHOLE_AT, WHOLE_LO_AT = 3, 5, 6
    OUT_AT = HT + 2
    with ExitStack() as ctx:
        sb = lambda n, s, dt=F32: p.sb(ctx, f"ffn_{n}", s, dt)
        split = lambda n, s: p.split(ctx, f"ffn_{n}", s)
        sem = lambda n: p.sem(ctx0, f"ffn_{n}")
        (w1, w1_words), (w3, w3_words), (w2, w2_words) = [
            p.split_and_words(ctx, f"ffn_{n}", [P, HT, 512]) for n in ("w1", "w3", "w2")]
        x = w2_words.lo[:, HT - TT:HT]
        z = w2_words.hi[:, HT - 2:HT]
        side_raw = w2_words.hi[0:R3, HT - 5:HT - 2]
        side = sb("side", [R3, 3, D], F32R)
        tile_raw = sb("tile_raw", [R3, 2, 3 * P])
        tile = sb("tile", [R3, 2, 3 * P], F32R)
        gate, gated = [acc[:, b * TB] for b in range(B)], [acc[:, b * TB + 1] for b in range(B)]
        gT = split("gT", [P, 2, S])
        x_back = [[part[:, t, 0:S] for t in range(TB)] for part in xT_words.passes]
        merge, (h1, h3) = p.banks(ctx, "ffn_merge", 2), p.banks(ctx, "ffn_h", 2)
        rows = p.banks(ctx, "ffn_rows", TB)
        norms = RowNorms(p, ctx, ctx0, "ffn_norm", 3, half)
        s_x = [sem("x_in0"), sem("x_in1")]
        s_side = sem("side_in")
        s_tile = [sem("tile_even"), sem("tile_odd")]
        s_raw = [[sem(f"{w}_{k}") for k in ("even", "odd")] for w in ("w1", "w3", "w2")]
        s_tile_hi, s_tile_lo, s_merged, s_whole, s_w_hi, s_w_lo = map(
            sem, "tile_hi tile_lo merged whole w_hi w_lo".split())
        s_h1, s_h3, s_gate, s_gated, s_g_hi, s_g_lo, s_used, s_rows, s_taken = map(
            sem, "h1 h3 gate gated g_hi g_lo used rows taken".split())
        s_add, s_turn, s_x_hi, s_x_lo, s_kept, s_out_add, s_stored = map(
            sem, "add turn x_hi x_lo kept out_add stored".split())
        s_back = [sem("x_back0"), sem("x_back1")]
        block = ctx.enter_context(nc.Block())
        weights = w1, w3, w2

        def tiles_at(step, stage):
            if stage == "attn" and step < TB:
                return range(TB) if step == 0 else []
            t = step - AT[stage]
            return [t] if 0 <= t < TT else []

        def cols(t):
            return slice(t * P, (t + 1) * P)

        def by_chunk(bank):
            return bank[:].rearrange("p (c t) -> p c t", c=C)

        def raw(j, o):
            return (w1_words, w3_words, w2_words)[j].lo[:, o]

        @block.sync
        def _(sp):
            def batch(rows_of, b):
                return rows_of[:, b * TB:(b + 1) * TB]

            def keep(b):
                sp.wait_ge(s_add, (b + 1) * TB)
                sp.dma_start(batch(kept, b), batch(x, b)).then_inc(s_kept, 16)

            sp.dma_start(batch(x, 0), batch(kept, 0)).then_inc(s_x[0], 16)
            for o in range(HT):
                if o == 0:
                    for j, n in enumerate(("f_a1", "f_a3", "f_b2")):
                        sp.dma_start(side_raw[:, j], a[n]).then_inc(s_side, 16)
                if o >= 2:
                    sp.wait_ge(s_tile_lo, o)
                sp.dma_start(tile_raw[:, o % 2], a["f_tile"][o]).then_inc(s_tile[o % 2], 16)
                if o == 1:
                    sp.dma_start(batch(x, 1), batch(kept, 1)).then_inc(s_x[1], 16)
                for j in range(3):
                    if o >= 2:
                        sp.wait_ge(s_whole, 3 * (o - 2) + j + 1)
                    if j == 2 and o == HT - TT:
                        keep(0)
                        keep(1)
                        sp.wait_ge(s_kept, B * 16)
                    sp.dma_start(raw(j, o), a[("f_w1", "f_w3", "f_w2")[j]][o]).then_inc(s_raw[j][o % 2], 16)
            sp.wait_ge(s_h3, HT)
            for b in range(B):
                for t in range(TB):
                    sp.dma_start(x_back[b][t], kept[:, b * TB + t]).then_inc(s_back[b], 16)
            for t in range(TT):
                sp.wait_ge(s_out_add, t + 1)
                sp.dma_start(out_rows[:, t], x_back[t // TB][t % TB]).then_inc(s_stored, 16)
            sp.wait_ge(s_stored, TT * 16)

        @block.tensor
        def _(pe):
            def prepare(o, parts=range(3)):
                pe.wait_ge(s_tile_lo, o + 2)
                for j in parts:
                    k = 3 * o + j
                    if k >= 2:
                        pe.wait_ge(s_whole, k - 1)
                    low = tile[:, o % 2, j * P:(j + 1) * P]
                    if j < 2:
                        for c in range(C):
                            last = pe.matmul(merge[k % 2][:, c * P:(c + 1) * P], side[:, j, c * P:(c + 1) * P], low,
                                             start=True, stop=True, skip_group_check=True)
                    else:
                        last = pe.matmul(merge[k % 2][:], low, side[:, j], start=True, stop=True)
                    last.then_inc(s_merged, 1)

            def norm_steps(steps):
                for step in steps:
                    if step == SIDE_AT:
                        pe.wait_ge(s_tile_lo, 1)
                    if step == WHOLE_AT:
                        prepare(0)
                    for t in tiles_at(step, "turn"):
                        pe.wait_ge(norms.normed[FFN_IN], t + 1)
                        if t >= TB:
                            pe.wait_ge(s_x_lo, t - TB + 1)
                        for c in range(C):
                            last = pe.transpose(rows[t % TB][:, c * P:(c + 1) * P], z[:, t % 2, c * P:(c + 1) * P],
                                                ident[:])
                        last.then_inc(s_turn, 1)

            def down(b, o):
                n = b * HT + o
                pe.wait_ge(s_g_lo, n + 1)
                if b == 0:
                    pe.wait_ge(s_w_lo, 3 * o + 3)
                if n == 0:
                    pe.wait_ge(s_x_lo, TT)
                if b == 1 and o == 0:
                    pe.wait_ge(s_taken, TB)
                for t in range(TB):
                    last = product(nc, rows[t][:], gT[:, n % 2, t * P:(t + 1) * P], w2[:, o], o == 0, o == HT - 1)
                    if o == HT - 1:
                        last.then_inc(s_rows, 1)
                if o < HT - 1:
                    last.then_inc(s_used, 1)

            norm_steps(FIRST)
            prepare(1, (0, 1))
            for b in range(B):
                for o in range(HT):
                    n = b * HT + o
                    if o == 0:
                        pe.wait_ge(s_x_lo, (b + 1) * TB)
                    for j, (h, s_h, out_of) in enumerate(((h1, s_h1, s_gate), (h3, s_h3, s_gated))):
                        if b == 0:
                            pe.wait_ge(s_w_lo, 3 * o + j + 1)
                        if n >= 1:
                            pe.wait_ge(out_of, n)
                        for c in range(C):
                            last = product(nc, h[:], weights[j][:, o, c * P:(c + 1) * P],
                                           xT[:, c, b * S:(b + 1) * S], c == 0, c == C - 1)
                        last.then_inc(s_h, 1)
                    if n == 0:
                        prepare(1, (2,))
                    norm_steps(LATER.get(n, ()))
                    if b == 0 and o + 2 < HT:
                        prepare(o + 2, (0, 1))
                    if n >= 1:
                        down(*divmod(n - 1, HT))
                    if b == 0 and o + 2 < HT:
                        prepare(o + 2, (2,))
            down(B - 1, HT - 1)

        @block.scalar
        def _(act):
            def tile_hi(o):
                act.wait_ge(s_tile[o % 2], 16 * (o // 2 + 1))
                if o >= 2:
                    act.wait_ge(s_merged, 3 * (o - 1))
                act.activation(tile[:, o % 2], tile_raw[:, o % 2], ACT.Copy).then_inc(s_tile_hi, 1)

            def whole_hi(o):
                for j in range(3):
                    act.wait_ge(s_whole, 3 * o + j + 1)
                    act.activation(weights[j].hi[:, o], raw(j, o), ACT.Copy).then_inc(s_w_hi, 1)

            def norm_steps(steps):
                for step in steps:
                    if step == SIDE_AT:
                        act.wait_ge(s_side, 48)
                        act.activation(side[:], side_raw, ACT.Copy, scale=2.0).then_inc(s_tile_hi, 1)
                        tile_hi(0)
                        tile_hi(1)
                    if step == WHOLE_AT:
                        whole_hi(0)
                    for t in tiles_at(step, "turn"):
                        act.wait_ge(s_turn, t + 1)
                        act.activation(xT.hi[:, :, cols(t)], by_chunk(rows[t % TB]), ACT.Copy).then_inc(s_x_hi, 1)
                    for t in tiles_at(step, "attn"):
                        norms.scaled(act, ATTN, t, acc[:, t], acc[:, t])
                    for t in tiles_at(step, "ffn_in"):
                        if t >= 2:
                            act.wait_ge(s_turn, t - 1)
                        norms.scaled(act, FFN_IN, t, z[:, t % 2], x[:, t])

            norm_steps(FIRST)
            for b in range(B):
                for o in range(HT):
                    n = b * HT + o
                    if b == 0:
                        if o + 2 < HT:
                            tile_hi(o + 2)
                        if o + 1 < HT:
                            whole_hi(o + 1)
                    norm_steps(LATER.get(n, ()))
                    act.wait_ge(s_h1, n + 1)
                    if n >= 1:
                        act.wait_ge(s_gated, n)
                    act.activation(gate[b], h1[:], ACT.Silu).then_inc(s_gate, 1)
                    act.wait_ge(s_gated, n + 1)
                    if n >= 2:
                        done_b, done_o = divmod(n - 2, HT)
                        if done_o == HT - 1:
                            act.wait_ge(s_rows, (done_b + 1) * TB)
                        else:
                            act.wait_ge(s_used, n - 1 - done_b)
                    act.activation(gT.hi[:, n % 2], gated[b], ACT.Copy).then_inc(s_g_hi, 1)
                    if n == HT:
                        act.wait_ge(s_rows, TB)
                        for t in range(TB):
                            act.activation(acc[:, t], rows[t][:], ACT.Copy).then_inc(s_taken, 1)
                    if 0 <= n - OUT_AT < TB:
                        norms.scaled(act, FFN_OUT, n - OUT_AT, acc[:, n - OUT_AT], acc[:, n - OUT_AT])
            act.wait_ge(s_g_lo, B * HT)
            for t in range(TB, TT):
                norms.scaled(act, FFN_OUT, t, acc[:, t], rows[t - TB][:])

        @block.vector
        def _(dve):
            def tile_lo(o):
                dve.wait_ge(s_tile_hi, o + 2)
                dve.tensor_tensor(tile[64:96, o % 2], tile_raw[64:96, o % 2], tile[64:96, o % 2].bitcast(F32),
                                  ALU.subtract).then_inc(s_tile_lo, 1)

            def whole(o):
                for j in range(3):
                    k = 3 * o + j
                    dve.wait_ge(s_raw[j][o % 2], 16 * (o // 2 + 1))
                    dve.wait_ge(s_merged, k + 1)
                    dve.tensor_tensor(raw(j, o), merge[k % 2][:], raw(j, o), ALU.add).then_inc(s_whole, 1)

            def norm_steps(steps):
                for step in steps:
                    if step == SIDE_AT:
                        dve.wait_ge(s_tile_hi, 1)
                        dve.scalar_tensor_tensor(side[32:64], side_raw[32:64], 2.0, side[32:64].bitcast(F32),
                                                 ALU.mult, ALU.subtract).then_inc(s_tile_lo, 1)
                        tile_lo(0)
                        tile_lo(1)
                    if step == WHOLE_AT:
                        whole(0)
                    for t in tiles_at(step, "attn"):
                        norms.sums(dve, ATTN, t, acc[:, t])
                        if step == 0:
                            norms.spread(dve, (ATTN, t))
                    for t in tiles_at(step, "ffn_in"):
                        dve.wait_ge(s_add, t + 1)
                        norms.sums(dve, FFN_IN, t, x[:, t])
                    norms.spread(dve, *[(ATTN, t) for t in tiles_at(step, "attn") if step],
                                  *[(FFN_IN, t) for t in tiles_at(step, "ffn_in")])
                    for t in tiles_at(step, "turn"):
                        dve.wait_ge(s_x_hi, t + 1)
                        rest(dve, xT.lo[:, :, cols(t)], by_chunk(rows[t % TB]), xT.hi[:, :, cols(t)])\
                            .then_inc(s_x_lo, 1)
                    for t in tiles_at(step, "attn"):
                        norms.center(dve, ATTN, t)
                    for t in tiles_at(step, "ffn_in"):
                        norms.center(dve, FFN_IN, t)

            def add_out(t):
                dve.wait_ge(norms.normed[FFN_OUT], t + 1)
                x_t = x_back[t // TB][t % TB]
                dve.tensor_tensor(x_t, x_t, acc[:, t], ALU.add).then_inc(s_out_add, 1)

            norm_steps(FIRST)
            for b in range(B):
                for o in range(HT):
                    n = b * HT + o
                    if b == 0:
                        if o + 2 < HT:
                            tile_lo(o + 2)
                        if o + 1 < HT:
                            whole(o + 1)
                    norm_steps(LATER.get(n, ()))
                    t = n - OUT_AT
                    if 0 <= t < TB:
                        dve.wait_ge(s_taken, t + 1)
                        norms.sums(dve, FFN_OUT, t, acc[:, t])
                        norms.spread(dve, (FFN_OUT, t))
                        norms.center(dve, FFN_OUT, t)
                    if n == OUT_AT + 1:
                        dve.wait_ge(s_back[0], TB * 16)
                    if 1 <= t <= TB:
                        add_out(t - 1)
                    dve.wait_ge(s_gate, n + 1)
                    dve.wait_ge(s_h3, n + 1)
                    if n >= 1:
                        dve.wait_ge(s_g_lo, n)
                    dve.tensor_tensor(gated[b], h3[:], gate[b], ALU.mult).then_inc(s_gated, 1)
                    dve.wait_ge(s_g_hi, n + 1)
                    rest(dve, gT.lo[:, n % 2], gated[b], gT.hi[:, n % 2]).then_inc(s_g_lo, 1)
            dve.wait_ge(s_back[1], TB * 16)
            for t in range(TB, TT + 2):
                if t < TT:
                    dve.wait_ge(s_rows, t + 1)
                    norms.sums(dve, FFN_OUT, t, rows[t - TB][:])
                    norms.spread(dve, (FFN_OUT, t))
                if TB < t <= TT:
                    norms.center(dve, FFN_OUT, t - 1)
                if t >= TB + 2:
                    add_out(t - 2)

        @block.gpsimd
        def _(pool):
            def whole_lo(o):
                for j in range(3):
                    pool.wait_ge(s_w_hi, 3 * o + j + 1)
                    rest(pool, weights[j].lo[:, o], raw(j, o), weights[j].hi[:, o]).then_inc(s_w_lo, 1)

            def norm_steps(steps):
                for step in steps:
                    if step == WHOLE_LO_AT:
                        whole_lo(0)
                    for t in tiles_at(step, "add"):
                        pool.wait_ge(s_x[t // TB], 16)
                        pool.wait_ge(norms.normed[ATTN], t + 1)
                        pool.tensor_tensor(x[:, t], x[:, t], acc[:, t], ALU.add).then_inc(s_add, 1)
                    for t in tiles_at(step, "attn"):
                        norms.root(pool, ATTN, t)
                    for t in tiles_at(step, "ffn_in"):
                        norms.root(pool, FFN_IN, t)

            norm_steps(FIRST)
            for o in range(HT):
                if o + 1 < HT:
                    whole_lo(o + 1)
                norm_steps(LATER.get(o, ()))
            for t in range(TT):
                norms.root(pool, FFN_OUT, t)


def build(nc, a, out):
    p = Program(nc, a)
    with ExitStack() as ctx:
        ident = p.sb(ctx, "ident", [P, P])
        half = p.sb(ctx, "half", [P, TB * GH])
        acc = p.sb(ctx, "acc", [P, TT, D])
        xT, xT_words = p.split_and_words(ctx, "xT", [P, C, T])
        made = p.sem(ctx, "made")
        x_rows = a["x"].rearrange("(t p) d -> p t d", p=P)
        out_rows = out.rearrange("(t p) d -> p t d", p=P)
        kept = nc.dram_tensor("x_kept", [T, D], F32, kind="Internal").ap().rearrange("(t p) d -> p t d", p=P)

        with nc.Block() as block:
            @block.gpsimd
            def _(pool):
                pool.memset(ident[:], 0.0).then_inc(made, 1)
                pool.wait_ge(made, 1)
                pool.affine_select(out=ident[:], in_=ident[:], compare_op=ALU.not_equal, fill=1.0, base=0,
                                   pattern=[[-1, P]], channel_multiplier=1).then_inc(made, 1)
                pool.memset(half[:], -0.5).then_inc(made, 1)
                pool.wait_ge(made, 3)

        attention_phase(p, ctx, 0, xT, acc, ident, half, x_rows)
        linear_phase(p, ctx, xT, acc, ident, half, x_rows, kept)
        attention_phase(p, ctx, 1, xT, acc, ident, half)
        swiglu_phase(p, ctx, xT, xT_words, acc, ident, half, kept, out_rows)


def layout(v):
    import numpy as np

    f = {k: np.asarray(x) for k, x in v.items()}
    tall = lambda w, n: w.T.reshape(C, P, n, HD).transpose(2, 1, 0, 3).reshape(n, P, C * HD)
    wide = lambda w: w.reshape(C, P, NG, GH * HD).transpose(2, 0, 1, 3).reshape(NG * C, P, GH * HD)
    inv_freq = (1.0 / np.float32(10000.0) ** (np.arange(0, HD, 2, dtype=np.float32) / np.float32(HD)))
    angle = np.arange(S, dtype=np.float32)[None, :] * inv_freq.astype(np.float32)[:, None]
    c, s = np.cos(angle), np.sin(angle)
    ahead = np.arange(P)[None, :] > np.arange(P)[:, None]
    out = {
        "x": f["L0_attn_hidden_states"].reshape(T, D),
        "l0_wq": tall(f["L0_attn_Wq"], NH), "l0_wk": tall(f["L0_attn_Wk"], NG), "l0_wv": tall(f["L0_attn_Wv"], NG),
        "l0_wo": f["L0_attn_Wo"].T.reshape(NH, HD, D),
        "trig": np.stack([x * k for k in (1.0, SCALE) for x in (np.concatenate([c, c]), np.concatenate([-s, s]))], 1),
        "mask": np.where(ahead, MASKED, 0.0),
        "l0_w": f["L0_ffn_W"].T, "l0_a": f["L0_ffn_lora_A"].reshape(8 * RK, D),
        "l0_b": f["L0_ffn_lora_B"].transpose(0, 2, 1).reshape(8 * RK, D), "l0_bias": f["L0_ffn_bias"].reshape(1, D),
        "l0_mix": f["L0_ffn_lora_weights"].reshape(8, 1),
        "l1_wq": wide(f["L1_attn_Wq"]), "l1_wk": wide(f["L1_attn_Wk"]), "l1_wv": wide(f["L1_attn_Wv"]),
        "l1_wo": f["L1_attn_Wo"].reshape(NH, HD, D),
        "l1_bq": f["L1_attn_bq"].reshape(NG, GH * HD), "l1_bk": f["L1_attn_bk"].reshape(NG, GH * HD),
        "l1_bv": f["L1_attn_bv"].reshape(NH, HD).T, "l1_bo": f["L1_attn_bo"].reshape(1, D),
        "l1_gq": f["L1_attn_gq"].reshape(HD, 1), "l1_gk": f["L1_attn_gk"].reshape(HD, 1),
    }

    def padded(w):
        return np.concatenate([w, np.zeros((w.shape[0], HP - HID), w.dtype)], axis=1)

    def thrice(w):
        three = np.zeros((3, 32, w.shape[1]), w.dtype)
        three[:, :RK] = w
        return three.reshape(96, w.shape[1])

    for n in "13":
        out[f"f_w{n}"] = padded(f[f"L1_ffn_w{n}"].T).reshape(C, P, HT, P).transpose(2, 1, 0, 3).reshape(HT, P, C * P)
        out[f"f_a{n}"] = thrice(f[f"L1_ffn_lora_A{n}"])
    out["f_w2"] = padded(f["L1_ffn_w2"]).T.reshape(HT, P, D)
    out["f_b2"] = thrice(f["L1_ffn_lora_B2"].T)
    ranks = f["L1_ffn_lora_B1"].T, f["L1_ffn_lora_B3"].T, f["L1_ffn_lora_A2"]
    out["f_tile"] = np.stack([thrice(padded(w)).reshape(96, HT, P) for w in ranks]).transpose(2, 1, 0, 3).reshape(
        HT, 96, 3 * P)
    return {k: np.ascontiguousarray(x, dtype=np.float32) for k, x in out.items()}


def kernel(**inputs):
    import concourse.bacc as bacc
    from concourse.bass_utils import run_bass_kernel_spmd

    nc = bacc.Bacc("TRN2", target_bir_lowering=False, num_devices=1)
    arrays = layout(inputs)
    a = {k: nc.dram_tensor(k, x.shape, F32, kind="ExternalInput").ap() for k, x in arrays.items()}
    out = nc.dram_tensor("out", (T, D), F32, kind="ExternalOutput").ap()
    build(nc, a, out)
    r = run_bass_kernel_spmd(nc, [arrays], core_ids=[0])
    return r.results[0]["out"].reshape(B, S, D)
```
